# Optimizing a Trainium2 kernel written in Bass

```python
import numpy as np
import jax
import jax.numpy as jnp

def _softmax(x, axis=-1):
    return jax.nn.softmax(x, axis=axis)

def _gelu(x):
    return jax.nn.gelu(x, approximate=True)

def _silu(x):
    return jax.nn.silu(x)

def _sigmoid(x):
    return jax.nn.sigmoid(x)

def _layernorm(x, axis=-1, eps=1e-05):
    m = jnp.mean(x, axis=axis, keepdims=True)
    v = jnp.var(x, axis=axis, keepdims=True)
    return (x - m) / jnp.sqrt(v + eps)

def _scatter_add(tgt, idx, src, axis=0):
    return tgt.at[idx].add(src)

def _segment_sum(src, seg, n):
    return jax.ops.segment_sum(src, seg, n)
kernel_name = 'mk_early_fusion_d2_tok_img768_r4_0912c6'

def setup_inputs(seed: int=0):
    np.random.seed(seed)
    _w = jnp.asarray

    def _rec_inputs():
        import jax
        import jax.numpy as jnp
        _rk = jax.random.key(seed)
        x = -0.00016672 + 0.999947 * jax.random.normal(jax.random.fold_in(_rk, 1), (32, 3, 64, 64), jnp.float32)
        txt = -3.52942e-05 + 0.577782 * jax.random.normal(jax.random.fold_in(_rk, 2), (32, 77, 192), jnp.float32)
        return (x, txt)
    x, txt = _rec_inputs()

    def _L0_tok_setup():
        import jax, jax.numpy as jnp
        import numpy as np
        PATCH = 16
        CHANNELS = 3
        DIM = 192
        PATCH_DIM = CHANNELS * PATCH * PATCH
        key = jax.random.key(seed)
        kx, kw, kb = jax.random.split(key, 3)
        x = jax.random.normal(kx, (64, 3, 96, 96), dtype=jnp.float32)
        bound = 1.0 / np.sqrt(PATCH_DIM)
        W = jax.random.uniform(kw, (DIM, PATCH_DIM), minval=-bound, maxval=bound, dtype=jnp.float32)
        b = jax.random.uniform(kb, (DIM,), minval=-bound, maxval=bound, dtype=jnp.float32)
        return {'x': x, 'W': W, 'b': b}
    _L0_tok_all = _L0_tok_setup()
    _L0_tok_in = {k: v for k, v in _L0_tok_all.items() if k in ('W', 'b')}
    del _L0_tok_all

    def _L0_attn_setup():
        import jax, jax.numpy as jnp
        import numpy as np
        ALPHA = 0.35

        def _round_ln_pow2(x):
            y = jnp.floor(jnp.log2(x))
            up = x - 2.0 ** y > 2.0 ** (y + 1.0) - x
            return 2.0 ** (y + up.astype(x.dtype))
        key = jax.random.key(seed)
        k1, k2, k3, k4, k5 = jax.random.split(key, 5)
        B, N, C = (64, 197, 192)
        return {'x': jax.random.normal(k1, (B, N, C), dtype=jnp.float32), 'qkv_weight': jax.random.normal(k2, (3 * C, C), dtype=jnp.float32) * 0.02, 'qkv_bias': jax.random.normal(k3, (3 * C,), dtype=jnp.float32) * 0.02, 'proj_weight': jax.random.normal(k4, (C, C), dtype=jnp.float32) * 0.02, 'proj_bias': jax.random.normal(k5, (C,), dtype=jnp.float32) * 0.02}
    _L0_attn_all = _L0_attn_setup()
    _L0_attn_in = {k: v for k, v in _L0_attn_all.items() if k in ('qkv_weight', 'qkv_bias', 'proj_weight', 'proj_bias')}
    del _L0_attn_all

    def _L0_ffn_setup():
        import jax, jax.numpy as jnp
        import numpy as np
        TOP_K = 2
        ROUTED_SCALE = 1.0

        def _swiglu_all(x, gw, uw, dw):
            g = jnp.einsum('th,eih->tei', x, gw)
            u = jnp.einsum('th,eih->tei', x, uw)
            h = jax.nn.silu(g) * u
            return jnp.einsum('tei,ehi->teh', h, dw)
        key = jax.random.key(seed)
        ks = jax.random.split(key, 8)
        B, S, H, I, E, NS = (2, 256, 192, 768, 8, 2)
        w = lambda k, shape: jax.random.normal(k, shape, jnp.float32) * 0.02
        return {'hidden_states': jax.random.normal(ks[0], (B, S, H), jnp.float32), 'gate_w': w(ks[1], (E, H)), 'shared_gate': w(ks[2], (NS, I, H)), 'shared_up': w(ks[3], (NS, I, H)), 'shared_down': w(ks[4], (NS, H, I)), 'routed_gate': w(ks[5], (E, I, H)), 'routed_up': w(ks[6], (E, I, H)), 'routed_down': w(ks[7], (E, H, I))}
    _L0_ffn_all = _L0_ffn_setup()
    _L0_ffn_in = {k: v for k, v in _L0_ffn_all.items() if k in ('gate_w', 'shared_gate', 'shared_up', 'shared_down', 'routed_gate', 'routed_up', 'routed_down')}
    del _L0_ffn_all

    def _L1_attn_setup():
        import jax, jax.numpy as jnp
        import numpy as np
        K, K_Q, M, H = (12, 6, 1, 64)
        N_REP = K // K_Q
        D = 192
        DIM_MEM = K * H
        DIM_MEM_TOT = DIM_MEM + K
        DIM_Q = K_Q * H * M * 2
        DIM_CONV = DIM_MEM_TOT + DIM_Q
        OUT_CPLX = K * 2 * H
        DIM_EXPAND = H * 3
        MAXLEN = 1024
        KSIZE = 4

        def _causal_dw_conv(z, w):
            return jax.lax.conv_general_dilated(z, w[:, None, :], window_strides=(1,), padding=[(w.shape[0] - 1, 0)], dimension_numbers=('NWC', 'WIO', 'NWC'), feature_group_count=z.shape[-1])

        def _gated_rmsnorm(x, gate, w, eps=1e-06):
            h = x * jax.nn.silu(gate)
            return h * jax.lax.rsqrt(jnp.mean(h * h, axis=-1, keepdims=True) + eps) * w
        key = jax.random.key(seed)
        ks = jax.random.split(key, 8)
        B, L = (4, 1024)
        decay_init = np.log(np.exp(np.geomspace(0.001, 0.1, K)) - 1).astype(np.float32)
        return {'x': jax.random.normal(ks[0], (B, L, D), jnp.float32), 'W_in': jax.random.normal(ks[1], (D, DIM_CONV), jnp.float32) * 0.02, 'conv_w': jax.random.normal(ks[2], (KSIZE, DIM_CONV), jnp.float32) * 0.2, 'theta_raw': jax.random.normal(ks[3], (1, 1, K, H, 1), jnp.float32), 'w_int_raw': jnp.ones((1, 1, K_Q, N_REP, H, M), jnp.float32), 'decay_slopes': jnp.asarray(decay_init), 'score_scale': jnp.ones((K,), jnp.float32), 'score_bias': jnp.zeros((K,), jnp.float32), 'phase_scale': jnp.ones((K,), jnp.float32), 'gated_norm_weight': jnp.ones((OUT_CPLX,), jnp.float32), 'W_readout': jax.random.normal(ks[4], (K, 2 * H, 2 * DIM_EXPAND), jnp.float32) * 0.05, 'W_gate': jax.random.normal(ks[5], (D, OUT_CPLX), jnp.float32) * 0.02, 'W_out': jax.random.normal(ks[6], (K * DIM_EXPAND, D), jnp.float32) * 0.02}
    _L1_attn_all = _L1_attn_setup()
    _L1_attn_in = {k: v for k, v in _L1_attn_all.items() if k in ('W_in', 'conv_w', 'theta_raw', 'w_int_raw', 'decay_slopes', 'score_scale', 'score_bias', 'phase_scale', 'gated_norm_weight', 'W_readout', 'W_gate', 'W_out')}
    del _L1_attn_all

    def _L1_ffn_setup():
        import jax, jax.numpy as jnp
        import numpy as np
        B, N, DIM, HEADS = (4, 256, 192, 12)
        HIDDEN, E, TOPK = (768, 8, 2)
        EPS = 1e-05

        def _layernorm(x, g, b):
            mu = jnp.mean(x, axis=-1, keepdims=True)
            var = jnp.var(x, axis=-1, keepdims=True)
            return (x - mu) * jax.lax.rsqrt(var + EPS) * g + b
        key = jax.random.key(seed)
        ks = jax.random.split(key, 10)
        s = 0.02
        return {'x': jax.random.normal(ks[0], (B, N, DIM), dtype=jnp.float32), 'ln1_g': jnp.ones((DIM,), jnp.float32), 'ln1_b': jnp.zeros((DIM,), jnp.float32), 'qkv_w': jax.random.normal(ks[1], (3 * DIM, DIM), jnp.float32) * s, 'proj_w': jax.random.normal(ks[2], (DIM, DIM), jnp.float32) * s, 'proj_b': jnp.zeros((DIM,), jnp.float32), 'ln2_g': jnp.ones((DIM,), jnp.float32), 'ln2_b': jnp.zeros((DIM,), jnp.float32), 'gate_w': jax.random.normal(ks[3], (E, DIM), jnp.float32) * s, 'gate_b': jnp.zeros((E,), jnp.float32), 'w1': jax.random.normal(ks[4], (E, HIDDEN, DIM), jnp.float32) * s, 'b1': jnp.zeros((E, HIDDEN), jnp.float32), 'w2': jax.random.normal(ks[5], (E, DIM, HIDDEN), jnp.float32) * s, 'b2': jnp.zeros((E, DIM), jnp.float32)}
    _L1_ffn_all = _L1_ffn_setup()
    _L1_ffn_in = {k: v for k, v in _L1_ffn_all.items() if k in ('ln1_g', 'ln1_b', 'qkv_w', 'proj_w', 'proj_b', 'ln2_g', 'ln2_b', 'gate_w', 'gate_b', 'w1', 'b1', 'w2', 'b2')}
    del _L1_ffn_all
    return {'x': x, 'txt': txt, 'L0_tok_W': _L0_tok_in['W'], 'L0_tok_b': _L0_tok_in['b'], 'L0_attn_qkv_weight': _L0_attn_in['qkv_weight'], 'L0_attn_qkv_bias': _L0_attn_in['qkv_bias'], 'L0_attn_proj_weight': _L0_attn_in['proj_weight'], 'L0_attn_proj_bias': _L0_attn_in['proj_bias'], 'L0_ffn_gate_w': _L0_ffn_in['gate_w'], 'L0_ffn_shared_gate': _L0_ffn_in['shared_gate'], 'L0_ffn_shared_up': _L0_ffn_in['shared_up'], 'L0_ffn_shared_down': _L0_ffn_in['shared_down'], 'L0_ffn_routed_gate': _L0_ffn_in['routed_gate'], 'L0_ffn_routed_up': _L0_ffn_in['routed_up'], 'L0_ffn_routed_down': _L0_ffn_in['routed_down'], 'L1_attn_W_in': _L1_attn_in['W_in'], 'L1_attn_conv_w': _L1_attn_in['conv_w'], 'L1_attn_theta_raw': _L1_attn_in['theta_raw'], 'L1_attn_w_int_raw': _L1_attn_in['w_int_raw'], 'L1_attn_decay_slopes': _L1_attn_in['decay_slopes'], 'L1_attn_score_scale': _L1_attn_in['score_scale'], 'L1_attn_score_bias': _L1_attn_in['score_bias'], 'L1_attn_phase_scale': _L1_attn_in['phase_scale'], 'L1_attn_gated_norm_weight': _L1_attn_in['gated_norm_weight'], 'L1_attn_W_readout': _L1_attn_in['W_readout'], 'L1_attn_W_gate': _L1_attn_in['W_gate'], 'L1_attn_W_out': _L1_attn_in['W_out'], 'L1_ffn_ln1_g': _L1_ffn_in['ln1_g'], 'L1_ffn_ln1_b': _L1_ffn_in['ln1_b'], 'L1_ffn_qkv_w': _L1_ffn_in['qkv_w'], 'L1_ffn_proj_w': _L1_ffn_in['proj_w'], 'L1_ffn_proj_b': _L1_ffn_in['proj_b'], 'L1_ffn_ln2_g': _L1_ffn_in['ln2_g'], 'L1_ffn_ln2_b': _L1_ffn_in['ln2_b'], 'L1_ffn_gate_w': _L1_ffn_in['gate_w'], 'L1_ffn_gate_b': _L1_ffn_in['gate_b'], 'L1_ffn_w1': _L1_ffn_in['w1'], 'L1_ffn_b1': _L1_ffn_in['b1'], 'L1_ffn_w2': _L1_ffn_in['w2'], 'L1_ffn_b2': _L1_ffn_in['b2']}

def reference(x, txt, L0_tok_W, L0_tok_b, L0_attn_qkv_weight, L0_attn_qkv_bias, L0_attn_proj_weight, L0_attn_proj_bias, L0_ffn_gate_w, L0_ffn_shared_gate, L0_ffn_shared_up, L0_ffn_shared_down, L0_ffn_routed_gate, L0_ffn_routed_up, L0_ffn_routed_down, L1_attn_W_in, L1_attn_conv_w, L1_attn_theta_raw, L1_attn_w_int_raw, L1_attn_decay_slopes, L1_attn_score_scale, L1_attn_score_bias, L1_attn_phase_scale, L1_attn_gated_norm_weight, L1_attn_W_readout, L1_attn_W_gate, L1_attn_W_out, L1_ffn_ln1_g, L1_ffn_ln1_b, L1_ffn_qkv_w, L1_ffn_proj_w, L1_ffn_proj_b, L1_ffn_ln2_g, L1_ffn_ln2_b, L1_ffn_gate_w, L1_ffn_gate_b, L1_ffn_w1, L1_ffn_b1, L1_ffn_w2, L1_ffn_b2):
    import jax
    import jax.numpy as jnp

    def _L0_tok_ref(x, W, b):
        import jax, jax.numpy as jnp
        import numpy as np
        PATCH = 16
        CHANNELS = 3
        DIM = 192
        PATCH_DIM = CHANNELS * PATCH * PATCH
        B, C, H, Wd = x.shape
        h, w = (H // PATCH, Wd // PATCH)
        patches = x.reshape(B, C, h, PATCH, w, PATCH)
        patches = patches.transpose(0, 2, 4, 3, 5, 1)
        patches = patches.reshape(B, h * w, PATCH * PATCH * C)
        return jnp.einsum('bnd,ed->bne', patches, W) + b

    def _L0_attn_ref(x, qkv_weight, qkv_bias, proj_weight, proj_bias):
        import jax, jax.numpy as jnp
        import numpy as np
        ALPHA = 0.35

        def _round_ln_pow2(x):
            y = jnp.floor(jnp.log2(x))
            up = x - 2.0 ** y > 2.0 ** (y + 1.0) - x
            return 2.0 ** (y + up.astype(x.dtype))
        B, N, C = x.shape
        num_heads = 12
        head_dim = C // num_heads
        scale = head_dim ** (-0.5)
        global_max_x = jnp.abs(x).max(axis=(0, 1))
        max_weight = jnp.abs(qkv_weight).max(axis=0)
        channel_scale = _round_ln_pow2(global_max_x ** ALPHA / max_weight ** (1.0 - ALPHA))
        x_smoothed = x / channel_scale[None, None, :]
        weight_smoothed = qkv_weight * channel_scale[None, :]
        h = jnp.einsum('bnc,mc->bnm', x_smoothed, weight_smoothed) + qkv_bias
        qkv = h.reshape(B, N, 3, num_heads, head_dim).transpose(2, 0, 3, 1, 4)
        q, k, v = (qkv[0], qkv[1], qkv[2])
        attn = jnp.einsum('bhnd,bhmd->bhnm', q, k) * scale
        attn = jax.nn.softmax(attn, axis=-1)
        out = jnp.einsum('bhnm,bhmd->bhnd', attn, v)
        out = out.transpose(0, 2, 1, 3).reshape(B, N, C)
        out = jnp.einsum('bnc,mc->bnm', out, proj_weight) + proj_bias
        return out

    def _L0_ffn_ref(hidden_states, gate_w, shared_gate, shared_up, shared_down, routed_gate, routed_up, routed_down):
        import jax, jax.numpy as jnp
        import numpy as np
        TOP_K = 2
        ROUTED_SCALE = 1.0

        def _swiglu_all(x, gw, uw, dw):
            g = jnp.einsum('th,eih->tei', x, gw)
            u = jnp.einsum('th,eih->tei', x, uw)
            h = jax.nn.silu(g) * u
            return jnp.einsum('tei,ehi->teh', h, dw)
        B, S, H = hidden_states.shape
        T = B * S
        x = hidden_states.reshape(T, H)
        router_logits = x @ gate_w.T
        scores = jax.nn.softmax(router_logits, axis=-1)
        _, topk_idx = jax.lax.top_k(scores, TOP_K)
        topk_w = jnp.take_along_axis(scores, topk_idx, axis=-1)
        topk_w = topk_w / (topk_w.sum(axis=-1, keepdims=True) + 1e-08)
        topk_w = topk_w * ROUTED_SCALE
        E = gate_w.shape[0]
        combine = jnp.zeros((T, E), scores.dtype).at[jnp.arange(T)[:, None], topk_idx].add(topk_w)
        routed_all = _swiglu_all(x, routed_gate, routed_up, routed_down)
        routed_out = jnp.einsum('teh,te->th', routed_all, combine)
        NS = shared_gate.shape[0]
        shared_all = _swiglu_all(x, shared_gate, shared_up, shared_down)
        shared_out = shared_all.sum(axis=1) / NS
        out = (shared_out + routed_out).reshape(B, S, H)
        return out

    def _L1_attn_ref(x, W_in, conv_w, theta_raw, w_int_raw, decay_slopes, score_scale, score_bias, phase_scale, gated_norm_weight, W_readout, W_gate, W_out):
        import jax, jax.numpy as jnp
        import numpy as np
        K, K_Q, M, H = (12, 6, 1, 64)
        N_REP = K // K_Q
        D = 192
        DIM_MEM = K * H
        DIM_MEM_TOT = DIM_MEM + K
        DIM_Q = K_Q * H * M * 2
        DIM_CONV = DIM_MEM_TOT + DIM_Q
        OUT_CPLX = K * 2 * H
        DIM_EXPAND = H * 3
        MAXLEN = 1024
        KSIZE = 4

        def _causal_dw_conv(z, w):
            return jax.lax.conv_general_dilated(z, w[:, None, :], window_strides=(1,), padding=[(w.shape[0] - 1, 0)], dimension_numbers=('NWC', 'WIO', 'NWC'), feature_group_count=z.shape[-1])

        def _gated_rmsnorm(x, gate, w, eps=1e-06):
            h = x * jax.nn.silu(gate)
            return h * jax.lax.rsqrt(jnp.mean(h * h, axis=-1, keepdims=True) + eps) * w
        B, L, _ = x.shape
        z = jax.nn.silu(_causal_dw_conv(x @ W_in, conv_w))
        z_mem = z[..., :DIM_MEM_TOT]
        q_raw = z[..., DIM_MEM_TOT:].reshape(B, L, K_Q, 1, H, M, 2)
        k_val = z_mem[..., :DIM_MEM].reshape(B, L, K, H)
        s_raw = z_mem[..., DIM_MEM:]
        q_re, q_im = (q_raw[..., 0], q_raw[..., 1])
        theta = 0.001 + 2.999 * jax.nn.sigmoid(theta_raw)
        w_int = jnp.exp(w_int_raw)
        w_int = w_int / (jnp.sum(w_int, axis=-1, keepdims=True) + 1e-06)
        pos = jnp.arange(L, dtype=jnp.float32)
        slopes = jax.nn.softplus(decay_slopes).reshape(1, 1, K)
        dist = jnp.maximum(float(MAXLEN - 1) - pos, 0.0)
        log_tw = -slopes * dist[None, :, None]
        p_w = jax.nn.softplus(score_scale[None, None, :] * s_raw + score_bias[None, None, :])
        p_w = jnp.clip(p_w * jnp.exp(log_tw), 0.0001, 5000.0)
        k5 = k_val[..., None]
        k_scaled = k5 * phase_scale[None, None, :, None, None]
        phi = k_scaled / (1.0 + jnp.abs(k_scaled)) * theta
        kvw = k5 * p_w[..., None, None]
        re = kvw * jnp.cos(phi)
        im = kvw * jnp.sin(phi)
        flat = K * H * M
        stack = jnp.concatenate([p_w, re.reshape(B, L, flat), im.reshape(B, L, flat)], axis=-1)
        cs = jnp.cumsum(stack, axis=1)
        den_acc = cs[..., :K]
        re_acc = cs[..., K:K + flat].reshape(B, L, K, H, M)
        im_acc = cs[..., K + flat:].reshape(B, L, K, H, M)
        inv_den = (1.0 / jnp.maximum(den_acc, 0.0001))[..., None, None]
        s_re = (re_acc * inv_den).reshape(B, L, K_Q, N_REP, H, M)
        s_im = (im_acc * inv_den).reshape(B, L, K_Q, N_REP, H, M)
        scale = H ** (-0.5)
        match_re = (s_re * q_re + s_im * q_im) * scale
        match_im = (s_im * q_re - s_re * q_im) * scale
        out_re = jnp.sum(match_re * w_int, axis=-1).reshape(B, L, K, H)
        out_im = jnp.sum(match_im * w_int, axis=-1).reshape(B, L, K, H)
        out_flat = jnp.concatenate([out_re, out_im], axis=-1).reshape(B, L, OUT_CPLX)
        out_n = _gated_rmsnorm(out_flat, x @ W_gate, gated_norm_weight)
        y_raw = jnp.einsum('blkf,kfn->blkn', out_n.reshape(B, L, K, 2 * H), W_readout)
        y_val, y_gate = jnp.split(y_raw, 2, axis=-1)
        y = (y_val * jax.nn.sigmoid(y_gate)).reshape(B, L, K * DIM_EXPAND)
        return y @ W_out

    def _L1_ffn_ref(x, ln1_g, ln1_b, qkv_w, proj_w, proj_b, ln2_g, ln2_b, gate_w, gate_b, w1, b1, w2, b2):
        import jax, jax.numpy as jnp
        import numpy as np
        B, N, DIM, HEADS = (4, 256, 192, 12)
        HIDDEN, E, TOPK = (768, 8, 2)
        EPS = 1e-05

        def _layernorm(x, g, b):
            mu = jnp.mean(x, axis=-1, keepdims=True)
            var = jnp.var(x, axis=-1, keepdims=True)
            return (x - mu) * jax.lax.rsqrt(var + EPS) * g + b
        b, n, d = x.shape
        hd = d // HEADS
        scale = hd ** (-0.5)
        h = _layernorm(x, ln1_g, ln1_b)
        qkv = h @ qkv_w.T
        qkv = qkv.reshape(b, n, 3, HEADS, hd).transpose(2, 0, 3, 1, 4)
        q, k, v = (qkv[0], qkv[1], qkv[2])
        attn = jax.nn.softmax(jnp.einsum('bhnd,bhmd->bhnm', q, k) * scale, axis=-1)
        a = jnp.einsum('bhnm,bhmd->bhnd', attn, v)
        a = a.transpose(0, 2, 1, 3).reshape(b, n, d)
        a = a @ proj_w.T + proj_b
        x = x + a
        h2 = _layernorm(x, ln2_g, ln2_b)
        t = h2.reshape(-1, d)
        T = t.shape[0]
        logits = t @ gate_w.T + gate_b
        top_val, top_idx = jax.lax.top_k(logits, TOPK)
        score = jax.nn.softmax(top_val, axis=-1)
        cw = jnp.zeros((T, E), t.dtype).at[jnp.arange(T)[:, None], top_idx].add(score)
        out = jnp.zeros_like(t)
        for e in range(E):
            he = jax.nn.gelu(t @ w1[e].T + b1[e], approximate=False)
            ye = he @ w2[e].T + b2[e]
            out = out + cw[:, e:e + 1] * ye
        return x + out.reshape(b, n, d)
    h = _L0_tok_ref(x, L0_tok_W, L0_tok_b)
    h = jnp.concatenate([h, txt], axis=1)
    h = h + _L0_attn_ref(_layernorm(h, axis=-1), L0_attn_qkv_weight, L0_attn_qkv_bias, L0_attn_proj_weight, L0_attn_proj_bias)
    h = h + _L0_ffn_ref(_layernorm(h, axis=-1), L0_ffn_gate_w, L0_ffn_shared_gate, L0_ffn_shared_up, L0_ffn_shared_down, L0_ffn_routed_gate, L0_ffn_routed_up, L0_ffn_routed_down)
    h = h + _L1_attn_ref(_layernorm(h, axis=-1), L1_attn_W_in, L1_attn_conv_w, L1_attn_theta_raw, L1_attn_w_int_raw, L1_attn_decay_slopes, L1_attn_score_scale, L1_attn_score_bias, L1_attn_phase_scale, L1_attn_gated_norm_weight, L1_attn_W_readout, L1_attn_W_gate, L1_attn_W_out)
    h = h + _L1_ffn_ref(_layernorm(h, axis=-1), L1_ffn_ln1_g, L1_ffn_ln1_b, L1_ffn_qkv_w, L1_ffn_proj_w, L1_ffn_proj_b, L1_ffn_ln2_g, L1_ffn_ln2_b, L1_ffn_gate_w, L1_ffn_gate_b, L1_ffn_w1, L1_ffn_b1, L1_ffn_w2, L1_ffn_b2)
    return h

_drawn_inputs = setup_inputs


def setup_inputs(seed=0):
    import zlib

    import numpy as np

    out = dict(_drawn_inputs(seed))
    spreads = {'L1_attn_w_int_raw': (1.0, 0.6),
     'L1_attn_score_scale': (1.0, 0.6),
     'L1_attn_score_bias': (0.0, 0.8),
     'L1_attn_phase_scale': (1.0, 0.6),
     'L1_attn_gated_norm_weight': (1.0, 0.6),
     'L1_ffn_ln1_g': (1.0, 0.6),
     'L1_ffn_ln1_b': (0.0, 0.8),
     'L1_ffn_proj_b': (0.0, 0.8),
     'L1_ffn_ln2_g': (1.0, 0.6),
     'L1_ffn_ln2_b': (0.0, 2.0),
     'L1_ffn_gate_b': (0.0, 0.8),
     'L1_ffn_b1': (0.0, 2.0),
     'L1_ffn_b2': (0.0, 2.0)}
    factors = {'L0_tok_b': 3.659,
     'L0_attn_qkv_weight': 3.822,
     'L0_attn_qkv_bias': 5.695,
     'L0_attn_proj_weight': 3.086,
     'L1_attn_W_in': 8.0,
     'L1_attn_conv_w': 8.0,
     'L1_attn_theta_raw': 8.0,
     'L1_attn_decay_slopes': 64.0,
     'L1_attn_W_readout': 8.0,
     'L1_attn_W_gate': 8.0,
     'L1_attn_W_out': 8.0,
     'L1_ffn_qkv_w': 6.326,
     'L1_ffn_proj_w': 6.26,
     'L1_ffn_gate_w': 8.0,
     'L1_ffn_w1': 8.0,
     'L1_ffn_w2': 8.0}
    for name, (base, spread) in spreads.items():
        noise = np.random.default_rng([zlib.crc32(name.encode()), seed]).standard_normal(out[name].shape)
        drawn = base * np.exp(spread * noise) if base else spread * noise
        out[name] = jnp.asarray(drawn.astype(out[name].dtype))
    for name, factor in factors.items():
        out[name] = (out[name] * factor).astype(out[name].dtype)
    return out
```

```python
from contextlib import ExitStack, contextmanager

import numpy as np
import concourse.bass as bass
from concourse import mybir

F32 = mybir.dt.float32
BF16 = mybir.dt.bfloat16
I32 = mybir.dt.int32
ALU = mybir.AluOpType
ACT = mybir.ActivationFunctionType
X = mybir.AxisListType.X
ds = bass.ds

B, NP_, NTXT, D = 32, 16, 77, 192
L = NP_ + NTXT
T = B * L
TP = 124
TPG = 3
SPG = 4
GT = TP * TPG
G = T // GT
NTILE = T // TP
D1 = D - 128
KP = 768
HEADS, HD = 12, 16
HID, NE = 768, 8
IC = HID // 128
assert GT == SPG * L and G * GT == T


class Core:

    def __init__(self, nc, ctx):
        self.nc = nc
        self.cleared = []
        self.H = self.sb(ctx, "H", [TP, NTILE * D])
        self.x0 = self.sb(ctx, "x0", [128, T])
        self.x1 = self.sb(ctx, "x1", [D1, T])
        self.ident = self.sb(ctx, "ident", [128, 128])
        self.ones_row = self.sb(ctx, "ones_row", [1, 128])
        self.eps5 = self.sb(ctx, "eps5", [128, 1])
        self.eps6 = self.sb(ctx, "eps6", [128, 1])
        self.PS = ctx.enter_context(nc.psum_tensor("PS", [128, 8, 512], F32))

    def sb(self, ctx, name, shape, dt=F32):
        return ctx.enter_context(self.nc.sbuf_tensor(name, shape, dt))

    def sem(self, ctx, name):
        self.sems.append(self.nc.alloc_semaphore(name))
        return self.sems[-1]

    @contextmanager
    def phase(self):
        self.sems = []
        with ExitStack() as ctx:
            yield ctx
        for sem in self.sems:
            self.nc.gpsimd.sem_clear(sem)
        self.nc.extend_free_semaphores([sem.num for sem in self.cleared])
        self.cleared = self.sems


def embed(k, a):
    nc = k.nc
    KC = KP // 128
    NPT = B * NP_ // 128
    with k.phase() as ctx:
        xp = k.sb(ctx, "xp", [128, KC, B * NP_])
        wp = k.sb(ctx, "wp", [128, KC, D])
        bp = k.sb(ctx, "bp", [1, D])
        eo = k.sb(ctx, "eo", [128, NPT, D])
        loaded = k.sem(ctx, "em_loaded")
        consts = k.sem(ctx, "em_consts")
        mm = k.sem(ctx, "em_mm")
        ev = k.sem(ctx, "em_ev")
        joined = k.sem(ctx, "em_joined")
        h_in = k.sem(ctx, "em_h_in")
        with nc.Block() as block:

            @block.sync
            def _(sp):
                sp.dma_start(xp[:, :, :], a["patches"].rearrange("(c p) n -> p c n", p=128)).then_inc(loaded, 16)
                sp.dma_start(wp[:, :, :], a["tokWT"].rearrange("(c p) n -> p c n", p=128)).then_inc(loaded, 16)
                sp.dma_start(bp[:, :], a["tok_b"]).then_inc(loaded, 16)
                sp.dma_start(k.ident[:, :], a["c_ident"]).then_inc(loaded, 16)
                sp.dma_start(a["h0"][:, NP_:L, :], a["txt"]).then_inc(joined, 16)
                for m in range(NPT):
                    sp.wait_ge(ev, m + 1)
                    sp.dma_start(a["h0"][8 * m:8 * m + 8, 0:NP_, :], eo[:, m, :]).then_inc(joined, 16)
                sp.wait_ge(joined, 16 * (NPT + 1))
                sp.dma_start(k.H[:, :].rearrange("p (t d) -> p t d", d=D),
                             a["h0"].rearrange("b l d -> (b l) d").rearrange("(t p) d -> p t d", p=TP)).then_inc(h_in, 16)
                sp.wait_ge(h_in, 16)

            @block.vector
            def _(v):
                v.memset(k.ones_row[:, :], 1.0).then_inc(consts, 1)
                v.memset(k.eps5[:, :], 1e-5).then_inc(consts, 1)
                v.memset(k.eps6[:, :], 1e-6).then_inc(consts, 1)

            @block.tensor
            def _(pe):
                pe.wait_ge(loaded, 64)
                pe.wait_ge(consts, 3)
                for m in range(NPT):
                    for c in range(KC):
                        pe.matmul(k.PS[:, m, 0:D], xp[:, c, m * 128:(m + 1) * 128], wp[:, c, :],
                                  start=(c == 0), stop=False)
                    pe.matmul(k.PS[:, m, 0:D], k.ones_row[:, :], bp[:, :], start=False, stop=True).then_inc(mm, 1)

            @block.scalar
            def _(act):
                for m in range(NPT):
                    act.wait_ge(mm, m + 1)
                    act.activation(eo[:, m, :], k.PS[:, m, 0:D], ACT.Copy).then_inc(ev, 1)


def layernorm(k, tag, src, keep=None, gain=None):
    nc = k.nc
    with k.phase() as ctx:
        st = k.sb(ctx, tag + "st", [TP, NTILE * 6])
        mv = k.sb(ctx, tag + "mv", [TP, NTILE * 2])
        sd = k.sb(ctx, tag + "sd", [TP, NTILE])
        rs = k.sb(ctx, tag + "rs", [TP, NTILE])
        xt = k.sb(ctx, tag + "xt", [TP, 2, TPG * D])
        gb = k.sb(ctx, tag + "gb", [128, 4])
        stats = k.sem(ctx, tag + "stats")
        aggr = k.sem(ctx, tag + "aggr")
        sd_ready = k.sem(ctx, tag + "sd_ready")
        rs_ready = k.sem(ctx, tag + "rs_ready")
        xt_ready = k.sem(ctx, tag + "xt_ready")
        turned = k.sem(ctx, tag + "turned")
        ps_free = k.sem(ctx, tag + "ps_free")
        gb_in = k.sem(ctx, tag + "gb_in")
        with nc.Block() as block:
            if gain:
                @block.sync
                def _(sp):
                    for n, ap in enumerate(gain):
                        sp.dma_start(gb[0:128, n:n + 1], ap[0:128, :]).then_inc(gb_in, 16)
                        sp.dma_start(gb[0:D1, n + 2:n + 3], ap[128:D, :]).then_inc(gb_in, 16)

            @block.vector
            def _(v):
                with v.Fori(0, NTILE) as t:
                    v.bn_stats(st[:, ds(t * 6, 6)], src[:, ds(t * D, D)]).then_inc(stats, 1)
                v.wait_ge(stats, NTILE)
                for t in range(NTILE):
                    v.bn_aggr(mv[:, t * 2:t * 2 + 2], st[:, t * 6:t * 6 + 6]).then_inc(aggr, 1)
                v.wait_ge(sd_ready, 1)
                v.reciprocal(rs[:, :], sd[:, :]).then_inc(rs_ready, 1)
                v.wait_ge(rs_ready, 1)
                if keep is not None:
                    with v.Fori(0, NTILE) as t:
                        v.tensor_scalar(keep[:, ds(t * D, D)], src[:, ds(t * D, D)], mv[:, ds(t * 2, 1)],
                                        rs[:, ds(t, 1)], ALU.subtract, ALU.mult)
                    return
                with v.Fori(0, G // 2) as i:
                    for half in range(2):
                        v.wait_ge(turned, i * 2 + half + 1)
                        for j in range(TPG):
                            t = (i * 2 + half) * TPG + j
                            ins = v.tensor_scalar(xt[:, half, j * D:(j + 1) * D], src[:, ds(t * D, D)],
                                                  mv[:, ds(t * 2, 1)], rs[:, ds(t, 1)], ALU.subtract, ALU.mult)
                        ins.then_inc(xt_ready, 1)

            @block.tensor
            def _(pe):
                if keep is not None:
                    return
                pe.sem_inc(turned, 2)
                with pe.Fori(0, G // 2) as i:
                    for half in range(2):
                        pe.wait_ge(xt_ready, i * 2 + half + 1)
                        pe.wait_ge(ps_free, i * 2 + half + 1)
                        for j in range(TPG):
                            pe.transpose(k.PS[:, 2 * half, j * TP:(j + 1) * TP], xt[:, half, j * D:j * D + 128],
                                         k.ident[0:TP, 0:TP])
                            ins = pe.transpose(k.PS[0:D1, 2 * half + 1, j * TP:(j + 1) * TP],
                                               xt[:, half, j * D + 128:(j + 1) * D], k.ident[0:TP, 0:TP])
                        ins.then_inc(turned, 1)

            @block.scalar
            def _(act):
                act.wait_ge(aggr, NTILE)
                act.activation(sd[:, :], mv[:, :].rearrange("p (t s) -> p t s", s=2)[:, :, 1], ACT.Sqrt,
                               bias=k.eps5[0:TP, :]).then_inc(sd_ready, 1)
                if keep is not None:
                    return
                act.sem_inc(ps_free, 2)
                if gain:
                    act.wait_ge(gb_in, 64)
                with act.Fori(0, G // 2) as i:
                    for half in range(2):
                        g = i * 2 + half
                        act.wait_ge(turned, g + 3)
                        for c, (dst, n) in enumerate(((k.x0, 128), (k.x1, D1))):
                            if gain:
                                ins = act.activation(dst[:, ds(g * GT, GT)], k.PS[0:n, 2 * half + c, 0:GT], ACT.Identity,
                                                     scale=gb[0:n, 2 * c:2 * c + 1], bias=gb[0:n, 2 * c + 1:2 * c + 2])
                            else:
                                ins = act.activation(dst[:, ds(g * GT, GT)], k.PS[0:n, 2 * half + c, 0:GT], ACT.Copy)
                        ins.then_inc(ps_free, 1)


def attention(k, tag, resid, w, proj, proj_b, qk_b=None, v_b=None, smooth=False):
    nc = k.nc
    NC = HEADS // 4
    WQK = 2 * NC * 128
    WC = WQK + D
    VA = HD + 1
    with k.phase() as ctx:
        w0 = k.sb(ctx, tag + "w0", [128, WC])
        w1 = k.sb(ctx, tag + "w1", [D1, WC])
        p0 = k.sb(ctx, tag + "p0", [128, D])
        p1 = k.sb(ctx, tag + "p1", [D1, D])
        pb = k.sb(ctx, tag + "pb", [1, D])
        qkb = k.sb(ctx, tag + "qkb", [128, 2 * NC])
        vb = k.sb(ctx, tag + "vb", [1, D])
        xg0 = k.sb(ctx, tag + "xg0", [128, GT])
        xg1 = k.sb(ctx, tag + "xg1", [D1, GT])
        qT = k.sb(ctx, tag + "qT", [128, NC, GT])
        kbd = k.sb(ctx, tag + "kbd", [128, NC, SPG, 4, L])
        vo = k.sb(ctx, tag + "vo", [L, 2, HEADS, VA])
        P = k.sb(ctx, tag + "P", [L, 2, NC, 4, L])
        PT = k.sb(ctx, tag + "PT", [L, 2, NC, 4, L])
        mx = k.sb(ctx, tag + "mx", [L, 2, NC, 4])
        rz = k.sb(ctx, tag + "rz", [L, 2, HEADS])
        o = k.sb(ctx, tag + "o", [L, 2, HEADS, HD])
        oT0 = k.sb(ctx, tag + "oT0", [128, GT])
        oT1 = k.sb(ctx, tag + "oT1", [D1, GT])
        sm = k.sb(ctx, tag + "sm", [128, 16])
        names = ("w_in", "smooth_max", "smooth_ln", "smooth_sum", "smooth_exp", "smooth_cs", "smooth_inv", "smoothed",
                 "prep", "xg_ready", "qk_mm", "q_ev", "k_ev_a", "k_ev_v", "v_mm", "v_ev", "s_mm", "mx_ready",
                 "s_free", "p_ready", "p_turned", "pt_ready", "o_mm", "rz_ready", "o_ready", "o_turned", "ot_ready",
                 "y_mm", "y_added")
        s = {n: k.sem(ctx, tag + n) for n in names}
        with nc.Block() as block:
            SB, TB, VB, OB = 0, NC, 2 * NC, 2 * NC + 1

            @block.sync
            def _(sp):
                loads = [(w0[:, :], w[0:128, :]), (w1[:, :], w[128:D, :]), (p0[:, :], proj[0:128, :]),
                         (p1[:, :], proj[128:D, :]), (pb[:, :], proj_b)]
                if qk_b is not None:
                    loads += [(qkb[:, :], qk_b), (vb[:, :], v_b)]
                for dst, src in loads:
                    sp.dma_start(dst, src).then_inc(s["w_in"], 16)

            n_loads = 7 if qk_b is not None else 5

            def ready(e):
                e.wait_ge(s["w_in"], 16 * n_loads)
                e.wait_ge(s["prep"], 3)
                if smooth:
                    e.wait_ge(s["smoothed"], 4)

            @block.gpsimd
            def _(po):
                po.memset(kbd[:, :, :, :, :], 0.0).then_inc(s["prep"], 1)
                for half in range(2):
                    po.memset(vo[:, half, :, HD:VA], 1.0).then_inc(s["prep"], 1)
                if smooth:
                    po.wait_ge(s["smoothed"], 4)
                with po.Fori(0, G) as g:
                    po.wait_ge(s["v_mm"], g * SPG + 1)
                    po.tensor_copy(xg0[:, :], k.x0[:, ds(g * GT, GT)]).then_inc(s["xg_ready"], 1)
                    po.tensor_copy(xg1[:, :], k.x1[:, ds(g * GT, GT)]).then_inc(s["xg_ready"], 1)

            @block.vector
            def _(v):
                for n in ("v_mm", "o_mm", "y_added", "v_ev", "s_free", "pt_ready", "ot_ready"):
                    v.sem_inc(s[n], 1)
                if smooth:
                    v.wait_ge(s["w_in"], 16 * n_loads)
                    for c, (xx, ww, n) in enumerate(((k.x0, w0, 128), (k.x1, w1, D1))):
                        v.tensor_reduce(sm[0:n, c:c + 1], xx[:, :], X, ALU.max, apply_absolute_value=True).then_inc(s["smooth_max"], 1)
                        v.tensor_reduce(sm[0:n, 2 + c:3 + c], ww[:, :], X, ALU.max, apply_absolute_value=True).then_inc(s["smooth_max"], 1)
                    v.wait_ge(s["smooth_ln"], 4)
                    for c, n in enumerate((128, D1)):
                        v.tensor_scalar(sm[0:n, 6 + c:7 + c], sm[0:n, 6 + c:7 + c], -0.65, None, ALU.mult).then_inc(s["smooth_sum"], 1)
                    v.wait_ge(s["smooth_sum"], 2)
                    for c, n in enumerate((128, D1)):
                        v.scalar_tensor_tensor(sm[0:n, 8 + c:9 + c], sm[0:n, 4 + c:5 + c], 0.35, sm[0:n, 6 + c:7 + c],
                                               ALU.mult, ALU.add).then_inc(s["smooth_sum"], 1)
                    v.wait_ge(s["smooth_exp"], 2)
                    for c, n in enumerate((128, D1)):
                        v.tensor_scalar(sm[0:n, 10 + c:11 + c], sm[0:n, 10 + c:11 + c], 4.0 / 3.0, None, ALU.mult).then_inc(s["smooth_cs"], 1)
                    v.wait_ge(s["smooth_cs"], 2)
                    for c, n in enumerate((128, D1)):
                        v.tensor_scalar(sm[0:n, 12 + c:13 + c].bitcast(I32), sm[0:n, 10 + c:11 + c].bitcast(I32),
                                        -8388608, None, ALU.bitwise_and).then_inc(s["smooth_cs"], 1)
                    v.wait_ge(s["smooth_cs"], 4)
                    for c, n in enumerate((128, D1)):
                        v.reciprocal(sm[0:n, 14 + c:15 + c], sm[0:n, 12 + c:13 + c]).then_inc(s["smooth_inv"], 1)
                    v.wait_ge(s["smooth_inv"], 2)
                    for c, (xx, ww, n) in enumerate(((k.x0, w0, 128), (k.x1, w1, D1))):
                        v.tensor_scalar(ww[:, :], ww[:, :], sm[0:n, 12 + c:13 + c], None, ALU.mult).then_inc(s["smoothed"], 1)
                        v.tensor_scalar(xx[:, :], xx[:, :], sm[0:n, 14 + c:15 + c], None, ALU.mult).then_inc(s["smoothed"], 1)
                ready(v)
                with v.Fori(0, G) as g:
                    for c in range(NC):
                        v.wait_ge(s["qk_mm"], g * 2 * NC + NC + c + 1)
                        for j in (2, 3):
                            r = slice(32 * j, 32 * j + 32)
                            dst = kbd[r, c, :, j, :]
                            src = k.PS[r, TB + c, 0:GT].rearrange("p (s l) -> p s l", s=SPG)
                            if qk_b is not None:
                                ins = v.tensor_scalar(dst, src, qkb[r, NC + c:NC + c + 1], None, ALU.add)
                            else:
                                ins = v.tensor_copy(dst, src)
                        ins.then_inc(s["k_ev_v"], 1)

                    def softmax_shift(n):
                        u = g * SPG + n
                        h = n % 2
                        v.wait_ge(s["v_mm"], u + 2)
                        v.wait_ge(s["o_mm"], u + 1)
                        v.tensor_copy(vo[:, h, :, 0:HD], k.PS[0:L, VB, 0:D].rearrange("p (h d) -> p h d", d=HD)).then_inc(s["v_ev"], 1)
                        v.wait_ge(s["s_mm"], u + 1)
                        sc = k.PS[0:L, SB:SB + NC, 0:4 * L].rearrange("p c (j l) -> p c j l", j=4)
                        v.tensor_reduce(mx[:, h, :, :], sc, X, ALU.max).then_inc(s["mx_ready"], 1)
                        v.wait_ge(s["mx_ready"], u + 1)
                        for c in range(NC):
                            ins = v.tensor_tensor(P[:, h, c, :, :], sc[:, c, :, :],
                                                  mx[:, h, c, :].unsqueeze(2).to_broadcast([L, 4, L]), ALU.subtract)
                        ins.then_inc(s["s_free"], 1)

                    def normalise(n):
                        u = g * SPG + n
                        h = n % 2
                        v.wait_ge(s["o_mm"], u + 2)
                        oo = k.PS[0:L, OB, 0:HEADS * VA].rearrange("p (h d) -> p h d", d=VA)
                        v.reciprocal(rz[:, h, :], oo[:, :, HD]).then_inc(s["rz_ready"], 1)
                        v.wait_ge(s["rz_ready"], u + 1)
                        v.tensor_tensor(o[:, h, :, :], oo[:, :, 0:HD], rz[:, h, :].unsqueeze(2).to_broadcast([L, HEADS, HD]),
                                        ALU.mult).then_inc(s["o_ready"], 1)

                    for n in range(SPG + 1):
                        if n < SPG:
                            softmax_shift(n)
                        if n > 0:
                            normalise(n - 1)
                    v.wait_ge(s["y_mm"], g + 1)
                    for j in range(TPG):
                        r = resid[:, ds((g * TPG + j) * D, D)]
                        ins = v.tensor_tensor(r, k.PS[0:TP, SB + j, 0:D], r, ALU.add)
                    ins.then_inc(s["y_added"], 1)

            @block.scalar
            def _(act):
                if smooth:
                    act.wait_ge(s["smooth_max"], 4)
                    for c, n in enumerate((128, D1)):
                        for q in (0, 2):
                            act.activation(sm[0:n, 4 + q + c:5 + q + c], sm[0:n, q + c:q + c + 1], ACT.Ln).then_inc(s["smooth_ln"], 1)
                    act.wait_ge(s["smooth_sum"], 4)
                    for c, n in enumerate((128, D1)):
                        act.activation(sm[0:n, 10 + c:11 + c], sm[0:n, 8 + c:9 + c], ACT.Exp).then_inc(s["smooth_exp"], 1)
                ready(act)
                act.preload_act_table(ACT.Exp)
                with act.Fori(0, G) as g:
                    for c in range(NC):
                        act.wait_ge(s["qk_mm"], g * 2 * NC + c + 1)
                        if qk_b is not None:
                            ins = act.activation(qT[:, c, :], k.PS[:, SB + c, 0:GT], ACT.Identity, bias=qkb[:, c:c + 1])
                        else:
                            ins = act.activation(qT[:, c, :], k.PS[:, SB + c, 0:GT], ACT.Copy)
                        ins.then_inc(s["q_ev"], 1)
                    for c in range(NC):
                        act.wait_ge(s["qk_mm"], g * 2 * NC + NC + c + 1)
                        for j in (0, 1):
                            r = slice(32 * j, 32 * j + 32)
                            dst = kbd[r, c, :, j, :]
                            src = k.PS[r, TB + c, 0:GT].rearrange("p (s l) -> p s l", s=SPG)
                            if qk_b is not None:
                                ins = act.activation(dst, src, ACT.Identity, bias=qkb[r, NC + c:NC + c + 1])
                            else:
                                ins = act.activation(dst, src, ACT.Copy)
                        ins.then_inc(s["k_ev_a"], 1)

                    def exps(n):
                        u = g * SPG + n
                        h = n % 2
                        act.wait_ge(s["s_free"], u + 2)
                        act.activation(P[:, h, :, :, :], P[:, h, :, :, :], ACT.Exp, scale=float(HD) ** -0.5).then_inc(s["p_ready"], 1)
                        act.wait_ge(s["p_turned"], u + 1)
                        for c in range(NC):
                            ins = act.activation(PT[:, h, c, :, :], k.PS[0:L, TB + c, 0:4 * L].rearrange("p (j l) -> p j l", j=4), ACT.Copy)
                        ins.then_inc(s["pt_ready"], 1)

                    def turn_out(n):
                        u = g * SPG + n
                        act.wait_ge(s["o_turned"], u + 1)
                        act.activation(oT0[:, n * L:(n + 1) * L], k.PS[:, OB, 210:210 + L], ACT.Copy).then_inc(s["ot_ready"], 1)
                        act.activation(oT1[:, n * L:(n + 1) * L], k.PS[0:D1, OB, 310:310 + L], ACT.Copy).then_inc(s["ot_ready"], 1)

                    for n in range(SPG + 1):
                        if n < SPG:
                            exps(n)
                        if n > 0:
                            turn_out(n - 1)

            @block.tensor
            def _(pe):
                ready(pe)
                with pe.Fori(0, G) as g:
                    pe.wait_ge(s["y_added"], g + 1)
                    for half, base in ((0, SB), (1, TB)):
                        for c in range(NC):
                            wc = slice((half * NC + c) * 128, (half * NC + c + 1) * 128)
                            pe.matmul(k.PS[:, base + c, 0:GT], w0[:, wc], k.x0[:, ds(g * GT, GT)], start=True, stop=False)
                            pe.matmul(k.PS[:, base + c, 0:GT], w1[:, wc], k.x1[:, ds(g * GT, GT)], start=False, stop=True).then_inc(s["qk_mm"], 1)
                    pe.wait_ge(s["xg_ready"], g * 2 + 2)

                    def v_and_scores(n):
                        u = g * SPG + n
                        pe.wait_ge(s["v_ev"], u + 1)
                        t = slice(n * L, (n + 1) * L)
                        pe.matmul(k.PS[0:L, VB, 0:D], xg0[:, t], w0[:, WQK:WC], start=True, stop=False)
                        ins = pe.matmul(k.PS[0:L, VB, 0:D], xg1[:, t], w1[:, WQK:WC], start=False, stop=v_b is None)
                        if v_b is not None:
                            ins = pe.matmul(k.PS[0:L, VB, 0:D], k.ones_row[:, 0:L], vb[:, :], start=False, stop=True)
                        ins.then_inc(s["v_mm"], 1)
                        if n == 0:
                            pe.wait_ge(s["q_ev"], g * NC + NC)
                            pe.wait_ge(s["k_ev_a"], g * NC + NC)
                            pe.wait_ge(s["k_ev_v"], g * NC + NC)
                        pe.wait_ge(s["s_free"], u + 1)
                        for c in range(NC):
                            ins = pe.matmul(k.PS[0:L, SB + c, 0:4 * L], qT[:, c, t], kbd[:, c, n, :, :], start=True, stop=True)
                        ins.then_inc(s["s_mm"], 1)

                    def turn_p(n):
                        u = g * SPG + n
                        h = n % 2
                        pe.wait_ge(s["p_ready"], u + 1)
                        pe.wait_ge(s["pt_ready"], u + 1)
                        for c in range(NC):
                            for j in range(4):
                                ins = pe.transpose(k.PS[0:L, TB + c, j * L:(j + 1) * L], P[:, h, c, j, :], k.ident[0:L, 0:L])
                        ins.then_inc(s["p_turned"], 1)

                    def weigh(n):
                        u = g * SPG + n
                        h = n % 2
                        pe.wait_ge(s["v_ev"], u + 2)
                        pe.wait_ge(s["pt_ready"], u + 2)
                        pe.wait_ge(s["ot_ready"], 2 * u + 1)
                        for hd in range(HEADS):
                            ins = pe.matmul(k.PS[0:L, OB, hd * VA:(hd + 1) * VA], PT[:, h, hd // 4, hd % 4, :], vo[:, h, hd, :],
                                            start=True, stop=True)
                        ins.then_inc(s["o_mm"], 1)

                    def turn_o(n):
                        u = g * SPG + n
                        h = n % 2
                        pe.wait_ge(s["o_ready"], u + 1)
                        oc = o[:, h, :, :].rearrange("p h d -> p (h d)")
                        pe.transpose(k.PS[:, OB, 210:210 + L], oc[:, 0:128], k.ident[0:L, 0:L])
                        pe.transpose(k.PS[0:D1, OB, 310:310 + L], oc[:, 128:D], k.ident[0:L, 0:L]).then_inc(s["o_turned"], 1)

                    v_and_scores(0)
                    for n in range(SPG):
                        turn_p(n)
                        if n + 1 < SPG:
                            v_and_scores(n + 1)
                        weigh(n)
                        turn_o(n)
                    pe.wait_ge(s["ot_ready"], g * 2 * SPG + 2 * SPG + 1)
                    for j in range(TPG):
                        t = slice(j * TP, (j + 1) * TP)
                        pe.matmul(k.PS[0:TP, SB + j, 0:D], oT0[:, t], p0[:, :], start=True, stop=False)
                        pe.matmul(k.PS[0:TP, SB + j, 0:D], oT1[:, t], p1[:, :], start=False, stop=False)
                        ins = pe.matmul(k.PS[0:TP, SB + j, 0:D], k.ones_row[:, 0:TP], pb[:, :], start=False, stop=True)
                    ins.then_inc(s["y_mm"], 1)


def router(k, tag, cw, gate, on_softmax, gate_b=None, b2=None, n_cols=NE):
    nc = k.nc
    NTE = NTILE * NE
    with k.phase() as ctx:
        g0 = k.sb(ctx, tag + "g0", [128, 128])
        g1 = k.sb(ctx, tag + "g1", [D1, 128])
        gbias = k.sb(ctx, tag + "gbias", [128, 1])
        b2s = k.sb(ctx, tag + "b2s", [NE, D])
        lt = k.sb(ctx, tag + "lt", [128, GT])
        big = lambda n: k.sb(ctx, tag + n, [TP, NTILE, NE])
        lg, pr, key, cand, oh1, oh2, rank = (big(n) for n in ("lg", "pr", "key", "cand", "oh1", "oh2", "rank"))
        r1 = k.sb(ctx, tag + "r1", [TP, 8, NTILE])
        cwg = k.sb(ctx, tag + "cwg", [TP, TPG, NE])
        cwT = k.sb(ctx, tag + "cwT", [NE, GT])
        w_in = k.sem(ctx, tag + "w_in")
        lt_mm = k.sem(ctx, tag + "lt_mm")
        lt_ready = k.sem(ctx, tag + "lt_ready")
        l_turned = k.sem(ctx, tag + "l_turned")
        l_ready = k.sem(ctx, tag + "l_ready")
        shifted = k.sem(ctx, tag + "shifted")
        exp_ready = k.sem(ctx, tag + "exp_ready")
        step = k.sem(ctx, tag + "step")
        cwg_ready = k.sem(ctx, tag + "cwg_ready")
        cw_turned = k.sem(ctx, tag + "cw_turned")
        cwT_ready = k.sem(ctx, tag + "cwT_ready")
        b_mm = k.sem(ctx, tag + "b_mm")
        b_added = k.sem(ctx, tag + "b_added")
        n_loads = 2 + (gate_b is not None) + (b2 is not None)
        with nc.Block() as block:

            @block.sync
            def _(sp):
                sp.dma_start(g0[:, :], gate[0:128, :]).then_inc(w_in, 16)
                sp.dma_start(g1[:, :], gate[128:D, :]).then_inc(w_in, 16)
                if gate_b is not None:
                    sp.dma_start(gbias[:, :], gate_b).then_inc(w_in, 16)
                if b2 is not None:
                    sp.dma_start(b2s[:, :], b2).then_inc(w_in, 16)

            @block.tensor
            def _(pe):
                pe.wait_ge(w_in, 16 * n_loads)
                with pe.Fori(0, G) as g:
                    pe.wait_ge(lt_ready, g + 1)
                    pe.matmul(k.PS[:, 0, 0:GT], g0[:, :], k.x0[:, ds(g * GT, GT)], start=True, stop=False)
                    pe.matmul(k.PS[:, 0, 0:GT], g1[:, :], k.x1[:, ds(g * GT, GT)], start=False, stop=True).then_inc(lt_mm, 1)
                    pe.wait_ge(lt_ready, g + 2)
                    pe.wait_ge(l_ready, g + 1)
                    for j in range(TPG):
                        ins = pe.transpose(k.PS[0:TP, 1, j * 128:(j + 1) * 128], lt[:, j * TP:(j + 1) * TP], k.ident[:, :])
                    ins.then_inc(l_turned, 1)
                if b2 is None:
                    return
                with pe.Fori(0, G) as g:
                    pe.wait_ge(cwg_ready, g + 1)
                    pe.wait_ge(cwT_ready, g + 1)
                    for j in range(TPG):
                        ins = pe.transpose(k.PS[0:NE, 2, j * TP:(j + 1) * TP], cwg[:, j, :], k.ident[0:TP, 0:TP])
                    ins.then_inc(cw_turned, 1)
                    pe.wait_ge(cwT_ready, g + 2)
                    pe.wait_ge(b_added, g + 1)
                    for j in range(TPG):
                        ins = pe.matmul(k.PS[0:TP, 3 + j, 0:D], cwT[:, j * TP:(j + 1) * TP], b2s[:, :], start=True, stop=True)
                    ins.then_inc(b_mm, 1)

            @block.scalar
            def _(act):
                act.wait_ge(w_in, 16 * n_loads)
                with act.Fori(0, G) as g:
                    act.wait_ge(lt_mm, g + 1)
                    act.wait_ge(l_turned, g + 1)
                    if gate_b is not None:
                        act.activation(lt[:, :], k.PS[:, 0, 0:GT], ACT.Identity, bias=gbias[:, :]).then_inc(lt_ready, 1)
                    else:
                        act.activation(lt[:, :], k.PS[:, 0, 0:GT], ACT.Copy).then_inc(lt_ready, 1)
                    act.wait_ge(l_turned, g + 2)
                    act.activation(lg[:, ds(g * TPG, TPG), :], k.PS[0:TP, 1, 0:TPG * 128].rearrange("p (t e) -> p t e", e=128)[:, :, 0:NE], ACT.Copy).then_inc(l_ready, 1)
                act.wait_ge(shifted, 1)
                act.activation(pr[:, :, :], pr[:, :, :], ACT.Exp).then_inc(exp_ready, 1)
                if b2 is None:
                    return
                with act.Fori(0, G) as g:
                    act.wait_ge(cw_turned, g + 2)
                    act.wait_ge(b_mm, g + 1)
                    act.activation(cwT[:, :], k.PS[0:NE, 2, 0:GT], ACT.Copy).then_inc(cwT_ready, 1)

            @block.vector
            def _(v):
                for sem in (lt_ready, l_ready, l_turned, cw_turned, cwT_ready, b_added, b_mm):
                    v.sem_inc(sem, 1)
                def over(x):
                    return x.unsqueeze(2).to_broadcast([TP, NTILE, NE])

                done = 0

                def after(ins):
                    nonlocal done
                    done += 1
                    ins.then_inc(step, 1)
                    v.wait_ge(step, done)

                for e in range(NE):
                    ins = v.memset(rank[:, :, e], float(NE - e))
                after(ins)
                cwv = cw[:, :].rearrange("p (t e) -> p t e", e=n_cols)
                if n_cols > NE:
                    after(v.memset(cwv[:, :, NE:n_cols], 0.5))
                v.wait_ge(l_ready, G + 1)
                after(v.tensor_reduce(r1[:, 0, :], lg[:, :, :], X, ALU.max))
                v.tensor_tensor(pr[:, :, :], lg[:, :, :], over(r1[:, 0, :]), ALU.subtract).then_inc(shifted, 1)
                v.wait_ge(exp_ready, 1)
                if on_softmax:
                    after(v.tensor_reduce(r1[:, 1, :], pr[:, :, :], X, ALU.add))
                    after(v.reciprocal(r1[:, 2, :], r1[:, 1, :]))
                    after(v.tensor_tensor(pr[:, :, :], pr[:, :, :], over(r1[:, 2, :]), ALU.mult))
                src = pr if on_softmax else lg
                for n, oh in enumerate((oh1, oh2)):
                    after(v.tensor_reduce(r1[:, 3, :], src[:, :, :], X, ALU.max))
                    after(v.tensor_tensor(cand[:, :, :], src[:, :, :], over(r1[:, 3, :]), ALU.is_equal))
                    after(v.tensor_tensor(cand[:, :, :], cand[:, :, :], rank[:, :, :], ALU.mult))
                    after(v.tensor_reduce(r1[:, 4, :], cand[:, :, :], X, ALU.max))
                    after(v.tensor_tensor(oh[:, :, :], cand[:, :, :], over(r1[:, 4, :]), ALU.is_equal))
                    if n == 0:
                        after(v.scalar_tensor_tensor(key[:, :, :], oh[:, :, :], -1e30, src[:, :, :], ALU.mult, ALU.add))
                        src = key
                after(v.tensor_tensor(oh1[:, :, :], oh1[:, :, :], oh2[:, :, :], ALU.add))
                after(v.tensor_tensor(pr[:, :, :], pr[:, :, :], oh1[:, :, :], ALU.mult))
                after(v.tensor_reduce(r1[:, 5, :], pr[:, :, :], X, ALU.add))
                if on_softmax:
                    after(v.tensor_scalar(r1[:, 5, :], r1[:, 5, :], 1e-8, None, ALU.add))
                after(v.reciprocal(r1[:, 6, :], r1[:, 5, :]))
                after(v.tensor_tensor(cwv[:, :, 0:NE], pr[:, :, :], over(r1[:, 6, :]), ALU.mult))
                if b2 is None:
                    return
                with v.Fori(0, G) as g:
                    v.wait_ge(cw_turned, g + 1)
                    v.tensor_copy(cwg[:, :, :], cwv[:, ds(g * TPG, TPG), 0:NE]).then_inc(cwg_ready, 1)
                    v.wait_ge(b_mm, g + 2)
                    for j in range(TPG):
                        r = k.H[:, ds((g * TPG + j) * D, D)]
                        ins = v.tensor_tensor(r, k.PS[0:TP, 3 + j, 0:D], r, ALU.add)
                    ins.then_inc(b_added, 1)


def experts(k, tag, cw, n_exp, up, down, gated, b1=None):
    nc = k.nc
    NQ = 2 if gated else 1
    NU = NQ * HID
    NG = n_exp * G
    LAG = 2
    NB = 3
    assert n_exp % 2 == 0 and IC % 2 == 0 and IC % NB == 0
    with k.phase() as ctx:
        xh = k.sb(ctx, tag + "xh", [128, T], BF16)
        xl = k.sb(ctx, tag + "xl", [128, T], BF16)
        xr = k.sb(ctx, tag + "xr", [128, T], BF16)
        f0 = k.sb(ctx, tag + "f0", [128, NU])
        f1 = k.sb(ctx, tag + "f1", [128, NU])
        fd = k.sb(ctx, tag + "fd", [128, IC * D])
        uh, ul, rh, rl = (k.sb(ctx, tag + n, [128, 2, NU], BF16) for n in ("uh", "ul", "rh", "rl"))
        dh, dl = (k.sb(ctx, tag + n, [128, 2, IC * D], BF16) for n in ("dh", "dl"))
        b1s = k.sb(ctx, tag + "b1s", [128, n_exp * IC])
        sg = k.sb(ctx, tag + "sg", [128, 2, GT])
        hf = k.sb(ctx, tag + "hf", [128, 2, GT])
        hi = k.sb(ctx, tag + "hi", [128, NB, GT], BF16)
        lo = k.sb(ctx, tag + "lo", [128, NB, GT], BF16)
        b1_in = k.sem(ctx, tag + "b1_in")
        w_in = k.sem(ctx, tag + "w_in")
        x_high = k.sem(ctx, tag + "x_high")
        x_split = k.sem(ctx, tag + "x_split")
        split_begun = k.sem(ctx, tag + "split_begun")
        w_high = k.sem(ctx, tag + "w_high")
        w_split = k.sem(ctx, tag + "w_split")
        up_mm = k.sem(ctx, tag + "up_mm")
        act_ready = k.sem(ctx, tag + "act_ready")
        hf_ready = k.sem(ctx, tag + "hf_ready")
        hi_ready = k.sem(ctx, tag + "hi_ready")
        h_ready = k.sem(ctx, tag + "h_ready")
        down_mm = k.sem(ctx, tag + "down_mm")
        y_added = k.sem(ctx, tag + "y_added")
        N_LOADS = 4
        with nc.Block() as block:

            @block.sync
            def _(sp):
                if b1 is not None:
                    sp.dma_start(b1s[:, :], b1).then_inc(b1_in, 16)
                with sp.Fori(0, n_exp) as e:
                    sp.wait_ge(w_split, e + 1)
                    sp.dma_start(f0[:, :], up[ds(e, 1), 0:128, :].rearrange("a p n -> (a p) n")).then_inc(w_in, 16)
                    sp.dma_start(f1[0:D1, :], up[ds(e, 1), 128:D, :].rearrange("a p n -> (a p) n")).then_inc(w_in, 16)
                    sp.dma_start(f1[D1:2 * D1, :], up[ds(e, 1), 128:D, :].rearrange("a p n -> (a p) n")).then_inc(w_in, 16)
                    sp.dma_start(fd[:, :].rearrange("p (c n) -> p c n", n=D),
                                 down[ds(e, 1), :, :].rearrange("a (c p) n -> p (a c) n", p=128)).then_inc(w_in, 16)

            @block.gpsimd
            def _(po):
                with po.Fori(0, n_exp // 2) as ee:
                    for h in range(2):
                        e = ee * 2 + h
                        po.wait_ge(w_in, (e + 1) * (16 * N_LOADS))
                        po.wait_ge(y_added, e * (G * TPG) + 1)
                        po.sem_inc(split_begun, 1)
                        parts = ((f0, uh, ul), (f1, rh, rl), (fd, dh, dl))
                        for q, (full, high, low) in enumerate(parts):
                            po.tensor_copy(high[:, h, :], full[:, :]).then_inc(w_high, 1)
                        for q, (full, high, low) in enumerate(parts):
                            po.wait_ge(w_high, e * 3 + q + 1)
                            ins = po.tensor_tensor(low[:, h, :], full[:, :], high[:, h, :], ALU.subtract)
                        ins.then_inc(w_split, 1)

            @block.tensor
            def _(pe):
                pe.sem_inc(down_mm, NB)

                def first(h, n, c, g):
                    pe.wait_ge(hf_ready, n + 1)
                    x = ds(g * GT, GT)
                    for q in range(NQ):
                        w = slice(q * HID + c * 128, q * HID + (c + 1) * 128)
                        y = k.PS[:, 2 * (c % 2) + q, 0:GT]
                        pe.matmul(y, uh[:, h, w], xh[:, x], start=True, stop=False)
                        pe.matmul(y, uh[:, h, w], xl[:, x], start=False, stop=False)
                        pe.matmul(y, ul[:, h, w], xh[:, x], start=False, stop=False)
                        pe.matmul(y, rh[:, h, w], xr[:, x], start=False, stop=False)
                        ins = pe.matmul(y, rl[:, h, w], xr[:, x], start=False, stop=True)
                    ins.then_inc(up_mm, 1)

                def second(h, n, c, ng):
                    pe.wait_ge(h_ready, n + 3)
                    w = slice(c * D, (c + 1) * D)
                    for j in range(TPG):
                        if c == 0:
                            pe.wait_ge(y_added, ng * TPG + (j + 2 + (G - 1) * TPG))
                        y = k.PS[0:TP, 4 + j, 0:D]
                        t = slice(j * TP, (j + 1) * TP)
                        pe.matmul(y, hi[:, c % NB, t], dh[:, h, w], start=(c == 0), stop=False)
                        pe.matmul(y, hi[:, c % NB, t], dl[:, h, w], start=False, stop=False)
                        ins = pe.matmul(y, lo[:, c % NB, t], dh[:, h, w], start=False, stop=(c == IC - 1))
                    ins.then_inc(down_mm, 1)

                def group(h, g, ng, before):
                    for c in range(IC):
                        first(h, ng * IC + c, c, g)
                        if c >= LAG:
                            second(h, ng * IC + (c - LAG), c - LAG, ng)
                        elif before is not None:
                            second(before, (ng - 1) * IC + (c + IC - LAG), c + IC - LAG, ng - 1)

                def rest(h, e):
                    with pe.Fori(1, G) as g:
                        group(h, g, e * G + g, h)

                def weights(e):
                    pe.wait_ge(w_split, e + 2)

                pe.wait_ge(x_split, 2)
                weights(0)
                group(0, 0, 0, None)
                rest(0, 0)
                weights(1)
                group(1, 0, G, 0)
                rest(1, 1)
                with pe.Fori(1, n_exp // 2) as ee:
                    for h in range(2):
                        e = ee * 2 + h
                        weights(e)
                        group(h, 0, e * G, 1 - h)
                        rest(h, e)
                for c in range(IC - LAG, IC):
                    second(1, (NG - 1) * IC + c, c, NG - 1)

            @block.scalar
            def _(act):
                act.activation(xh[:, :], k.x0[:, :], ACT.Copy).then_inc(x_high, 1)
                act.activation(xr[0:D1, :], k.x1[:, :], ACT.Copy).then_inc(x_high, 1)
                if b1 is not None:
                    act.wait_ge(b1_in, 16)
                act.preload_act_table(ACT.Silu if gated else ACT.Gelu)

                def high(n, c):
                    act.wait_ge(hf_ready, n + 3)
                    act.wait_ge(down_mm, n + 1)
                    act.activation(hi[:, c % NB, :], hf[:, c % 2, :], ACT.Copy).then_inc(hi_ready, 1)

                with act.Fori(0, n_exp) as e:
                    with act.Fori(0, G) as g:
                        for c in range(IC):
                            n = (e * G + g) * IC + c
                            bank = 2 * (c % 2)
                            act.wait_ge(up_mm, n + 1)
                            if gated:
                                act.wait_ge(hf_ready, n + 1)
                                act.activation(sg[:, c % 2, :], k.PS[:, bank, 0:GT], ACT.Silu).then_inc(act_ready, 1)
                            else:
                                act.wait_ge(h_ready, n + 1)
                                act.activation(hf[:, c % 2, :], k.PS[:, bank, 0:GT], ACT.Gelu,
                                               bias=b1s[:, ds(e * IC + c, 1)]).then_inc(hf_ready, 1)
                            high(n, c)

            @block.vector
            def _(v):
                v.sem_inc(hf_ready, 2)
                v.sem_inc(h_ready, 2)
                v.sem_inc(w_split, 1)
                v.sem_inc(y_added, G * TPG + 1)
                v.wait_ge(x_high, 2)
                v.tensor_tensor(xl[:, :], k.x0[:, :], xh[:, :], ALU.subtract).then_inc(x_split, 1)
                v.tensor_tensor(xr[D1:2 * D1, :], k.x1[:, :], xr[0:D1, :], ALU.subtract).then_inc(x_split, 1)

                def low(n, c):
                    v.wait_ge(hi_ready, n + 1)
                    v.wait_ge(down_mm, n + 1)
                    v.tensor_tensor(lo[:, c % NB, :], hf[:, c % 2, :], hi[:, c % NB, :], ALU.subtract).then_inc(h_ready, 1)

                def chunk(n, c):
                    v.wait_ge(act_ready, n + 1)
                    v.wait_ge(h_ready, n + 1)
                    v.tensor_tensor(hf[:, c % 2, :], sg[:, c % 2, :], k.PS[:, 2 * (c % 2) + 1, 0:GT],
                                    ALU.mult).then_inc(hf_ready, 1)

                def add(e, g, ng):
                    v.wait_ge(down_mm, ng * IC + IC + NB)
                    for j in range(TPG):
                        t = g * TPG + j
                        r = k.H[:, ds(t * D, D)]
                        v.scalar_tensor_tensor(r, k.PS[0:TP, 4 + j, 0:D], cw[:, ds(t * n_exp + e, 1)], r,
                                               ALU.mult, ALU.add).then_inc(y_added, 1)

                def group(ng, before):
                    for c in range(IC):
                        if gated:
                            chunk(ng * IC + c, c)
                        if c == LAG - 1 and before is not None:
                            add(*before)
                        low(ng * IC + c, c)

                def rest(e):
                    with v.Fori(1, G) as g:
                        group(e * G + g, (e, g - 1, e * G + g - 1))

                group(0, None)
                rest(0)
                with v.Fori(1, n_exp) as e:
                    group(e * G, (e - 1, G - 1, e * G - 1))
                    rest(e)
                add(n_exp - 1, G - 1, NG - 1)


KH, KQ, HH = 12, 6, 64
NKC = KH // 2
NQC = KQ // 2
NZ = 1 + NKC + 2 * NQC
KS = 4
EX = 3 * HH
MAXLEN = 1024


def heads_of(c):
    return 4 * (c // 2) + c % 2, 4 * (c // 2) + 2 + c % 2


def memory_mixer(k, tag, a):
    nc = k.nc
    with k.phase() as ctx:
        wi0 = k.sb(ctx, tag + "wi0", [128, NZ * 128])
        wi1 = k.sb(ctx, tag + "wi1", [D1, NZ * 128])
        wg0 = k.sb(ctx, tag + "wg0", [128, KH * 128])
        wg1 = k.sb(ctx, tag + "wg1", [D1, KH * 128])
        wr = k.sb(ctx, tag + "wr", [128, KH, 2 * EX])
        wo = k.sb(ctx, tag + "wo", [128, KH + KH // 2, D])
        cwt = k.sb(ctx, tag + "cwt", [128, NZ, KS])
        par = k.sb(ctx, tag + "par", [128, 4, NKC])
        nw = k.sb(ctx, tag + "nw", [128, KH])
        hp = k.sb(ctx, tag + "hp", [KH, 8])
        sel = k.sb(ctx, tag + "sel", [KH, NKC, 128])
        tw = k.sb(ctx, tag + "tw", [KH, GT])
        mask = k.sb(ctx, tag + "mask", [128, GT])
        mean = k.sb(ctx, tag + "mean", [128, 128])
        halfpi = k.sb(ctx, tag + "halfpi", [128, 1])
        z = k.sb(ctx, tag + "z", [128, NZ, GT])
        sg = k.sb(ctx, tag + "sg", [128, KH, GT])
        f = k.sb(ctx, tag + "f", [128, KH, GT])
        pw, pd = (k.sb(ctx, tag + n, [KH, GT]) for n in ("pw", "pd"))
        st, sa = pw, pd
        two = lambda n: k.sb(ctx, tag + n, [128, 2, GT])
        ab, phi, cs, kvw, cc, rr, ii, re, im, m1, m2, m3, m4, sq = (two(n) for n in (
            "ab", "phi", "cs", "kvw", "cc", "rr", "ii", "re", "im", "m1", "m2", "m3", "m4", "sq"))
        sn = phi
        s0, s1, y0, y1 = cs, re, kvw, im
        rs = ab[:, 0, :]
        names = ("w_in", "set", "par_a", "par_v", "tw_a", "z_mm", "tap_a", "tap_v", "z_taken", "z_ready", "g_taken",
                 "sp_a", "sp_v", "sp_ready", "pw_ready", "id_v", "id_ready", "bc_mm", "abs_ready", "rd_v", "phi_ready",
                 "kvw_ready", "trig_a", "trig_ready", "cc_ready", "rot_ready", "run_v", "run_ready", "prod_ready",
                 "f_ready", "h_ready", "sq_ready", "ssq_mm", "sd_ready", "rs_ready", "hn_ready", "ro_mm", "sig_ready",
                 "y_ready", "wo_mm", "o_added", "par_ready", "tw_ready")
        s = {n: k.sem(ctx, tag + n) for n in names}
        N_LOADS = 14
        BC, SS, OB = 2, 4, 5
        with nc.Block() as block:

            @block.sync
            def _(sp):
                for dst, src in ((wi0[:, :], a["mm_wi"][0:128, :]), (wi1[:, :], a["mm_wi"][128:D, :]),
                                 (wg0[:, :], a["mm_wg"][0:128, :]), (wg1[:, :], a["mm_wg"][128:D, :]),
                                 (wr[:, :, :], a["mm_wr"]), (wo[:, :, :], a["mm_wo"]), (cwt[:, :, :], a["mm_cw"]),
                                 (par[:, 0:3, :], a["mm_par"]), (nw[:, :], a["mm_nw"]), (hp[:, 0:3], a["mm_hp"]),
                                 (sel[:, :, :], a["c_sel"]), (tw[:, :], a["c_dist"]), (mask[:, :], a["c_mask"]),
                                 (mean[:, :], a["c_mean"])):
                    sp.dma_start(dst, src).then_inc(s["w_in"], 16)

            @block.tensor
            def _(pe):
                pe.wait_ge(s["w_in"], 16 * N_LOADS)
                with pe.Fori(0, G) as g:
                    pe.wait_ge(s["y_ready"], g * (2 * KH) + 1)
                    for u in range(NZ + KH):
                        if 2 <= u < NZ + 2:
                            pe.wait_ge(s["z_taken"], g * NZ + (u - 1))
                        elif u >= NZ + 2:
                            pe.wait_ge(s["g_taken"], g * KH + (u - 1 - NZ))
                        w0, w1, m = (wi0, wi1, u) if u < NZ else (wg0, wg1, u - NZ)
                        wc = slice(m * 128, (m + 1) * 128)
                        pe.matmul(k.PS[:, u % 2, 0:GT], w0[:, wc], k.x0[:, ds(g * GT, GT)], start=True, stop=False)
                        pe.matmul(k.PS[:, u % 2, 0:GT], w1[:, wc], k.x1[:, ds(g * GT, GT)], start=False, stop=True).then_inc(s["z_mm"], 1)

                    def squares(c):
                        for hd in range(2):
                            n = 2 * c + hd
                            pe.wait_ge(s["sq_ready"], g * KH + n + 1)
                            pe.matmul(k.PS[:, SS, 0:GT], mean[:, :], sq[:, n % 2, :], start=(n == 0), stop=(n == KH - 1)).then_inc(s["ssq_mm"], 1)

                    for c in range(NKC):
                        pe.wait_ge(s["id_ready"], g + 1)
                        if c > 0:
                            pe.wait_ge(s["kvw_ready"], g * NKC + c)
                            pe.wait_ge(s["cc_ready"], g * NKC + c)
                        pe.matmul(k.PS[:, BC, 0:GT], sel[:, c, :], pw[:, :], start=True, stop=True)
                        pe.matmul(k.PS[:, BC + 1, 0:GT], sel[:, c, :], pd[:, :], start=True, stop=True).then_inc(s["bc_mm"], 1)
                        if c >= 2:
                            squares(c - 2)
                    squares(NKC - 2)
                    squares(NKC - 1)

                    def out_product(n):
                        for j in range(TPG):
                            t = slice(j * TP, (j + 1) * TP)
                            y = y0[:, n % 2, t] if n < KH else y1[:, n % 2, t]
                            ins = pe.matmul(k.PS[0:TP, OB + j, 0:D], y, wo[:, n, :], start=(n == 0), stop=(n == KH + KH // 2 - 1))
                        ins.then_inc(s["wo_mm"], 1)

                    for hd in range(KH + 1):
                        if hd < KH:
                            pe.wait_ge(s["hn_ready"], g * KH + hd + 1)
                            for q in range(3):
                                u = 3 * hd + q
                                if u >= 4:
                                    pe.wait_ge(s["y_ready"], g * (2 * KH) + 2 * ((u - 4) // 3) + (1 if (u - 4) % 3 < 2 else 2) + 1)
                                pe.matmul(k.PS[:, u % 4, 0:GT], wr[:, hd, q * 128:(q + 1) * 128], f[:, hd, :], start=True, stop=True).then_inc(s["ro_mm"], 1)
                        if hd >= 1:
                            e = hd - 1
                            if e == 0:
                                pe.wait_ge(s["o_added"], g + 1)
                            pe.wait_ge(s["y_ready"], g * (2 * KH) + 2 * e + 2)
                            out_product(e)
                            if e % 2:
                                pe.wait_ge(s["y_ready"], g * (2 * KH) + 2 * e + 3)
                                out_product(KH + e // 2)

            @block.scalar
            def _(act):
                act.wait_ge(s["w_in"], 16 * N_LOADS)
                act.activation(par[:, 0, :], par[:, 0, :], ACT.Sigmoid).then_inc(s["par_a"], 1)
                act.activation(par[:, 1, :], par[:, 1, :], ACT.Exp).then_inc(s["par_a"], 1)
                act.activation(hp[:, 3:4], hp[:, 2:3], ACT.Abs).then_inc(s["tw_a"], 1)
                act.wait_ge(s["tw_a"], 1)
                act.activation(hp[:, 4:5], hp[:, 3:4], ACT.Exp, scale=-1.0).then_inc(s["tw_a"], 1)
                act.wait_ge(s["tw_a"], 2)
                act.activation(hp[:, 5:6], hp[:, 4:5], ACT.Ln, bias=1.0).then_inc(s["par_a"], 1)
                act.wait_ge(s["tw_ready"], 1)
                act.activation(tw[:, :], tw[:, :], ACT.Exp, scale=hp[:, 7:8]).then_inc(s["tw_a"], 1)
                act.wait_ge(s["par_ready"], 1)
                act.wait_ge(s["set"], 1)
                with act.Fori(0, G) as g:
                    def silu_of(m):
                        n = KH if m == 0 else 128
                        act.wait_ge(s["z_taken"], g * NZ + m + 1)
                        act.activation(z[0:n, m, :], z[0:n, m, :], ACT.Silu).then_inc(s["z_ready"], 1)

                    act.wait_ge(s["prod_ready"], g * NKC + 1)
                    for m in range(NZ):
                        n = KH if m == 0 else 128
                        act.wait_ge(s["z_mm"], g * (NZ + KH) + m + 1)
                        act.activation(z[0:n, m, :], k.PS[0:n, m % 2, 0:GT], ACT.Copy, scale=cwt[0:n, m, KS - 1:KS]).then_inc(s["tap_a"], 1)
                        if m >= 1:
                            silu_of(m - 1)
                    silu_of(NZ - 1)
                    for hd in range(KH):
                        act.wait_ge(s["z_mm"], g * (NZ + KH) + NZ + hd + 1)
                        act.activation(sg[:, hd, :], k.PS[:, (NZ + hd) % 2, 0:GT], ACT.Silu).then_inc(s["g_taken"], 1)
                    act.wait_ge(s["z_ready"], g * NZ + 1)
                    act.activation(st[:, :], z[0:KH, 0, :], ACT.Identity, scale=hp[:, 0:1], bias=hp[:, 1:2]).then_inc(s["sp_a"], 1)
                    act.wait_ge(s["sp_a"], g * 3 + 1)
                    act.activation(sa[:, :], st[:, :], ACT.Abs).then_inc(s["sp_a"], 1)
                    act.wait_ge(s["sp_a"], g * 3 + 2)
                    act.activation(sa[:, :], sa[:, :], ACT.Exp, scale=-1.0).then_inc(s["sp_a"], 1)
                    act.wait_ge(s["sp_a"], g * 3 + 3)
                    act.activation(sa[:, :], sa[:, :], ACT.Ln, bias=1.0).then_inc(s["sp_ready"], 1)

                    def square(c):
                        act.wait_ge(s["h_ready"], g * NKC + c + 1)
                        for i, hd in enumerate(heads_of(c)):
                            n = 2 * c + i
                            act.wait_ge(s["ssq_mm"], g * KH + n - 1) if n >= 2 else None
                            act.activation(sq[:, n % 2, :], f[:, hd, :], ACT.Square).then_inc(s["sq_ready"], 1)

                    for c in range(NKC):
                        p = c % 2
                        act.activation(ab[:, p, :], z[:, 1 + c, :], ACT.Abs, scale=par[:, 2, c:c + 1]).then_inc(s["abs_ready"], 1)
                        act.wait_ge(s["phi_ready"], g * NKC + c + 1)
                        act.activation(cs[:, p, :], phi[:, p, :], ACT.Abs).then_inc(s["trig_a"], 1)
                        act.wait_ge(s["bc_mm"], g * NKC + c + 1)
                        act.activation(cc[:, p, :], k.PS[:, BC + 1, 0:GT], ACT.Copy, scale=par[:, 1, c:c + 1]).then_inc(s["cc_ready"], 1)
                        act.wait_ge(s["trig_a"], g * NKC + c + 1)
                        act.activation(sn[:, p, :], phi[:, p, :], ACT.Sin)
                        act.activation(cs[:, p, :], cs[:, p, :], ACT.Sin, scale=-1.0, bias=halfpi[:, :]).then_inc(s["trig_ready"], 1)
                        if c >= 2:
                            square(c - 2)
                    square(NKC - 2)
                    square(NKC - 1)
                    act.wait_ge(s["ssq_mm"], g * KH + KH)
                    act.activation(ab[:, 1, :], k.PS[:, SS, 0:GT], ACT.Sqrt, bias=k.eps6[:, :]).then_inc(s["sd_ready"], 1)
                    for hd in range(KH):
                        for q in range(2):
                            act.wait_ge(s["ro_mm"], g * (3 * KH) + 3 * hd + q + 2)
                            if hd >= 2:
                                act.wait_ge(s["y_ready"], g * (2 * KH) + 2 * (hd - 2) + 3)
                            if q == 0:
                                act.activation(s0[:, hd % 2, :], k.PS[:, (3 * hd + 1) % 4, 0:GT], ACT.Sigmoid).then_inc(s["sig_ready"], 1)
                            else:
                                gr, vr = (slice(64, 128), slice(0, 64)) if hd % 2 == 0 else (slice(0, 64), slice(64, 128))
                                act.activation(s1[vr, hd % 2, :], k.PS[gr, (3 * hd + 2) % 4, 0:GT], ACT.Sigmoid).then_inc(s["sig_ready"], 1)

            def gate(v, g, hd):
                nwo = KH + KH // 2
                v.wait_ge(s["sig_ready"], g * (2 * KH) + 2 * hd + 1)
                if hd >= 2:
                    v.wait_ge(s["wo_mm"], g * nwo + (hd - 2) + (hd - 2) // 2 + 1)
                v.tensor_tensor(y0[:, hd % 2, :], s0[:, hd % 2, :], k.PS[:, (3 * hd) % 4, 0:GT], ALU.mult).then_inc(s["y_ready"], 1)
                v.wait_ge(s["sig_ready"], g * (2 * KH) + 2 * hd + 2)
                if hd >= 4 and hd % 2 == 0:
                    v.wait_ge(s["wo_mm"], g * nwo + 3 * (hd // 2 - 1))
                vr = slice(0, 64) if hd % 2 == 0 else slice(64, 128)
                v.tensor_tensor(y1[vr, (hd // 2) % 2, :], s1[vr, hd % 2, :], k.PS[vr, (3 * hd + 2) % 4, 0:GT], ALU.mult).then_inc(s["y_ready"], 1)

            @block.vector
            def _(v):
                for n in ("y_ready", "prod_ready", "o_added"):
                    v.sem_inc(s[n], 1)
                v.memset(halfpi[:, :], float(np.pi / 2)).then_inc(s["set"], 1)
                v.wait_ge(s["par_a"], 3)
                v.tensor_scalar(par[:, 0, :], par[:, 0, :], 2.999, 0.001, ALU.mult, ALU.add).then_inc(s["par_v"], 1)
                v.tensor_scalar(par[:, 3, :], par[:, 1, :], 1e-6, None, ALU.add).then_inc(s["par_v"], 1)
                v.scalar_tensor_tensor(hp[:, 6:7], hp[:, 2:3], 0.0, hp[:, 5:6], ALU.max, ALU.add).then_inc(s["par_v"], 1)
                v.wait_ge(s["par_v"], 3)
                v.reciprocal(par[:, 3, :], par[:, 3, :]).then_inc(s["par_v"], 1)
                v.tensor_scalar(hp[:, 7:8], hp[:, 6:7], -1.0, None, ALU.mult).then_inc(s["tw_ready"], 1)
                v.wait_ge(s["par_v"], 4)
                v.scalar_tensor_tensor(par[:, 1, :], par[:, 1, :], float(HH) ** -0.5, par[:, 3, :], ALU.mult, ALU.mult).then_inc(s["par_v"], 1)
                v.wait_ge(s["par_v"], 5)
                v.tensor_tensor(par[:, 3, :], par[:, 0, :], par[:, 2, :], ALU.mult).then_inc(s["par_ready"], 1)
                v.wait_ge(s["par_ready"], 1)
                v.wait_ge(s["w_in"], 16 * N_LOADS)
                v.wait_ge(s["tw_a"], 3)
                with v.Fori(0, G) as g:
                    for m in range(NZ):
                        n = KH if m == 0 else 128
                        v.wait_ge(s["tap_a"], g * NZ + m + 1)
                        zs = z[0:n, m, :].rearrange("p (s l) -> p s l", s=SPG)
                        ps = k.PS[0:n, m % 2, 0:GT].rearrange("p (s l) -> p s l", s=SPG)
                        for q in range(1, KS):
                            ins = v.scalar_tensor_tensor(zs[:, :, q:L], ps[:, :, 0:L - q], cwt[0:n, m, KS - 1 - q:KS - q], zs[:, :, q:L],
                                                         ALU.mult, ALU.add)
                            if q < KS - 1:
                                ins.then_inc(s["tap_v"], 1)
                                v.wait_ge(s["tap_v"], g * (2 * NZ) + 2 * m + q)
                        ins.then_inc(s["z_taken"], 1)

                    v.wait_ge(s["sp_ready"], g + 1)
                    v.scalar_tensor_tensor(st[:, :], st[:, :], 0.0, sa[:, :], ALU.max, ALU.add).then_inc(s["sp_v"], 1)
                    v.wait_ge(s["sp_v"], g * 2 + 1)
                    v.tensor_tensor(st[:, :], st[:, :], tw[:, :], ALU.mult).then_inc(s["sp_v"], 1)
                    v.wait_ge(s["sp_v"], g * 2 + 2)
                    v.tensor_scalar(pw[:, :], st[:, :], 1e-4, 5000.0, ALU.max, ALU.min).then_inc(s["pw_ready"], 1)
                    v.wait_ge(s["pw_ready"], g + 1)
                    v.tensor_tensor_scan(pd[:, :], mask[0:KH, :], pw[:, :], 0.0, ALU.mult, ALU.add).then_inc(s["id_v"], 1)
                    v.wait_ge(s["id_v"], g * 2 + 1)
                    v.tensor_scalar(pd[:, :], pd[:, :], 1e-4, None, ALU.max).then_inc(s["id_v"], 1)
                    v.wait_ge(s["id_v"], g * 2 + 2)
                    v.reciprocal(pd[:, :], pd[:, :]).then_inc(s["id_ready"], 1)

                    def phase(c):
                        p = c % 2
                        i = g * NKC + c
                        kv = z[:, 1 + c, :]
                        v.wait_ge(s["abs_ready"], i + 1)
                        v.tensor_scalar(ab[:, p, :], ab[:, p, :], 1.0, None, ALU.add).then_inc(s["rd_v"], 1)
                        v.wait_ge(s["bc_mm"], i + 1)
                        v.tensor_tensor(kvw[:, p, :], kv, k.PS[:, BC, 0:GT], ALU.mult).then_inc(s["kvw_ready"], 1)
                        v.wait_ge(s["rd_v"], i * 2 + 1)
                        v.reciprocal(ab[:, p, :], ab[:, p, :]).then_inc(s["rd_v"], 1)
                        v.wait_ge(s["rd_v"], i * 2 + 2)
                        v.scalar_tensor_tensor(phi[:, p, :], kv, par[:, 3, c:c + 1], ab[:, p, :], ALU.mult, ALU.mult).then_inc(s["phi_ready"], 1)

                    def running(c):
                        p = c % 2
                        i = g * NKC + c
                        v.wait_ge(s["rot_ready"], i + 1)
                        v.tensor_tensor_scan(re[:, p, :], mask[:, :], rr[:, p, :], 0.0, ALU.mult, ALU.add).then_inc(s["run_v"], 1)
                        v.tensor_tensor_scan(im[:, p, :], mask[:, :], ii[:, p, :], 0.0, ALU.mult, ALU.add).then_inc(s["run_v"], 1)
                        v.wait_ge(s["cc_ready"], i + 1)
                        v.wait_ge(s["run_v"], i * 2 + 2)
                        v.tensor_tensor(re[:, p, :], re[:, p, :], cc[:, p, :], ALU.mult)
                        v.tensor_tensor(im[:, p, :], im[:, p, :], cc[:, p, :], ALU.mult).then_inc(s["run_ready"], 1)

                    def match(c):
                        p = c % 2
                        v.wait_ge(s["prod_ready"], g * NKC + c + 2)
                        for i, hd in enumerate(heads_of(c)):
                            r = slice(64 * i, 64 * i + 64)
                            v.tensor_tensor(f[0:64, hd, :], m1[r, p, :], m2[r, p, :], ALU.add)
                            ins = v.tensor_tensor(f[64:128, hd, :], m3[r, p, :], m4[r, p, :], ALU.subtract)
                        ins.then_inc(s["f_ready"], 1)

                    v.wait_ge(s["z_ready"], g * NZ + NZ)
                    for c in range(NKC + 2):
                        if c < NKC:
                            phase(c)
                        if 1 <= c <= NKC:
                            running(c - 1)
                        if c >= 2:
                            match(c - 2)

                    v.wait_ge(s["sd_ready"], g + 1)
                    v.reciprocal(rs, ab[:, 1, :]).then_inc(s["rs_ready"], 1)
                    v.wait_ge(s["rs_ready"], g + 1)
                    for hd in range(KH):
                        v.scalar_tensor_tensor(f[:, hd, :], f[:, hd, :], nw[:, hd:hd + 1], rs, ALU.mult, ALU.mult).then_inc(s["hn_ready"], 1)
                        if hd >= 1:
                            gate(v, g, hd - 1)
                    gate(v, g, KH - 1)
                    v.wait_ge(s["wo_mm"], (g + 1) * (KH + KH // 2))
                    for j in range(TPG):
                        r = k.H[:, ds((g * TPG + j) * D, D)]
                        ins = v.tensor_tensor(r, k.PS[0:TP, OB + j, 0:D], r, ALU.add)
                    ins.then_inc(s["o_added"], 1)

            @block.gpsimd
            def _(po):
                with po.Fori(0, G) as g:
                    def rotate(c):
                        p = c % 2
                        i = g * NKC + c
                        po.wait_ge(s["kvw_ready"], i + 1)
                        po.wait_ge(s["trig_ready"], i + 1)
                        po.tensor_tensor(rr[:, p, :], kvw[:, p, :], cs[:, p, :], ALU.mult)
                        po.tensor_tensor(ii[:, p, :], kvw[:, p, :], sn[:, p, :], ALU.mult).then_inc(s["rot_ready"], 1)

                    def products(c):
                        p = c % 2
                        i = g * NKC + c
                        po.wait_ge(s["run_ready"], i + 1)
                        qr, qi = z[:, 1 + NKC + c // 2, :], z[:, 1 + NKC + NQC + c // 2, :]
                        po.tensor_tensor(m1[:, p, :], re[:, p, :], qr, ALU.mult)
                        po.tensor_tensor(m2[:, p, :], im[:, p, :], qi, ALU.mult)
                        po.tensor_tensor(m3[:, p, :], im[:, p, :], qr, ALU.mult)
                        po.tensor_tensor(m4[:, p, :], re[:, p, :], qi, ALU.mult).then_inc(s["prod_ready"], 1)

                    def gated(c):
                        po.wait_ge(s["f_ready"], g * NKC + c + 1)
                        for hd in heads_of(c):
                            ins = po.tensor_tensor(f[:, hd, :], f[:, hd, :], sg[:, hd, :], ALU.mult)
                        ins.then_inc(s["h_ready"], 1)

                    po.wait_ge(s["g_taken"], g * KH + KH)
                    for c in range(NKC + 2):
                        if c < NKC:
                            rotate(c)
                        if 1 <= c <= NKC:
                            products(c - 1)
                        if c >= 2:
                            gated(c - 2)


def program(nc, a, out):
    with ExitStack() as ctx:
        k = Core(nc, ctx)
        embed(k, a)
        layernorm(k, "ln1_", k.H)
        attention(k, "at1_", k.H, a["at1_w"], a["at1_proj"], a["at1_proj_b"], a["at1_qk_b"], a["at1_v_b"], smooth=True)
        with ExitStack() as part:
            layernorm(k, "ln2_", k.H)
            cw = k.sb(part, "cw1", [TP, NTILE * (NE + 2)])
            router(k, "rt1_", cw, a["rt1_gate"], True, n_cols=NE + 2)
            experts(k, "ex1_", cw, NE + 2, a["ex1_up"], a["ex1_down"], True)
        layernorm(k, "ln3_", k.H)
        memory_mixer(k, "mm_", a)
        with ExitStack() as part:
            k.Zr = k.sb(part, "Zr", [TP, NTILE * D])
            layernorm(k, "ln4_", k.H, keep=k.Zr)
            layernorm(k, "ln5_", k.Zr, gain=(a["ln1_g"], a["ln1_b"]))
            attention(k, "at2_", k.Zr, a["at2_w"], a["at2_proj"], a["at2_proj_b"])
            layernorm(k, "ln6_", k.Zr, gain=(a["ln2_g"], a["ln2_b"]))
            add_branch(k)
            cw = k.sb(part, "cw2", [TP, NTILE * NE])
            router(k, "rt2_", cw, a["rt2_gate"], False, gate_b=a["rt2_gate_b"], b2=a["ex2_b2"])
            experts(k, "ex2_", cw, NE, a["ex2_up"], a["ex2_down"], False, b1=a["ex2_b1"])
        store(k, out)


def add_branch(k):
    with k.nc.Block() as block:

        @block.vector
        def _(v):
            v.tensor_tensor(k.H[:, :], k.H[:, :], k.Zr[:, :], ALU.add)


def store(k, out):
    nc = k.nc
    with k.phase() as ctx:
        stored = k.sem(ctx, "stored")
        with nc.Block() as block:

            @block.sync
            def _(sp):
                sp.dma_start(out.rearrange("b l d -> (b l) d").rearrange("(t p) d -> p t d", p=TP),
                             k.H[:, :].rearrange("p (t d) -> p t d", d=D)).then_inc(stored, 16)
                sp.wait_ge(stored, 16)


def layout(x):
    def col(v, n=1):
        return v.reshape(-1, n)

    def heads32(w):
        p = np.zeros((HEADS, 32) + w.shape[1:], w.dtype)
        p[:, 0:HD] = w.reshape((HEADS, HD) + w.shape[1:])
        return p.reshape((HEADS * 32,) + w.shape[1:])

    def qkv(w):
        return np.concatenate([heads32(w[0:D]), heads32(w[D:2 * D]), w[2 * D:3 * D]], axis=0).T

    a = {}
    a["patches"] = x["x"].reshape(B, 3, 4, 16, 4, 16).transpose(3, 5, 1, 0, 2, 4).reshape(KP, B * NP_)
    a["tokWT"] = x["L0_tok_W"].T
    a["tok_b"] = x["L0_tok_b"].reshape(1, D)
    a["txt"] = x["txt"]
    a["c_ident"] = np.eye(128, dtype=np.float32)
    a["at1_w"] = qkv(x["L0_attn_qkv_weight"])
    b = x["L0_attn_qkv_bias"]
    a["at1_qk_b"] = np.concatenate([heads32(b[0:D]), heads32(b[D:2 * D])]).reshape(6, 128).T
    a["at1_v_b"] = b[2 * D:].reshape(1, D)
    a["at1_proj"] = x["L0_attn_proj_weight"].T
    a["at1_proj_b"] = x["L0_attn_proj_bias"].reshape(1, D)
    def out128(w):
        return np.concatenate([w, np.zeros((128 - NE,) + w.shape[1:], w.dtype)])

    a["rt1_gate"] = out128(x["L0_ffn_gate_w"]).T
    gate = np.concatenate([x["L0_ffn_routed_gate"], x["L0_ffn_shared_gate"]])
    up = np.concatenate([x["L0_ffn_routed_up"], x["L0_ffn_shared_up"]])
    down = np.concatenate([x["L0_ffn_routed_down"], x["L0_ffn_shared_down"]])
    a["ex1_up"] = np.concatenate([gate, up], axis=1).transpose(0, 2, 1)
    a["ex1_down"] = down.transpose(0, 2, 1)
    pair = np.array([[heads_of(c)[i] * HH + f for i in range(2) for f in range(HH)] for c in range(NKC)])
    nk = KH * HH
    qcol = nk + KH + 2 * np.arange(KQ * HH).reshape(NQC, 128)
    def chunks(w):
        sc = np.zeros(w.shape[:-1] + (1, 128), w.dtype)
        sc[..., 0, 0:KH] = w[..., nk:nk + KH]
        return np.concatenate([sc, w[..., pair], w[..., qcol], w[..., qcol + 1]], axis=-2)
    a["mm_wi"] = chunks(x["L1_attn_W_in"]).reshape(D, NZ * 128)
    a["mm_cw"] = chunks(x["L1_attn_conv_w"]).transpose(2, 1, 0)
    ph = np.repeat(x["L1_attn_phase_scale"], HH)
    a["mm_par"] = np.stack([x["L1_attn_theta_raw"].reshape(-1)[pair], x["L1_attn_w_int_raw"].reshape(-1)[pair],
                            ph[pair]]).transpose(2, 0, 1)
    a["mm_hp"] = np.stack([x["L1_attn_score_scale"], x["L1_attn_score_bias"], x["L1_attn_decay_slopes"]], axis=1)
    a["mm_nw"] = x["L1_attn_gated_norm_weight"].reshape(KH, 128).T
    a["mm_wg"] = x["L1_attn_W_gate"]
    val, gt = np.arange(EX), EX + np.arange(EX)
    even = np.concatenate([val[:128], gt[:128], val[128:], gt[128:]])
    odd = np.concatenate([val[:128], gt[:128], gt[128:], val[128:]])
    order = np.stack([odd if h % 2 else even for h in range(KH)])
    a["mm_wr"] = np.take_along_axis(x["L1_attn_W_readout"], order[:, None, :], axis=2).transpose(1, 0, 2)
    w = x["L1_attn_W_out"].reshape(KH, EX, D)
    rest = w[:, 128:].reshape(KH // 2, 128, D)
    a["mm_wo"] = np.concatenate([w[:, :128], rest]).transpose(1, 0, 2)
    a["c_sel"] = np.zeros((KH, NKC, 128), np.float32)
    for c in range(NKC):
        for i, h in enumerate(heads_of(c)):
            a["c_sel"][h, c, HH * i:HH * i + HH] = 1
    pos = np.tile(np.arange(L), SPG)
    a["c_dist"] = np.tile((MAXLEN - 1 - pos).astype(np.float32), (KH, 1))
    a["c_mask"] = np.tile((pos > 0).astype(np.float32), (128, 1))
    a["c_mean"] = np.full((128, 128), 1.0 / (KH * 2 * HH), np.float32)
    a["ln1_g"], a["ln1_b"] = col(x["L1_ffn_ln1_g"]), col(x["L1_ffn_ln1_b"])
    a["ln2_g"], a["ln2_b"] = col(x["L1_ffn_ln2_g"]), col(x["L1_ffn_ln2_b"])
    a["at2_w"] = qkv(x["L1_ffn_qkv_w"])
    a["at2_proj"] = x["L1_ffn_proj_w"].T
    a["at2_proj_b"] = x["L1_ffn_proj_b"].reshape(1, D)
    a["rt2_gate"], a["rt2_gate_b"] = out128(x["L1_ffn_gate_w"]).T, out128(col(x["L1_ffn_gate_b"]))
    a["ex2_up"] = x["L1_ffn_w1"].transpose(0, 2, 1)
    a["ex2_b1"] = x["L1_ffn_b1"].reshape(NE * IC, 128).T
    a["ex2_down"] = x["L1_ffn_w2"].transpose(0, 2, 1)
    a["ex2_b2"] = x["L1_ffn_b2"]
    return {n: np.ascontiguousarray(v) for n, v in a.items()}


def build(nc, arrays):
    a = {n: nc.dram_tensor(n + "_dram", v.shape, F32, kind="ExternalInput").ap() for n, v in arrays.items()}
    a["h0"] = nc.dram_tensor("h0_scratch", (B, L, D), F32).ap()
    out = nc.dram_tensor("out_dram", (B, L, D), F32, kind="ExternalOutput").ap()
    program(nc, a, out)


def kernel(**inputs):
    import concourse.bacc as bacc
    from concourse.bass_utils import run_bass_kernel_spmd

    arrays = layout({n: np.asarray(v) for n, v in inputs.items()})
    nc = bacc.Bacc("TRN2", target_bir_lowering=False, num_devices=1)
    build(nc, arrays)
    r = run_bass_kernel_spmd(nc, [{n + "_dram": v for n, v in arrays.items()}], core_ids=[0])
    return r.results[0]["out_dram"]
```

```python
from contextlib import ExitStack, contextmanager

import numpy as np
import concourse.bass as bass
from concourse import mybir

F32 = mybir.dt.float32
BF16 = mybir.dt.bfloat16
I32 = mybir.dt.int32
ALU = mybir.AluOpType
ACT = mybir.ActivationFunctionType
X = mybir.AxisListType.X
ds = bass.ds

B, NP_, NTXT, D = 32, 16, 77, 192
L = NP_ + NTXT
T = B * L
TP = 124
TPG = 3
SPG = 4
GT = TP * TPG
G = T // GT
NTILE = T // TP
D1 = D - 128
KP = 768
HEADS, HD = 12, 16
HID, NE = 768, 8
IC = HID // 128
assert GT == SPG * L and G * GT == T


class Core:

    def __init__(self, nc, ctx):
        self.nc = nc
        self.cleared = []
        self.H = self.sb(ctx, "H", [TP, NTILE * D])
        self.x0 = self.sb(ctx, "x0", [128, T])
        self.x1 = self.sb(ctx, "x1", [D1, T])
        self.ident = self.sb(ctx, "ident", [128, 128])
        self.ones_row = self.sb(ctx, "ones_row", [1, 128])
        self.eps5 = self.sb(ctx, "eps5", [128, 1])
        self.eps6 = self.sb(ctx, "eps6", [128, 1])
        self.PS = ctx.enter_context(nc.psum_tensor("PS", [128, 8, 512], F32))

    def sb(self, ctx, name, shape, dt=F32):
        return ctx.enter_context(self.nc.sbuf_tensor(name, shape, dt))

    def sem(self, ctx, name):
        self.sems.append(self.nc.alloc_semaphore(name))
        return self.sems[-1]

    @contextmanager
    def phase(self):
        self.sems = []
        with ExitStack() as ctx:
            yield ctx
        for sem in self.sems:
            self.nc.gpsimd.sem_clear(sem)
        self.nc.extend_free_semaphores([sem.num for sem in self.cleared])
        self.cleared = self.sems


def embed(k, a):
    nc = k.nc
    KC = KP // 128
    NPT = B * NP_ // 128
    with k.phase() as ctx:
        xp = k.sb(ctx, "xp", [128, KC, B * NP_])
        wp = k.sb(ctx, "wp", [128, KC, D])
        bp = k.sb(ctx, "bp", [1, D])
        eo = k.sb(ctx, "eo", [128, NPT, D])
        loaded = k.sem(ctx, "em_loaded")
        consts = k.sem(ctx, "em_consts")
        mm = k.sem(ctx, "em_mm")
        ev = k.sem(ctx, "em_ev")
        joined = k.sem(ctx, "em_joined")
        h_in = k.sem(ctx, "em_h_in")
        with nc.Block() as block:

            @block.sync
            def _(sp):
                sp.dma_start(xp[:, :, :], a["patches"].rearrange("(c p) n -> p c n", p=128)).then_inc(loaded, 16)
                sp.dma_start(wp[:, :, :], a["tokWT"].rearrange("(c p) n -> p c n", p=128)).then_inc(loaded, 16)
                sp.dma_start(bp[:, :], a["tok_b"]).then_inc(loaded, 16)
                sp.dma_start(k.ident[:, :], a["c_ident"]).then_inc(loaded, 16)
                sp.dma_start(a["h0"][:, NP_:L, :], a["txt"]).then_inc(joined, 16)
                for m in range(NPT):
                    sp.wait_ge(ev, m + 1)
                    sp.dma_start(a["h0"][8 * m:8 * m + 8, 0:NP_, :], eo[:, m, :]).then_inc(joined, 16)
                sp.wait_ge(joined, 16 * (NPT + 1))
                sp.dma_start(k.H[:, :].rearrange("p (t d) -> p t d", d=D),
                             a["h0"].rearrange("b l d -> (b l) d").rearrange("(t p) d -> p t d", p=TP)).then_inc(h_in, 16)
                sp.wait_ge(h_in, 16)

            @block.vector
            def _(v):
                v.memset(k.ones_row[:, :], 1.0).then_inc(consts, 1)
                v.memset(k.eps5[:, :], 1e-5).then_inc(consts, 1)
                v.memset(k.eps6[:, :], 1e-6).then_inc(consts, 1)

            @block.tensor
            def _(pe):
                pe.wait_ge(loaded, 64)
                pe.wait_ge(consts, 3)
                for m in range(NPT):
                    for c in range(KC):
                        pe.matmul(k.PS[:, m, 0:D], xp[:, c, m * 128:(m + 1) * 128], wp[:, c, :],
                                  start=(c == 0), stop=False)
                    pe.matmul(k.PS[:, m, 0:D], k.ones_row[:, :], bp[:, :], start=False, stop=True).then_inc(mm, 1)

            @block.scalar
            def _(act):
                for m in range(NPT):
                    act.wait_ge(mm, m + 1)
                    act.activation(eo[:, m, :], k.PS[:, m, 0:D], ACT.Copy).then_inc(ev, 1)


def layernorm(k, tag, src, keep=None, gain=None):
    nc = k.nc
    with k.phase() as ctx:
        st = k.sb(ctx, tag + "st", [TP, NTILE * 6])
        mv = k.sb(ctx, tag + "mv", [TP, NTILE * 2])
        sd = k.sb(ctx, tag + "sd", [TP, NTILE])
        rs = k.sb(ctx, tag + "rs", [TP, NTILE])
        xt = k.sb(ctx, tag + "xt", [TP, 2, TPG * D])
        gb = k.sb(ctx, tag + "gb", [128, 4])
        stats = k.sem(ctx, tag + "stats")
        aggr = k.sem(ctx, tag + "aggr")
        sd_ready = k.sem(ctx, tag + "sd_ready")
        rs_ready = k.sem(ctx, tag + "rs_ready")
        xt_ready = k.sem(ctx, tag + "xt_ready")
        turned = k.sem(ctx, tag + "turned")
        ps_free = k.sem(ctx, tag + "ps_free")
        gb_in = k.sem(ctx, tag + "gb_in")
        with nc.Block() as block:
            if gain:
                @block.sync
                def _(sp):
                    for n, ap in enumerate(gain):
                        sp.dma_start(gb[0:128, n:n + 1], ap[0:128, :]).then_inc(gb_in, 16)
                        sp.dma_start(gb[0:D1, n + 2:n + 3], ap[128:D, :]).then_inc(gb_in, 16)

            @block.vector
            def _(v):
                with v.Fori(0, NTILE) as t:
                    v.bn_stats(st[:, ds(t * 6, 6)], src[:, ds(t * D, D)]).then_inc(stats, 1)
                v.wait_ge(stats, NTILE)
                for t in range(NTILE):
                    v.bn_aggr(mv[:, t * 2:t * 2 + 2], st[:, t * 6:t * 6 + 6]).then_inc(aggr, 1)
                v.wait_ge(sd_ready, 1)
                v.reciprocal(rs[:, :], sd[:, :]).then_inc(rs_ready, 1)
                v.wait_ge(rs_ready, 1)
                if keep is not None:
                    with v.Fori(0, NTILE) as t:
                        v.tensor_scalar(keep[:, ds(t * D, D)], src[:, ds(t * D, D)], mv[:, ds(t * 2, 1)],
                                        rs[:, ds(t, 1)], ALU.subtract, ALU.mult)
                    return
                with v.Fori(0, G // 2) as i:
                    for half in range(2):
                        v.wait_ge(turned, i * 2 + half + 1)
                        for j in range(TPG):
                            t = (i * 2 + half) * TPG + j
                            ins = v.tensor_scalar(xt[:, half, j * D:(j + 1) * D], src[:, ds(t * D, D)],
                                                  mv[:, ds(t * 2, 1)], rs[:, ds(t, 1)], ALU.subtract, ALU.mult)
                        ins.then_inc(xt_ready, 1)

            @block.tensor
            def _(pe):
                if keep is not None:
                    return
                pe.sem_inc(turned, 2)
                with pe.Fori(0, G // 2) as i:
                    for half in range(2):
                        pe.wait_ge(xt_ready, i * 2 + half + 1)
                        pe.wait_ge(ps_free, i * 2 + half + 1)
                        for j in range(TPG):
                            pe.transpose(k.PS[:, 2 * half, j * TP:(j + 1) * TP], xt[:, half, j * D:j * D + 128],
                                         k.ident[0:TP, 0:TP])
                            ins = pe.transpose(k.PS[0:D1, 2 * half + 1, j * TP:(j + 1) * TP],
                                               xt[:, half, j * D + 128:(j + 1) * D], k.ident[0:TP, 0:TP])
                        ins.then_inc(turned, 1)

            @block.scalar
            def _(act):
                act.wait_ge(aggr, NTILE)
                act.activation(sd[:, :], mv[:, :].rearrange("p (t s) -> p t s", s=2)[:, :, 1], ACT.Sqrt,
                               bias=k.eps5[0:TP, :]).then_inc(sd_ready, 1)
                if keep is not None:
                    return
                act.sem_inc(ps_free, 2)
                if gain:
                    act.wait_ge(gb_in, 64)
                with act.Fori(0, G // 2) as i:
                    for half in range(2):
                        g = i * 2 + half
                        act.wait_ge(turned, g + 3)
                        for c, (dst, n) in enumerate(((k.x0, 128), (k.x1, D1))):
                            if gain:
                                ins = act.activation(dst[:, ds(g * GT, GT)], k.PS[0:n, 2 * half + c, 0:GT], ACT.Identity,
                                                     scale=gb[0:n, 2 * c:2 * c + 1], bias=gb[0:n, 2 * c + 1:2 * c + 2])
                            else:
                                ins = act.activation(dst[:, ds(g * GT, GT)], k.PS[0:n, 2 * half + c, 0:GT], ACT.Copy)
                        ins.then_inc(ps_free, 1)


def attention(k, tag, resid, w, proj, proj_b, qk_b=None, v_b=None, smooth=False):
    nc = k.nc
    NC = HEADS // 4
    WQK = 2 * NC * 128
    WC = WQK + D
    VA = HD + 1
    with k.phase() as ctx:
        w0 = k.sb(ctx, tag + "w0", [128, WC])
        w1 = k.sb(ctx, tag + "w1", [D1, WC])
        p0 = k.sb(ctx, tag + "p0", [128, D])
        p1 = k.sb(ctx, tag + "p1", [D1, D])
        pb = k.sb(ctx, tag + "pb", [1, D])
        qkb = k.sb(ctx, tag + "qkb", [128, 2 * NC])
        vb = k.sb(ctx, tag + "vb", [1, D])
        xg0 = k.sb(ctx, tag + "xg0", [128, GT])
        xg1 = k.sb(ctx, tag + "xg1", [D1, GT])
        qT = k.sb(ctx, tag + "qT", [128, NC, GT])
        kbd = k.sb(ctx, tag + "kbd", [128, NC, SPG, 4, L])
        vo = k.sb(ctx, tag + "vo", [L, 2, HEADS, VA])
        P = k.sb(ctx, tag + "P", [L, 2, NC, 4, L])
        PT = k.sb(ctx, tag + "PT", [L, 2, NC, 4, L])
        mx = k.sb(ctx, tag + "mx", [L, 2, NC, 4])
        rz = k.sb(ctx, tag + "rz", [L, 2, HEADS])
        o = k.sb(ctx, tag + "o", [L, 2, HEADS, HD])
        oT0 = k.sb(ctx, tag + "oT0", [128, GT])
        oT1 = k.sb(ctx, tag + "oT1", [D1, GT])
        sm = k.sb(ctx, tag + "sm", [128, 16])
        names = ("w_in", "smooth_max", "smooth_ln", "smooth_sum", "smooth_exp", "smooth_cs", "smooth_inv", "smoothed",
                 "prep", "xg_begun", "xg_ready", "qk_mm", "q_ev", "k_ev_a", "k_ev_v", "v_mm", "v_ev", "s_mm", "mx_ready",
                 "s_free", "p_ready", "p_turned", "pt_ready", "o_mm", "rz_ready", "o_ready", "o_turned", "ot_ready",
                 "y_mm", "y_added")
        s = {n: k.sem(ctx, tag + n) for n in names}
        with nc.Block() as block:
            SB, TB, VB, OB = 0, NC, 2 * NC, 2 * NC + 1
            OT = 4 * L

            def after(e, sem, value):
                if not isinstance(value, int) or value > 0:
                    e.wait_ge(s[sem], value)

            def all_groups(e, group):
                group(0, True, False)
                with e.Fori(1, G - 1) as g:
                    group(g, False, False)
                group(G - 1, False, True)

            @block.sync
            def _(sp):
                loads = [(w0[:, :], w[0:128, :]), (w1[:, :], w[128:D, :]), (p0[:, :], proj[0:128, :]),
                         (p1[:, :], proj[128:D, :]), (pb[:, :], proj_b)]
                if qk_b is not None:
                    loads += [(qkb[:, :], qk_b), (vb[:, :], v_b)]
                for dst, src in loads:
                    sp.dma_start(dst, src).then_inc(s["w_in"], 16)

            n_loads = 7 if qk_b is not None else 5

            def ready(e):
                e.wait_ge(s["w_in"], 16 * n_loads)
                e.wait_ge(s["prep"], 3)
                if smooth:
                    e.wait_ge(s["smoothed"], 4)

            @block.gpsimd
            def _(po):
                po.memset(kbd[:, :, :, :, :], 0.0).then_inc(s["prep"], 1)
                for half in range(2):
                    po.memset(vo[:, half, :, HD:VA], 1.0).then_inc(s["prep"], 1)
                if smooth:
                    po.wait_ge(s["smoothed"], 4)

                def group(g, first, last):
                    if not first:
                        po.wait_ge(s["v_mm"], g * SPG)
                        po.sem_inc(s["xg_begun"], 1)
                    po.tensor_copy(xg0[:, :], k.x0[:, ds(g * GT, GT)]).then_inc(s["xg_ready"], 1)
                    po.tensor_copy(xg1[:, :], k.x1[:, ds(g * GT, GT)]).then_inc(s["xg_ready"], 1)

                all_groups(po, group)

            @block.vector
            def _(v):
                if smooth:
                    v.wait_ge(s["w_in"], 16 * n_loads)
                    for c, (xx, ww, n) in enumerate(((k.x0, w0, 128), (k.x1, w1, D1))):
                        v.tensor_reduce(sm[0:n, c:c + 1], xx[:, :], X, ALU.max, apply_absolute_value=True).then_inc(s["smooth_max"], 1)
                        v.tensor_reduce(sm[0:n, 2 + c:3 + c], ww[:, :], X, ALU.max, apply_absolute_value=True).then_inc(s["smooth_max"], 1)
                    v.wait_ge(s["smooth_ln"], 4)
                    for c, n in enumerate((128, D1)):
                        v.tensor_scalar(sm[0:n, 6 + c:7 + c], sm[0:n, 6 + c:7 + c], -0.65, None, ALU.mult).then_inc(s["smooth_sum"], 1)
                    v.wait_ge(s["smooth_sum"], 2)
                    for c, n in enumerate((128, D1)):
                        v.scalar_tensor_tensor(sm[0:n, 8 + c:9 + c], sm[0:n, 4 + c:5 + c], 0.35, sm[0:n, 6 + c:7 + c],
                                               ALU.mult, ALU.add).then_inc(s["smooth_sum"], 1)
                    v.wait_ge(s["smooth_exp"], 2)
                    for c, n in enumerate((128, D1)):
                        v.tensor_scalar(sm[0:n, 10 + c:11 + c], sm[0:n, 10 + c:11 + c], 4.0 / 3.0, None, ALU.mult).then_inc(s["smooth_cs"], 1)
                    v.wait_ge(s["smooth_cs"], 2)
                    for c, n in enumerate((128, D1)):
                        v.tensor_scalar(sm[0:n, 12 + c:13 + c].bitcast(I32), sm[0:n, 10 + c:11 + c].bitcast(I32),
                                        -8388608, None, ALU.bitwise_and).then_inc(s["smooth_cs"], 1)
                    v.wait_ge(s["smooth_cs"], 4)
                    for c, n in enumerate((128, D1)):
                        v.reciprocal(sm[0:n, 14 + c:15 + c], sm[0:n, 12 + c:13 + c]).then_inc(s["smooth_inv"], 1)
                    v.wait_ge(s["smooth_inv"], 2)
                    for c, (xx, ww, n) in enumerate(((k.x0, w0, 128), (k.x1, w1, D1))):
                        v.tensor_scalar(ww[:, :], ww[:, :], sm[0:n, 12 + c:13 + c], None, ALU.mult).then_inc(s["smoothed"], 1)
                        v.tensor_scalar(xx[:, :], xx[:, :], sm[0:n, 14 + c:15 + c], None, ALU.mult).then_inc(s["smoothed"], 1)
                ready(v)

                def k_blocks(g):
                    for c in range(NC):
                        v.wait_ge(s["qk_mm"], g * 2 * NC + NC + c + 1)
                        for j in (2, 3):
                            r = slice(32 * j, 32 * j + 32)
                            dst = kbd[r, c, :, j, :]
                            src = k.PS[r, TB + c, 0:GT].rearrange("p (s l) -> p s l", s=SPG)
                            if qk_b is not None:
                                ins = v.tensor_scalar(dst, src, qkb[r, NC + c:NC + c + 1], None, ALU.add)
                            else:
                                ins = v.tensor_copy(dst, src)
                        ins.then_inc(s["k_ev_v"], 1)

                def softmax_shift(u, h):
                    v.wait_ge(s["s_mm"], u + 1)
                    sc = k.PS[0:L, SB:SB + NC, 0:4 * L].rearrange("p c (j l) -> p c j l", j=4)
                    v.tensor_reduce(mx[:, h, :, :], sc, X, ALU.max).then_inc(s["mx_ready"], 1)
                    v.wait_ge(s["mx_ready"], u + 1)
                    after(v, "p_turned", u - 1)
                    for c in range(NC):
                        ins = v.tensor_tensor(P[:, h, c, :, :], sc[:, c, :, :],
                                              mx[:, h, c, :].unsqueeze(2).to_broadcast([L, 4, L]), ALU.subtract)
                    ins.then_inc(s["s_free"], 1)
                    v.wait_ge(s["v_mm"], u + 1)
                    after(v, "o_mm", u - 1)
                    v.tensor_copy(vo[:, h, :, 0:HD], k.PS[0:L, VB, 0:D].rearrange("p (h d) -> p h d", d=HD)).then_inc(s["v_ev"], 1)

                def normalise(u, h):
                    v.wait_ge(s["o_mm"], u + 1)
                    oo = k.PS[0:L, OB, 0:HEADS * VA].rearrange("p (h d) -> p h d", d=VA)
                    v.reciprocal(rz[:, h, :], oo[:, :, HD]).then_inc(s["rz_ready"], 1)
                    v.wait_ge(s["rz_ready"], u + 1)
                    after(v, "o_turned", u - 1)
                    v.tensor_tensor(o[:, h, :, :], oo[:, :, 0:HD], rz[:, h, :].unsqueeze(2).to_broadcast([L, HEADS, HD]),
                                    ALU.mult).then_inc(s["o_ready"], 1)

                def add(g):
                    v.wait_ge(s["y_mm"], g + 1)
                    for j in range(TPG):
                        r = resid[:, ds((g * TPG + j) * D, D)]
                        ins = v.tensor_tensor(r, k.PS[0:TP, TB + j, 0:D], r, ALU.add)
                    ins.then_inc(s["y_added"], 1)

                def group(g, first, last):
                    u = g * SPG
                    if first:
                        k_blocks(0)
                        softmax_shift(0, 0)
                    softmax_shift(u + 1, 1)
                    if not first:
                        normalise(u - 1, 1)
                    softmax_shift(u + 2, 0)
                    normalise(u, 0)
                    softmax_shift(u + 3, 1)
                    if not first:
                        add(g - 1)
                    normalise(u + 1, 1)
                    if not last:
                        k_blocks(g + 1)
                    normalise(u + 2, 0)
                    if not last:
                        softmax_shift(u + 4, 0)

                all_groups(v, group)
                normalise(G * SPG - 1, 1)
                add(G - 1)

            @block.scalar
            def _(act):
                if smooth:
                    act.wait_ge(s["smooth_max"], 4)
                    for c, n in enumerate((128, D1)):
                        for q in (0, 2):
                            act.activation(sm[0:n, 4 + q + c:5 + q + c], sm[0:n, q + c:q + c + 1], ACT.Ln).then_inc(s["smooth_ln"], 1)
                    act.wait_ge(s["smooth_sum"], 4)
                    for c, n in enumerate((128, D1)):
                        act.activation(sm[0:n, 10 + c:11 + c], sm[0:n, 8 + c:9 + c], ACT.Exp).then_inc(s["smooth_exp"], 1)
                ready(act)
                act.preload_act_table(ACT.Exp)

                def q_and_k(g):
                    for c in range(NC):
                        act.wait_ge(s["qk_mm"], g * 2 * NC + c + 1)
                        if qk_b is not None:
                            ins = act.activation(qT[:, c, :], k.PS[:, SB + c, 0:GT], ACT.Identity, bias=qkb[:, c:c + 1])
                        else:
                            ins = act.activation(qT[:, c, :], k.PS[:, SB + c, 0:GT], ACT.Copy)
                        ins.then_inc(s["q_ev"], 1)
                    for c in range(NC):
                        act.wait_ge(s["qk_mm"], g * 2 * NC + NC + c + 1)
                        for j in (0, 1):
                            r = slice(32 * j, 32 * j + 32)
                            dst = kbd[r, c, :, j, :]
                            src = k.PS[r, TB + c, 0:GT].rearrange("p (s l) -> p s l", s=SPG)
                            if qk_b is not None:
                                ins = act.activation(dst, src, ACT.Identity, bias=qkb[r, NC + c:NC + c + 1])
                            else:
                                ins = act.activation(dst, src, ACT.Copy)
                        ins.then_inc(s["k_ev_a"], 1)

                def exps(u, h):
                    act.wait_ge(s["s_free"], u + 1)
                    act.activation(P[:, h, :, :, :], P[:, h, :, :, :], ACT.Exp, scale=float(HD) ** -0.5).then_inc(s["p_ready"], 1)

                def turned_p(u, h):
                    act.wait_ge(s["p_turned"], u + 1)
                    after(act, "o_mm", u - 1)
                    for c in range(NC):
                        ins = act.activation(PT[:, h, c, :, :], k.PS[0:L, TB + c, 0:4 * L].rearrange("p (j l) -> p j l", j=4), ACT.Copy)
                    ins.then_inc(s["pt_ready"], 1)

                def turned_out(u, n):
                    act.wait_ge(s["o_turned"], u + 1)
                    act.activation(oT0[:, n * L:(n + 1) * L], k.PS[:, TB, OT:OT + L], ACT.Copy).then_inc(s["ot_ready"], 1)
                    act.activation(oT1[:, n * L:(n + 1) * L], k.PS[0:D1, TB + 1, OT:OT + L], ACT.Copy).then_inc(s["ot_ready"], 1)

                def group(g, first, last):
                    u = g * SPG
                    if first:
                        q_and_k(0)
                        exps(0, 0)
                    for n in range(SPG):
                        if n + 1 == SPG and not last:
                            q_and_k(g + 1)
                        if n + 1 < SPG or not last:
                            exps(u + n + 1, (n + 1) % 2)
                        turned_p(u + n, n % 2)
                        if n >= 2:
                            turned_out(u + n - 2, n - 2)
                        elif not first:
                            turned_out(u + n - 2, n + 2)

                all_groups(act, group)
                for n in (2, 3):
                    turned_out((G - 1) * SPG + n, n)

            @block.tensor
            def _(pe):
                ready(pe)

                def q_and_k(g):
                    for half, base in ((0, SB), (1, TB)):
                        for c in range(NC):
                            wc = slice((half * NC + c) * 128, (half * NC + c + 1) * 128)
                            pe.matmul(k.PS[:, base + c, 0:GT], w0[:, wc], k.x0[:, ds(g * GT, GT)], start=True, stop=False)
                            pe.matmul(k.PS[:, base + c, 0:GT], w1[:, wc], k.x1[:, ds(g * GT, GT)], start=False, stop=True).then_inc(s["qk_mm"], 1)

                def scores_and_v(g, n):
                    u = g * SPG + n
                    t = slice(n * L, (n + 1) * L)
                    if n == 0:
                        pe.wait_ge(s["q_ev"], g * NC + NC)
                        pe.wait_ge(s["k_ev_a"], g * NC + NC)
                        pe.wait_ge(s["k_ev_v"], g * NC + NC)
                        pe.wait_ge(s["xg_ready"], g * 2 + 2)
                    after(pe, "s_free", u)
                    for c in range(NC):
                        ins = pe.matmul(k.PS[0:L, SB + c, 0:4 * L], qT[:, c, t], kbd[:, c, n, :, :], start=True, stop=True)
                    ins.then_inc(s["s_mm"], 1)
                    after(pe, "v_ev", u)
                    pe.matmul(k.PS[0:L, VB, 0:D], xg0[:, t], w0[:, WQK:WC], start=True, stop=False)
                    ins = pe.matmul(k.PS[0:L, VB, 0:D], xg1[:, t], w1[:, WQK:WC], start=False, stop=v_b is None)
                    if v_b is not None:
                        ins = pe.matmul(k.PS[0:L, VB, 0:D], k.ones_row[:, 0:L], vb[:, :], start=False, stop=True)
                    ins.then_inc(s["v_mm"], 1)

                def turn(p, o_too, h):
                    after(pe, "pt_ready", p)
                    after(pe, "ot_ready", 2 * (p - 2))
                    if o_too:
                        turn_o(p - 2, h)
                    pe.wait_ge(s["p_ready"], p + 1)
                    for c in range(NC):
                        for j in range(4):
                            ins = pe.transpose(k.PS[0:L, TB + c, j * L:(j + 1) * L], P[:, h, c, j, :], k.ident[0:L, 0:L])
                    ins.then_inc(s["p_turned"], 1)

                def weigh(u, h):
                    pe.wait_ge(s["v_ev"], u + 1)
                    pe.wait_ge(s["pt_ready"], u + 1)
                    after(pe, "o_ready", u)
                    for hd in range(HEADS):
                        ins = pe.matmul(k.PS[0:L, OB, hd * VA:(hd + 1) * VA], PT[:, h, hd // 4, hd % 4, :], vo[:, h, hd, :],
                                        start=True, stop=True)
                    ins.then_inc(s["o_mm"], 1)

                def turn_o(u, h):
                    pe.wait_ge(s["o_ready"], u + 1)
                    oc = o[:, h, :, :].rearrange("p h d -> p (h d)")
                    pe.transpose(k.PS[:, TB, OT:OT + L], oc[:, 0:128], k.ident[0:L, 0:L])
                    pe.transpose(k.PS[0:D1, TB + 1, OT:OT + L], oc[:, 128:D], k.ident[0:L, 0:L]).then_inc(s["o_turned"], 1)

                def project(g):
                    pe.wait_ge(s["ot_ready"], g * 2 * SPG + 2 * SPG)
                    for j in range(TPG):
                        t = slice(j * TP, (j + 1) * TP)
                        pe.matmul(k.PS[0:TP, TB + j, 0:D], oT0[:, t], p0[:, :], start=True, stop=False)
                        pe.matmul(k.PS[0:TP, TB + j, 0:D], oT1[:, t], p1[:, :], start=False, stop=False)
                        ins = pe.matmul(k.PS[0:TP, TB + j, 0:D], k.ones_row[:, 0:TP], pb[:, :], start=False, stop=True)
                    ins.then_inc(s["y_mm"], 1)

                def group(g, first, last):
                    u = g * SPG
                    if first:
                        q_and_k(0)
                        scores_and_v(0, 0)
                    for n in range(SPG):
                        if n + 1 < SPG:
                            scores_and_v(g, n + 1)
                        elif not last:
                            pe.wait_ge(s["s_free"], u + SPG)
                            pe.wait_ge(s["pt_ready"], u + SPG - 1)
                            pe.wait_ge(s["ot_ready"], 2 * (u + 1))
                            q_and_k(g + 1)
                        if n >= 1 or not first:
                            weigh(u + n - 1, (n - 1) % 2)
                        if n + 1 == SPG and not last:
                            scores_and_v(g + 1, 0)
                        if n == 2 and not first:
                            project(g - 1)
                            pe.wait_ge(s["y_added"], g)
                        turn(u + n, n >= 2 or not first, n % 2)

                all_groups(pe, group)
                u = G * SPG
                weigh(u - 1, 1)
                pe.wait_ge(s["pt_ready"], u)
                pe.wait_ge(s["ot_ready"], 2 * (u - 2))
                turn_o(u - 2, 0)
                pe.wait_ge(s["ot_ready"], 2 * (u - 1))
                turn_o(u - 1, 1)
                project(G - 1)


class ExpertBuffers:

    def __init__(self, k, ctx, tag, up, down, n_up):
        self.up, self.down = up, down
        self.xh = k.sb(ctx, tag + "xh", [128, T], BF16)
        self.xl = k.sb(ctx, tag + "xl", [128, T], BF16)
        self.xr = k.sb(ctx, tag + "xr", [128, T], BF16)
        self.f0 = k.sb(ctx, tag + "f0", [128, n_up])
        self.f1 = k.sb(ctx, tag + "f1", [128, n_up])
        self.fd = k.sb(ctx, tag + "fd", [128, IC * D])
        self.uh, self.ul, self.rh, self.rl = (k.sb(ctx, tag + n, [128, 2, n_up], BF16) for n in ("uh", "ul", "rh", "rl"))
        self.dh, self.dl = (k.sb(ctx, tag + n, [128, 2, IC * D], BF16) for n in ("dh", "dl"))

    N_LOADS = 4

    def load(self, e):
        return ((self.f0[:, :], self.up[ds(e, 1), 0:128, :].rearrange("a p n -> (a p) n")),
                (self.f1[0:D1, :], self.up[ds(e, 1), 128:D, :].rearrange("a p n -> (a p) n")),
                (self.f1[D1:2 * D1, :], self.up[ds(e, 1), 128:D, :].rearrange("a p n -> (a p) n")),
                (self.fd[:, :].rearrange("p (c n) -> p c n", n=D),
                 self.down[ds(e, 1), :, :].rearrange("a (c p) n -> p (a c) n", p=128)))

    def parts(self):
        return (self.f0, self.uh, self.ul), (self.f1, self.rh, self.rl), (self.fd, self.dh, self.dl)


def router(k, tag, cw, gate, on_softmax, eb, gate_b=None, b2=None, n_cols=NE):
    nc = k.nc
    HT = NTILE // 2
    NB = 4
    with k.phase() as ctx:
        g0 = k.sb(ctx, tag + "g0", [128, NE])
        g1 = k.sb(ctx, tag + "g1", [D1, NE])
        gbias = k.sb(ctx, tag + "gbias", [TP, NE])
        big = lambda n: k.sb(ctx, tag + n, [TP, NTILE, NE])
        lg, pr, key, cand, oh1, oh2, rank = (big(n) for n in ("lg", "pr", "key", "cand", "oh1", "oh2", "rank"))
        r1 = k.sb(ctx, tag + "r1", [TP, 8, NTILE])
        w_in = k.sem(ctx, tag + "w_in")
        l_mm = k.sem(ctx, tag + "l_mm")
        l_ready = k.sem(ctx, tag + "l_ready")
        shifted = k.sem(ctx, tag + "shifted")
        exp_ready = k.sem(ctx, tag + "exp_ready")
        step = k.sem(ctx, tag + "step")
        e_in = k.sem(ctx, tag + "e_in")
        w_high = k.sem(ctx, tag + "w_high")
        x_high = k.sem(ctx, tag + "x_high")
        n_loads = 2 + (gate_b is not None)
        if b2 is not None:
            b2s = k.sb(ctx, tag + "b2s", [HT * NE, HT, D])
            cwT = k.sb(ctx, tag + "cwT", [HT * NE, 2, TP])
            b2_in = k.sem(ctx, tag + "b2_in")
            cw_ready = k.sem(ctx, tag + "cw_ready")
            cw_turned = k.sem(ctx, tag + "cw_turned")
            cwT_ready = k.sem(ctx, tag + "cwT_ready")
            b_mm = k.sem(ctx, tag + "b_mm")
            b_added = k.sem(ctx, tag + "b_added")
        with nc.Block() as block:

            @block.sync
            def _(sp):
                sp.dma_start(g0[:, :], gate[0:128, :]).then_inc(w_in, 16)
                sp.dma_start(g1[:, :], gate[128:D, :]).then_inc(w_in, 16)
                if gate_b is not None:
                    sp.dma_start(gbias[:, :], gate_b.to_broadcast([TP, NE])).then_inc(w_in, 16)
                for dst, src in eb.load(0):
                    sp.dma_start(dst, src).then_inc(e_in, 16)
                if b2 is not None:
                    sp.dma_start(b2s[:, :, :], b2).then_inc(b2_in, 16)

            @block.gpsimd
            def _(po):
                po.wait_ge(e_in, 16 * eb.N_LOADS)
                for full, high, low in eb.parts():
                    po.tensor_copy(high[:, 0, :], full[:, :]).then_inc(w_high, 1)
                for q, (full, high, low) in enumerate(eb.parts()):
                    po.wait_ge(w_high, q + 1)
                    po.tensor_tensor(low[:, 0, :], full[:, :], high[:, 0, :], ALU.subtract)

            @block.tensor
            def _(pe):
                pe.wait_ge(w_in, 16 * n_loads)
                for t in range(NTILE):
                    y = k.PS[0:TP, 0, t * NE:(t + 1) * NE]
                    c = slice(t * TP, (t + 1) * TP)
                    pe.matmul(y, k.x0[:, c], g0[:, :], start=True, stop=False)
                    ins = pe.matmul(y, k.x1[:, c], g1[:, :], start=False, stop=True)
                ins.then_inc(l_mm, 1)
                if b2 is None:
                    return
                pe.wait_ge(cw_ready, 1)
                for h in range(2):
                    pe.transpose(k.PS[0:HT * NE, 1 + h, 0:TP], cw[:, h * HT * NE:(h + 1) * HT * NE],
                                 k.ident[0:TP, 0:TP]).then_inc(cw_turned, 1)
                pe.wait_ge(b2_in, 16)
                for t in range(NTILE):
                    if t % HT == 0:
                        pe.wait_ge(cwT_ready, t // HT + 1)
                    if t >= NB:
                        pe.wait_ge(b_added, t - NB + 1)
                    pe.matmul(k.PS[0:TP, 3 + t % NB, 0:D], cwT[:, t // HT, :], b2s[:, t % HT, :],
                              start=True, stop=True).then_inc(b_mm, 1)

            @block.scalar
            def _(act):
                act.activation(eb.xh[:, :], k.x0[:, :], ACT.Copy).then_inc(x_high, 1)
                act.activation(eb.xr[0:D1, :], k.x1[:, :], ACT.Copy).then_inc(x_high, 1)
                act.wait_ge(l_mm, 1)
                act.activation(lg[:, :, :], k.PS[0:TP, 0, 0:NTILE * NE].rearrange("p (t e) -> p t e", e=NE), ACT.Copy).then_inc(l_ready, 1)
                act.wait_ge(shifted, 1)
                act.activation(pr[:, :, :], pr[:, :, :], ACT.Exp).then_inc(exp_ready, 1)
                if b2 is None:
                    return
                for h in range(2):
                    act.wait_ge(cw_turned, h + 1)
                    act.activation(cwT[:, h, :], k.PS[0:HT * NE, 1 + h, 0:TP], ACT.Copy).then_inc(cwT_ready, 1)

            @block.vector
            def _(v):
                v.wait_ge(x_high, 2)
                v.tensor_tensor(eb.xl[:, :], k.x0[:, :], eb.xh[:, :], ALU.subtract)
                v.tensor_tensor(eb.xr[D1:2 * D1, :], k.x1[:, :], eb.xr[0:D1, :], ALU.subtract)

                def over(x):
                    return x.unsqueeze(2).to_broadcast([TP, NTILE, NE])

                done = 0

                def after(ins):
                    nonlocal done
                    done += 1
                    ins.then_inc(step, 1)
                    v.wait_ge(step, done)

                for e in range(NE):
                    ins = v.memset(rank[:, :, e], float(NE - e))
                after(ins)
                cwv = cw[:, :].rearrange("p (t e) -> p t e", e=n_cols)
                if n_cols > NE:
                    after(v.memset(cwv[:, :, NE:n_cols], 0.5))
                v.wait_ge(l_ready, 1)
                if gate_b is not None:
                    v.wait_ge(w_in, 16 * n_loads)
                    after(v.tensor_tensor(lg[:, :, :], lg[:, :, :], gbias[:, :].unsqueeze(1).to_broadcast([TP, NTILE, NE]), ALU.add))
                after(v.tensor_reduce(r1[:, 0, :], lg[:, :, :], X, ALU.max))
                v.tensor_tensor(pr[:, :, :], lg[:, :, :], over(r1[:, 0, :]), ALU.subtract).then_inc(shifted, 1)
                v.wait_ge(exp_ready, 1)
                if on_softmax:
                    after(v.tensor_reduce(r1[:, 1, :], pr[:, :, :], X, ALU.add))
                    after(v.reciprocal(r1[:, 2, :], r1[:, 1, :]))
                    after(v.tensor_tensor(pr[:, :, :], pr[:, :, :], over(r1[:, 2, :]), ALU.mult))
                src = pr if on_softmax else lg
                for n, oh in enumerate((oh1, oh2)):
                    after(v.tensor_reduce(r1[:, 3, :], src[:, :, :], X, ALU.max))
                    after(v.tensor_tensor(cand[:, :, :], src[:, :, :], over(r1[:, 3, :]), ALU.is_equal))
                    after(v.tensor_tensor(cand[:, :, :], cand[:, :, :], rank[:, :, :], ALU.mult))
                    after(v.tensor_reduce(r1[:, 4, :], cand[:, :, :], X, ALU.max))
                    after(v.tensor_tensor(oh[:, :, :], cand[:, :, :], over(r1[:, 4, :]), ALU.is_equal))
                    if n == 0:
                        after(v.scalar_tensor_tensor(key[:, :, :], oh[:, :, :], -1e30, src[:, :, :], ALU.mult, ALU.add))
                        src = key
                after(v.tensor_tensor(oh1[:, :, :], oh1[:, :, :], oh2[:, :, :], ALU.add))
                after(v.tensor_tensor(pr[:, :, :], pr[:, :, :], oh1[:, :, :], ALU.mult))
                after(v.tensor_reduce(r1[:, 5, :], pr[:, :, :], X, ALU.add))
                if on_softmax:
                    after(v.tensor_scalar(r1[:, 5, :], r1[:, 5, :], 1e-8, None, ALU.add))
                after(v.reciprocal(r1[:, 6, :], r1[:, 5, :]))
                after(v.tensor_tensor(cwv[:, :, 0:NE], pr[:, :, :], over(r1[:, 6, :]), ALU.mult))
                if b2 is None:
                    return
                v.sem_inc(cw_ready, 1)
                for t in range(NTILE):
                    v.wait_ge(b_mm, t + 1)
                    r = k.H[:, t * D:(t + 1) * D]
                    v.tensor_tensor(r, k.PS[0:TP, 3 + t % NB, 0:D], r, ALU.add).then_inc(b_added, 1)


def experts(k, tag, cw, n_exp, eb, gated, b1=None):
    nc = k.nc
    NQ = 2 if gated else 1
    NU = NQ * HID
    NG = n_exp * G
    LAG = 2
    NB = 3
    assert n_exp % 2 == 0 and IC % 2 == 0 and IC % NB == 0
    with k.phase() as ctx:
        xh, xl, xr, uh, ul, rh, rl, dh, dl = eb.xh, eb.xl, eb.xr, eb.uh, eb.ul, eb.rh, eb.rl, eb.dh, eb.dl
        b1s = k.sb(ctx, tag + "b1s", [128, n_exp * IC])
        sg = k.sb(ctx, tag + "sg", [128, 2, GT])
        hf = k.sb(ctx, tag + "hf", [128, 2, GT])
        hi = k.sb(ctx, tag + "hi", [128, NB, GT], BF16)
        lo = k.sb(ctx, tag + "lo", [128, NB, GT], BF16)
        b1_in = k.sem(ctx, tag + "b1_in")
        w_in = k.sem(ctx, tag + "w_in")
        split_begun = k.sem(ctx, tag + "split_begun")
        w_high = k.sem(ctx, tag + "w_high")
        w_split = k.sem(ctx, tag + "w_split")
        up_mm = k.sem(ctx, tag + "up_mm")
        act_ready = k.sem(ctx, tag + "act_ready")
        hf_ready = k.sem(ctx, tag + "hf_ready")
        hi_ready = k.sem(ctx, tag + "hi_ready")
        h_ready = k.sem(ctx, tag + "h_ready")
        down_mm = k.sem(ctx, tag + "down_mm")
        y_added = k.sem(ctx, tag + "y_added")
        with nc.Block() as block:

            @block.sync
            def _(sp):
                if b1 is not None:
                    sp.dma_start(b1s[:, :], b1).then_inc(b1_in, 16)
                with sp.Fori(1, n_exp) as e:
                    sp.wait_ge(w_split, e + 1)
                    for dst, src in eb.load(e):
                        sp.dma_start(dst, src).then_inc(w_in, 16)

            @block.gpsimd
            def _(po):
                def split(e, h):
                    po.wait_ge(w_in, e * (16 * eb.N_LOADS))
                    po.wait_ge(y_added, e * (G * TPG) + 1)
                    po.sem_inc(split_begun, 1)
                    for full, high, low in eb.parts():
                        po.tensor_copy(high[:, h, :], full[:, :]).then_inc(w_high, 1)
                    for q, (full, high, low) in enumerate(eb.parts()):
                        po.wait_ge(w_high, (e - 1) * 3 + q + 1)
                        ins = po.tensor_tensor(low[:, h, :], full[:, :], high[:, h, :], ALU.subtract)
                    ins.then_inc(w_split, 1)

                split(1, 1)
                with po.Fori(1, n_exp // 2) as ee:
                    for h in range(2):
                        split(ee * 2 + h, h)

            @block.tensor
            def _(pe):
                pe.sem_inc(down_mm, NB)

                def first(h, n, c, g):
                    pe.wait_ge(hf_ready, n + 1)
                    x = ds(g * GT, GT)
                    for q in range(NQ):
                        w = slice(q * HID + c * 128, q * HID + (c + 1) * 128)
                        y = k.PS[:, 2 * (c % 2) + q, 0:GT]
                        pe.matmul(y, uh[:, h, w], xh[:, x], start=True, stop=False)
                        pe.matmul(y, uh[:, h, w], xl[:, x], start=False, stop=False)
                        pe.matmul(y, ul[:, h, w], xh[:, x], start=False, stop=False)
                        pe.matmul(y, rh[:, h, w], xr[:, x], start=False, stop=False)
                        ins = pe.matmul(y, rl[:, h, w], xr[:, x], start=False, stop=True)
                    ins.then_inc(up_mm, 1)

                def second(h, n, c, ng):
                    pe.wait_ge(h_ready, n + 3)
                    w = slice(c * D, (c + 1) * D)
                    for j in range(TPG):
                        if c == 0:
                            pe.wait_ge(y_added, ng * TPG + (j + 2 + (G - 1) * TPG))
                        y = k.PS[0:TP, 4 + j, 0:D]
                        t = slice(j * TP, (j + 1) * TP)
                        pe.matmul(y, hi[:, c % NB, t], dh[:, h, w], start=(c == 0), stop=False)
                        pe.matmul(y, hi[:, c % NB, t], dl[:, h, w], start=False, stop=False)
                        ins = pe.matmul(y, lo[:, c % NB, t], dh[:, h, w], start=False, stop=(c == IC - 1))
                    ins.then_inc(down_mm, 1)

                def group(h, g, ng, before):
                    for c in range(IC):
                        first(h, ng * IC + c, c, g)
                        if c >= LAG:
                            second(h, ng * IC + (c - LAG), c - LAG, ng)
                        elif before is not None:
                            second(before, (ng - 1) * IC + (c + IC - LAG), c + IC - LAG, ng - 1)

                def rest(h, e):
                    with pe.Fori(1, G) as g:
                        group(h, g, e * G + g, h)

                def weights(e):
                    pe.wait_ge(w_split, e + 2)

                weights(0)
                group(0, 0, 0, None)
                rest(0, 0)
                weights(1)
                group(1, 0, G, 0)
                rest(1, 1)
                with pe.Fori(1, n_exp // 2) as ee:
                    for h in range(2):
                        e = ee * 2 + h
                        weights(e)
                        group(h, 0, e * G, 1 - h)
                        rest(h, e)
                for c in range(IC - LAG, IC):
                    second(1, (NG - 1) * IC + c, c, NG - 1)

            @block.scalar
            def _(act):
                if b1 is not None:
                    act.wait_ge(b1_in, 16)
                act.preload_act_table(ACT.Silu if gated else ACT.Gelu)

                def high(n, c):
                    act.wait_ge(hf_ready, n + 3)
                    act.wait_ge(down_mm, n + 1)
                    act.activation(hi[:, c % NB, :], hf[:, c % 2, :], ACT.Copy).then_inc(hi_ready, 1)

                with act.Fori(0, n_exp) as e:
                    with act.Fori(0, G) as g:
                        for c in range(IC):
                            n = (e * G + g) * IC + c
                            bank = 2 * (c % 2)
                            act.wait_ge(up_mm, n + 1)
                            if gated:
                                act.wait_ge(hf_ready, n + 1)
                                act.activation(sg[:, c % 2, :], k.PS[:, bank, 0:GT], ACT.Silu).then_inc(act_ready, 1)
                            else:
                                act.wait_ge(h_ready, n + 1)
                                act.activation(hf[:, c % 2, :], k.PS[:, bank, 0:GT], ACT.Gelu,
                                               bias=b1s[:, ds(e * IC + c, 1)]).then_inc(hf_ready, 1)
                            high(n, c)

            @block.vector
            def _(v):
                v.sem_inc(hf_ready, 2)
                v.sem_inc(h_ready, 2)
                v.sem_inc(w_split, 2)
                v.sem_inc(y_added, G * TPG + 1)

                def low(n, c):
                    v.wait_ge(hi_ready, n + 1)
                    v.wait_ge(down_mm, n + 1)
                    v.tensor_tensor(lo[:, c % NB, :], hf[:, c % 2, :], hi[:, c % NB, :], ALU.subtract).then_inc(h_ready, 1)

                def chunk(n, c):
                    v.wait_ge(act_ready, n + 1)
                    v.wait_ge(h_ready, n + 1)
                    v.tensor_tensor(hf[:, c % 2, :], sg[:, c % 2, :], k.PS[:, 2 * (c % 2) + 1, 0:GT],
                                    ALU.mult).then_inc(hf_ready, 1)

                def add(e, g, ng):
                    v.wait_ge(down_mm, ng * IC + IC + NB)
                    for j in range(TPG):
                        t = g * TPG + j
                        r = k.H[:, ds(t * D, D)]
                        v.scalar_tensor_tensor(r, k.PS[0:TP, 4 + j, 0:D], cw[:, ds(t * n_exp + e, 1)], r,
                                               ALU.mult, ALU.add).then_inc(y_added, 1)

                def group(ng, before):
                    for c in range(IC):
                        if gated:
                            chunk(ng * IC + c, c)
                        if c == LAG - 1 and before is not None:
                            add(*before)
                        low(ng * IC + c, c)

                def rest(e):
                    with v.Fori(1, G) as g:
                        group(e * G + g, (e, g - 1, e * G + g - 1))

                group(0, None)
                rest(0)
                with v.Fori(1, n_exp) as e:
                    group(e * G, (e - 1, G - 1, e * G - 1))
                    rest(e)
                add(n_exp - 1, G - 1, NG - 1)


KH, KQ, HH = 12, 6, 64
NKC = KH // 2
NQC = KQ // 2
NZ = 1 + NKC + 2 * NQC
KS = 4
EX = 3 * HH
MAXLEN = 1024


def heads_of(c):
    return 4 * (c // 2) + c % 2, 4 * (c // 2) + 2 + c % 2


def memory_mixer(k, tag, a):
    nc = k.nc
    NWO = 3 * NKC
    with k.phase() as ctx:
        wi0 = k.sb(ctx, tag + "wi0", [128, NZ * 128])
        wi1 = k.sb(ctx, tag + "wi1", [D1, NZ * 128])
        wg0 = k.sb(ctx, tag + "wg0", [128, KH * 128])
        wg1 = k.sb(ctx, tag + "wg1", [D1, KH * 128])
        wr = k.sb(ctx, tag + "wr", [128, KH, 2 * EX])
        wo = k.sb(ctx, tag + "wo", [128, NWO, D])
        cwt = k.sb(ctx, tag + "cwt", [128, NZ, KS])
        par = k.sb(ctx, tag + "par", [128, 4, NKC])
        nw = k.sb(ctx, tag + "nw", [128, KH])
        hp = k.sb(ctx, tag + "hp", [KH, 8])
        sel = k.sb(ctx, tag + "sel", [KH, NKC, 128])
        tw = k.sb(ctx, tag + "tw", [KH, GT])
        mask = k.sb(ctx, tag + "mask", [128, GT])
        mean = k.sb(ctx, tag + "mean", [128, 128])
        halfpi = k.sb(ctx, tag + "halfpi", [128, 1])
        z = k.sb(ctx, tag + "z", [128, NZ, GT])
        r = k.sb(ctx, tag + "r", [128, NKC, GT])
        f = k.sb(ctx, tag + "f", [128, KH, GT])
        pw, pd = (k.sb(ctx, tag + n, [KH, GT]) for n in ("pw", "pd"))
        st, sa = pw, pd
        one = lambda n: k.sb(ctx, tag + n, [128, GT])
        two = lambda n: k.sb(ctx, tag + n, [128, 2, GT])
        four = lambda n: k.sb(ctx, tag + n, [128, 2, 2, GT])
        ab, t1, rq, rn, rs = (one(n) for n in ("ab", "t1", "rq", "rn", "rs"))
        kvw, cc, sq, t0, y0, y1 = (two(n) for n in ("kvw", "cc", "sq", "t0", "y0", "y1"))
        sg, cs, ri, ma, mb = (four(n) for n in ("sg", "cs", "ri", "ma", "mb"))
        names = ("w_in", "w_late", "set", "wr_scaled", "wo_scaled", "par_a", "par_v", "tw_a", "z_mm", "tap_a", "tap_v", "z_taken",
                 "z_ready", "q_ready", "sp_a", "sp_v", "sp_ready", "pw_ready", "id_v", "id_ready", "r_a", "r_ready", "bc_mm",
                 "g_mm", "g_ready", "abs_ready", "newton", "phi_ready", "kvw_ready", "trig_a", "trig_ready", "cc_ready",
                 "rot_ready", "run_v", "run_ready", "prod_ready", "f_ready", "h_ready", "sq_ready", "ssq_mm", "rs_a",
                 "rs_v", "rs_ready", "hn_ready", "ro_mm", "th_ready", "y_ready", "wo_mm", "o_added", "par_ready",
                 "tw_ready")
        s = {n: k.sem(ctx, tag + n) for n in names}
        TH0, Y0, WO0, ADD0 = 2, 4, 4, 1
        N_EARLY, N_LATE = 11, 3
        BC, SS, RO, OB = 2, 3, 4, 6
        out_tile = lambda j: k.PS[0:TP, OB + j // 2, (j % 2) * D:(j % 2 + 1) * D]

        def after(e, sem, value):
            if not isinstance(value, int) or value > 0:
                e.wait_ge(s[sem], value)

        with nc.Block() as block:

            @block.sync
            def _(sp):
                for dst, src in ((wi0[:, :], a["mm_wi"][0:128, :]), (wi1[:, :], a["mm_wi"][128:D, :]),
                                 (cwt[:, :, :], a["mm_cw"]),
                                 (par[:, 0:3, :], a["mm_par"]), (hp[:, 0:3], a["mm_hp"]),
                                 (sel[:, :, :], a["c_sel"]), (tw[:, :], a["c_dist"]), (mask[:, :], a["c_mask"]),
                                 (mean[:, :], a["c_mean"]),
                                 (wg0[:, :], a["mm_wg"][0:128, :]), (wg1[:, :], a["mm_wg"][128:D, :])):
                    sp.dma_start(dst, src).then_inc(s["w_in"], 16)
                for dst, src in ((nw[:, :], a["mm_nw"]), (wr[:, :, :], a["mm_wr"]), (wo[:, :, :], a["mm_wo"])):
                    sp.dma_start(dst, src).then_inc(s["w_late"], 16)

            @block.tensor
            def _(pe):
                pe.sem_inc(s["wo_mm"], WO0)

                def conv(g, m):
                    after(pe, "z_taken", g * NZ + (m - 1 if m >= 2 else 0))
                    wc = slice(m * 128, (m + 1) * 128)
                    pe.matmul(k.PS[:, m % 2, 0:GT], wi0[:, wc], k.x0[:, ds(g * GT, GT)], start=True, stop=False)
                    pe.matmul(k.PS[:, m % 2, 0:GT], wi1[:, wc], k.x1[:, ds(g * GT, GT)], start=False, stop=True).then_inc(s["z_mm"], 1)

                def weight(g, c):
                    if c == 0:
                        pe.wait_ge(s["id_ready"], g + 1)
                        after(pe, "g_ready", g * KH)
                    elif c == 1:
                        pe.wait_ge(s["cc_ready"], g * NKC + 1)
                    else:
                        pe.wait_ge(s["g_ready"], g * KH + 2 * (c - 1))
                    pe.matmul(k.PS[:, BC, 0:GT], sel[:, c, :], pw[:, :], start=True, stop=True).then_inc(s["bc_mm"], 1)

                def inverse_sum(g, c):
                    pe.wait_ge(s["kvw_ready"], g * NKC + c + 1)
                    pe.matmul(k.PS[:, BC, 0:GT], sel[:, c, :], pd[:, :], start=True, stop=True).then_inc(s["bc_mm"], 1)

                def gate(g, c, i):
                    if i == 1:
                        pe.wait_ge(s["g_ready"], g * KH + 2 * c + 1)
                    elif c + 1 < NKC:
                        pe.wait_ge(s["cc_ready"], g * NKC + c + 2)
                    else:
                        pe.wait_ge(s["g_ready"], g * KH + 2 * c)
                    hd = heads_of(c)[i]
                    wc = slice(hd * 128, (hd + 1) * 128)
                    pe.matmul(k.PS[:, BC, 0:GT], wg0[:, wc], k.x0[:, ds(g * GT, GT)], start=True, stop=False)
                    pe.matmul(k.PS[:, BC, 0:GT], wg1[:, wc], k.x1[:, ds(g * GT, GT)], start=False, stop=True).then_inc(s["g_mm"], 1)

                def squares(g, c):
                    for n in (2 * c, 2 * c + 1):
                        if n == 0:
                            after(pe, "rs_ready", g)
                        pe.wait_ge(s["sq_ready"], g * KH + n + 1)
                        pe.matmul(k.PS[:, SS, 0:GT], mean[:, :], sq[:, n % 2, :], start=(n == 0), stop=(n == KH - 1)).then_inc(s["ssq_mm"], 1)

                def readout(g, c, i, q):
                    n = 2 * c + i
                    if q == 0:
                        pe.wait_ge(s["hn_ready"], g * KH + n + 1)
                        pe.wait_ge(s["th_ready"], g * (2 * KH) + (2 * (n - 1) + 1 + TH0))
                    elif q == 1:
                        pe.wait_ge(s["y_ready"], g * (2 * KH) + (2 * (n - 1) + 2 + Y0))
                    else:
                        pe.wait_ge(s["y_ready"], g * (2 * KH) + (2 * n + 1 + Y0))
                    hd = heads_of(c)[i]
                    pe.matmul(k.PS[:, RO + (3 * i + q) % 2, 0:GT], wr[:, hd, q * 128:(q + 1) * 128], f[:, hd, :],
                              start=True, stop=True).then_inc(s["ro_mm"], 1)

                def out_product(g, c, q):
                    if c == 0 and q == 0:
                        pe.wait_ge(s["o_added"], g + ADD0)
                        pe.wait_ge(s["wo_scaled"], 1)
                    pe.wait_ge(s["y_ready"], g * (2 * KH) + (4 * c + (1, 3, 4)[q] + Y0))
                    n = 3 * c + q
                    for j in range(TPG):
                        t = slice(j * TP, (j + 1) * TP)
                        y = y0[:, q, t] if q < 2 else y1[:, c % 2, t]
                        ins = pe.matmul(out_tile(j), y, wo[:, n, :], start=(n == 0 and j != 1), stop=(n == NWO - 1 and j != 0))
                    ins.then_inc(s["wo_mm"], 1)

                def round_of(A, B, C):
                    for t in range(NKC):
                        if B is not None:
                            weight(B, t)
                        if C is not None:
                            readout(C, t, 0, 0)
                            readout(C, t, 0, 1)
                        if C is not None and t >= 1:
                            for q in range(3):
                                out_product(C, t - 1, q)
                        if B is not None:
                            inverse_sum(B, t)
                        if A is not None:
                            conv(A, t)
                        if C is not None:
                            readout(C, t, 0, 2)
                            readout(C, t, 1, 0)
                        if B is not None and t >= 1:
                            gate(B, t - 1, 0)
                        if C is not None:
                            readout(C, t, 1, 1)
                        if B is not None and t >= 1:
                            gate(B, t - 1, 1)
                        if C is not None:
                            readout(C, t, 1, 2)
                        if B is not None and t >= 3:
                            squares(B, t - 3)
                    if B is not None:
                        gate(B, NKC - 1, 0)
                    if A is not None:
                        conv(A, NKC)
                    if B is not None:
                        gate(B, NKC - 1, 1)
                    if C is not None:
                        for q in range(3):
                            out_product(C, NKC - 1, q)
                    if A is not None:
                        conv(A, NKC + 1)
                    if B is not None:
                        squares(B, NKC - 3)
                    if A is not None:
                        conv(A, NKC + 2)
                        conv(A, NKC + 3)
                    if B is not None:
                        squares(B, NKC - 2)
                    if A is not None:
                        conv(A, NKC + 4)
                    if B is not None:
                        squares(B, NKC - 1)
                    if A is not None:
                        conv(A, NKC + 5)
                        conv(A, NKC + 6)

                pe.wait_ge(s["w_in"], 16 * N_EARLY)
                round_of(0, None, None)
                round_of(1, 0, None)
                pe.wait_ge(s["wr_scaled"], KH)
                with pe.Fori(1, G - 1) as g:
                    round_of(g + 1, g, g - 1)
                round_of(None, G - 1, G - 2)
                round_of(None, None, G - 1)

            @block.scalar
            def _(act):
                act.sem_inc(s["th_ready"], TH0)
                act.wait_ge(s["w_in"], 16 * N_EARLY)
                act.activation(par[:, 0, :], par[:, 0, :], ACT.Sigmoid).then_inc(s["par_a"], 1)
                act.activation(par[:, 1, :], par[:, 1, :], ACT.Exp).then_inc(s["par_a"], 1)
                act.activation(hp[:, 3:4], hp[:, 2:3], ACT.Abs).then_inc(s["tw_a"], 1)
                act.wait_ge(s["tw_a"], 1)
                act.activation(hp[:, 4:5], hp[:, 3:4], ACT.Exp, scale=-1.0).then_inc(s["tw_a"], 1)
                act.wait_ge(s["tw_a"], 2)
                act.activation(hp[:, 5:6], hp[:, 4:5], ACT.Ln, bias=1.0).then_inc(s["par_a"], 1)
                act.wait_ge(s["tw_ready"], 1)
                act.activation(tw[:, :], tw[:, :], ACT.Exp, scale=hp[:, 7:8]).then_inc(s["tw_a"], 1)
                act.wait_ge(s["par_ready"], 1)
                act.wait_ge(s["set"], 1)

                def tap(g, m):
                    n = KH if m == 0 else 128
                    act.wait_ge(s["z_mm"], g * NZ + m + 1)
                    if 1 <= m <= NKC:
                        after(act, "phi_ready", (g - 1) * NKC + m)
                    elif m > NKC:
                        after(act, "prod_ready", (g - 1) * NKC + (2 * ((m - 1 - NKC) // 2) + 2))
                    act.activation(z[0:n, m, :], k.PS[0:n, m % 2, 0:GT], ACT.Copy, scale=cwt[0:n, m, KS - 1:KS]).then_inc(s["tap_a"], 1)

                def silu(g, m):
                    n = KH if m == 0 else 128
                    act.wait_ge(s["z_taken"], g * NZ + m + 1)
                    act.activation(z[0:n, m, :], z[0:n, m, :], ACT.Silu).then_inc(s["z_ready" if m <= NKC else "q_ready"], 1)

                def phase_abs(g, c):
                    i = g * NKC + c
                    after(act, "phi_ready", i)
                    act.activation(ab[:, :], z[:, 1 + c, :], ACT.Abs, scale=par[:, 2, c:c + 1]).then_inc(s["abs_ready"], 1)

                def trig(g, c):
                    p = c % 2
                    i = g * NKC + c
                    act.wait_ge(s["phi_ready"], i + 1)
                    act.activation(cs[:, p, 0, :], cs[:, p, 1, :], ACT.Abs).then_inc(s["trig_a"], 1)
                    act.wait_ge(s["trig_a"], i + 1)
                    act.activation(cs[:, p, 1, :], cs[:, p, 1, :], ACT.Sin)
                    act.activation(cs[:, p, 0, :], cs[:, p, 0, :], ACT.Sin, scale=-1.0, bias=halfpi[:, :]).then_inc(s["trig_ready"], 1)

                def norm_scale(g, c):
                    i = g * NKC + c
                    after(act, "run_ready", i - 1)
                    act.wait_ge(s["bc_mm"], g * (2 * NKC) + 2 * c + 2)
                    act.activation(cc[:, c % 2, :], k.PS[:, BC, 0:GT], ACT.Copy, scale=par[:, 1, c:c + 1]).then_inc(s["cc_ready"], 1)

                def gate(g, c, i):
                    after(act, "h_ready", g * NKC + (c - 1))
                    act.wait_ge(s["g_mm"], g * KH + 2 * c + i + 1)
                    act.activation(sg[:, c % 2, i, :], k.PS[:, BC, 0:GT], ACT.Silu).then_inc(s["g_ready"], 1)

                def square(g, c):
                    act.wait_ge(s["h_ready"], g * NKC + c + 1)
                    for i, hd in enumerate(heads_of(c)):
                        n = 2 * c + i
                        after(act, "ssq_mm", g * KH + (n - 1))
                        act.activation(sq[:, n % 2, :], f[:, hd, :], ACT.Square).then_inc(s["sq_ready"], 1)

                def gates_tanh(g, c, i):
                    ro = g * (3 * KH) + 6 * c + 3 * i
                    act.wait_ge(s["y_ready"], g * (2 * KH) + (4 * (c - 1) + 2 * i + 2 + Y0))
                    act.wait_ge(s["ro_mm"], ro + 2)
                    act.activation(t0[:, i, :], k.PS[:, RO + (3 * i + 1) % 2, 0:GT], ACT.Tanh, scale=0.5).then_inc(s["th_ready"], 1)

                def rest_tanh(g, c, i):
                    ro = g * (3 * KH) + 6 * c + 3 * i
                    act.wait_ge(s["ro_mm"], ro + 3)
                    gr, vr = (slice(64, 128), slice(0, 64)) if i == 0 else (slice(0, 64), slice(64, 128))
                    act.activation(t1[vr, :], k.PS[gr, RO + (3 * i + 2) % 2, 0:GT], ACT.Tanh, scale=0.5).then_inc(s["th_ready"], 1)

                def softplus_start(g):
                    act.wait_ge(s["z_ready"], g * (1 + NKC) + 1)
                    after(act, "bc_mm", g * (2 * NKC))
                    act.activation(st[:, :], z[0:KH, 0, :], ACT.Identity, scale=hp[:, 0:1], bias=hp[:, 1:2]).then_inc(s["sp_a"], 1)
                    act.wait_ge(s["sp_a"], g * 3 + 1)
                    act.activation(sa[:, :], st[:, :], ACT.Abs).then_inc(s["sp_a"], 1)

                def divisor_abs(g, c):
                    act.wait_ge(s["z_ready"], g * (1 + NKC) + 2 + c)
                    act.activation(r[:, c, :], z[:, 1 + c, :], ACT.Abs, scale=par[:, 2, c:c + 1]).then_inc(s["r_a"], 1)

                def softplus_end(g):
                    act.wait_ge(s["sp_a"], g * 3 + 2)
                    act.activation(sa[:, :], sa[:, :], ACT.Exp, scale=-1.0).then_inc(s["sp_a"], 1)
                    act.wait_ge(s["sp_a"], g * 3 + 3)
                    act.activation(sa[:, :], sa[:, :], ACT.Ln, bias=1.0).then_inc(s["sp_ready"], 1)

                def logarithms(g):
                    for c in range(NKC):
                        act.wait_ge(s["r_a"], g * (2 * NKC) + c + 1)
                        act.activation(r[:, c, :], r[:, c, :], ACT.Ln, bias=1.0).then_inc(s["r_a"], 1)

                def exponentials(g):
                    for c in range(NKC):
                        act.wait_ge(s["r_a"], g * (2 * NKC) + NKC + c + 1)
                        act.activation(r[:, c, :], r[:, c, :], ACT.Exp, scale=-1.0).then_inc(s["r_ready"], 1)

                def norm(g):
                    after(act, "rs_ready", g)
                    act.wait_ge(s["ssq_mm"], g * KH + KH)
                    act.activation(rq[:, :], k.PS[:, SS, 0:GT], ACT.Ln, bias=k.eps6[:, :]).then_inc(s["rs_a"], 1)
                    act.wait_ge(s["rs_a"], g * 2 + 1)
                    act.activation(rq[:, :], rq[:, :], ACT.Exp, scale=-0.5).then_inc(s["rs_a"], 1)

                def round_of(A, B, C):
                    for t in range(NKC):
                        if B is not None:
                            phase_abs(B, t)
                        if C is not None:
                            gates_tanh(C, t, 0)
                        if B is not None:
                            norm_scale(B, t)
                            trig(B, t)
                        if C is not None:
                            rest_tanh(C, t, 0)
                        if A is not None:
                            tap(A, t)
                        if B is not None and t >= 1:
                            gate(B, t - 1, 0)
                        if C is not None:
                            gates_tanh(C, t, 1)
                        if B is not None and t >= 1:
                            gate(B, t - 1, 1)
                        if C is not None:
                            rest_tanh(C, t, 1)
                        if B is not None and t >= 3:
                            square(B, t - 3)
                        if A is not None and t >= 1:
                            silu(A, t - 1)
                            if t >= 2:
                                divisor_abs(A, t - 2)
                        if B is not None and t < NQC:
                            silu(B, 1 + NKC + 2 * t)
                            silu(B, 2 + NKC + 2 * t)
                    if B is not None:
                        gate(B, NKC - 1, 0)
                    if A is not None:
                        tap(A, NKC)
                    if B is not None:
                        gate(B, NKC - 1, 1)
                    if A is not None:
                        silu(A, NKC - 1)
                        softplus_start(A)
                        tap(A, NKC + 1)
                        divisor_abs(A, NKC - 2)
                    if B is not None:
                        square(B, NKC - 3)
                    if A is not None:
                        silu(A, NKC)
                        tap(A, NKC + 2)
                        divisor_abs(A, NKC - 1)
                        softplus_end(A)
                        tap(A, NKC + 3)
                    if B is not None:
                        square(B, NKC - 2)
                    if A is not None:
                        tap(A, NKC + 4)
                        logarithms(A)
                    if B is not None:
                        square(B, NKC - 1)
                    if A is not None:
                        tap(A, NKC + 5)
                    if B is not None:
                        norm(B)
                    if A is not None:
                        tap(A, NKC + 6)
                        exponentials(A)

                round_of(0, None, None)
                round_of(1, 0, None)
                with act.Fori(1, G - 1) as g:
                    round_of(g + 1, g, g - 1)
                round_of(None, G - 1, G - 2)
                round_of(None, None, G - 1)

            @block.vector
            def _(v):
                v.sem_inc(s["y_ready"], Y0)
                v.sem_inc(s["o_added"], ADD0)
                v.memset(halfpi[:, :], float(np.pi / 2)).then_inc(s["set"], 1)
                v.wait_ge(s["par_a"], 3)
                v.tensor_scalar(par[:, 0, :], par[:, 0, :], -2.999, -0.001, ALU.mult, ALU.add).then_inc(s["par_v"], 1)
                v.tensor_scalar(par[:, 3, :], par[:, 1, :], 1e-6, None, ALU.add).then_inc(s["par_v"], 1)
                v.scalar_tensor_tensor(hp[:, 6:7], hp[:, 2:3], 0.0, hp[:, 5:6], ALU.max, ALU.add).then_inc(s["par_v"], 1)
                v.wait_ge(s["par_v"], 3)
                v.reciprocal(par[:, 3, :], par[:, 3, :]).then_inc(s["par_v"], 1)
                v.tensor_scalar(hp[:, 7:8], hp[:, 6:7], -1.0, None, ALU.mult).then_inc(s["tw_ready"], 1)
                v.wait_ge(s["par_v"], 4)
                v.scalar_tensor_tensor(par[:, 1, :], par[:, 1, :], float(HH) ** -0.5, par[:, 3, :], ALU.mult, ALU.mult).then_inc(s["par_v"], 1)
                v.wait_ge(s["par_v"], 5)
                v.tensor_tensor(par[:, 3, :], par[:, 0, :], par[:, 2, :], ALU.mult).then_inc(s["par_ready"], 1)
                v.wait_ge(s["par_ready"], 1)
                v.wait_ge(s["w_in"], 16 * N_EARLY)
                v.wait_ge(s["tw_a"], 3)

                def taps(g, m):
                    n = KH if m == 0 else 128
                    v.wait_ge(s["tap_a"], g * NZ + m + 1)
                    zs = z[0:n, m, :].rearrange("p (s l) -> p s l", s=SPG)
                    ps = k.PS[0:n, m % 2, 0:GT].rearrange("p (s l) -> p s l", s=SPG)
                    for q in range(1, KS):
                        ins = v.scalar_tensor_tensor(zs[:, :, q:L], ps[:, :, 0:L - q], cwt[0:n, m, KS - 1 - q:KS - q], zs[:, :, q:L],
                                                     ALU.mult, ALU.add)
                        if q < KS - 1:
                            ins.then_inc(s["tap_v"], 1)
                            v.wait_ge(s["tap_v"], g * (2 * NZ) + 2 * m + q)
                    ins.then_inc(s["z_taken"], 1)

                def weights(g):
                    v.wait_ge(s["sp_ready"], g + 1)
                    v.scalar_tensor_tensor(st[:, :], st[:, :], 0.0, sa[:, :], ALU.max, ALU.add).then_inc(s["sp_v"], 1)
                    v.wait_ge(s["sp_v"], g * 2 + 1)
                    v.tensor_tensor(st[:, :], st[:, :], tw[:, :], ALU.mult).then_inc(s["sp_v"], 1)
                    v.wait_ge(s["sp_v"], g * 2 + 2)
                    v.tensor_scalar(pw[:, :], st[:, :], 1e-4, 5000.0, ALU.max, ALU.min).then_inc(s["pw_ready"], 1)
                    v.wait_ge(s["pw_ready"], g + 1)
                    v.tensor_tensor_scan(pd[:, :], mask[0:KH, :], pw[:, :], 0.0, ALU.mult, ALU.add).then_inc(s["id_v"], 1)
                    v.wait_ge(s["id_v"], g * 2 + 1)
                    v.tensor_scalar(pd[:, :], pd[:, :], 1e-4, None, ALU.max).then_inc(s["id_v"], 1)
                    v.wait_ge(s["id_v"], g * 2 + 2)
                    v.reciprocal(pd[:, :], pd[:, :]).then_inc(s["id_ready"], 1)

                def weighted(g, c):
                    i = g * NKC + c
                    after(v, "rot_ready", i - 1)
                    v.wait_ge(s["bc_mm"], g * (2 * NKC) + 2 * c + 1)
                    v.tensor_tensor(kvw[:, c % 2, :], z[:, 1 + c, :], k.PS[:, BC, 0:GT], ALU.mult).then_inc(s["kvw_ready"], 1)

                def phase(g, c):
                    i = g * NKC + c
                    v.wait_ge(s["abs_ready"], i + 1)
                    v.wait_ge(s["r_ready"], i + 1)
                    v.scalar_tensor_tensor(ab[:, :], ab[:, :], 1.0, r[:, c, :], ALU.add, ALU.mult).then_inc(s["newton"], 1)
                    v.wait_ge(s["newton"], i * 2 + 1)
                    v.scalar_tensor_tensor(ab[:, :], ab[:, :], 2.0, r[:, c, :], ALU.subtract, ALU.mult).then_inc(s["newton"], 1)
                    v.wait_ge(s["newton"], i * 2 + 2)
                    v.scalar_tensor_tensor(cs[:, c % 2, 1, :], z[:, 1 + c, :], par[:, 3, c:c + 1], ab[:, :], ALU.mult, ALU.mult).then_inc(s["phi_ready"], 1)

                def running(g, c):
                    p = c % 2
                    i = g * NKC + c
                    v.wait_ge(s["rot_ready"], i + 1)
                    for h in range(2):
                        v.tensor_tensor_scan(ri[:, p, h, :], mask[:, :], ri[:, p, h, :], 0.0, ALU.mult, ALU.add).then_inc(s["run_v"], 1)
                    v.wait_ge(s["cc_ready"], i + 1)
                    v.wait_ge(s["run_v"], i * 2 + 2)
                    v.tensor_tensor(ri[:, p, :, :], ri[:, p, :, :], cc[:, p, :].unsqueeze(1).to_broadcast([128, 2, GT]), ALU.mult).then_inc(s["run_ready"], 1)

                def match(g, c):
                    p = c % 2
                    v.wait_ge(s["prod_ready"], g * NKC + c + 1)
                    after(v, "ro_mm", (g - 1) * (3 * KH) + 6 * c + 6)
                    for i, hd in enumerate(heads_of(c)):
                        w = slice(64 * i, 64 * i + 64)
                        v.tensor_tensor(f[0:64, hd, :], ma[w, p, 0, :], mb[w, p, 1, :], ALU.add)
                        ins = v.tensor_tensor(f[64:128, hd, :], ma[w, p, 1, :], mb[w, p, 0, :], ALU.subtract)
                    ins.then_inc(s["f_ready"], 1)

                def values(g, c, i):
                    n = 2 * c + i
                    v.wait_ge(s["wo_mm"], g * NWO + (3 * (c - 1) + i + 1 + WO0))
                    v.wait_ge(s["th_ready"], g * (2 * KH) + (2 * n + 1 + TH0))
                    v.scalar_tensor_tensor(y0[:, i, :], t0[:, i, :], 1.0, k.PS[:, RO + (3 * i) % 2, 0:GT], ALU.add, ALU.mult).then_inc(s["y_ready"], 1)

                def rest(g, c, i):
                    n = 2 * c + i
                    v.wait_ge(s["wo_mm"], g * NWO + (3 * (c - 1) + WO0))
                    v.wait_ge(s["th_ready"], g * (2 * KH) + (2 * n + 2 + TH0))
                    vr = slice(0, 64) if i == 0 else slice(64, 128)
                    v.scalar_tensor_tensor(y1[vr, c % 2, :], t1[vr, :], 1.0, k.PS[vr, RO + (3 * i + 2) % 2, 0:GT], ALU.add, ALU.mult).then_inc(s["y_ready"], 1)

                def add(g):
                    v.wait_ge(s["wo_mm"], (g + 1) * NWO + WO0)
                    for j in range(TPG):
                        h = k.H[:, ds((g * TPG + j) * D, D)]
                        ins = v.tensor_tensor(h, out_tile(j), h, ALU.add)
                    ins.then_inc(s["o_added"], 1)

                def norm(g):
                    v.wait_ge(s["rs_a"], g * 2 + 2)
                    v.scalar_tensor_tensor(rn[:, :], k.PS[:, SS, 0:GT], 1e-6, rq[:, :], ALU.add, ALU.mult).then_inc(s["rs_v"], 1)
                    v.wait_ge(s["rs_v"], g * 2 + 1)
                    v.tensor_tensor(rn[:, :], rn[:, :], rq[:, :], ALU.mult).then_inc(s["rs_v"], 1)
                    v.wait_ge(s["rs_v"], g * 2 + 2)
                    after(v, "hn_ready", g * KH)
                    v.scalar_tensor_tensor(rs[:, :], rn[:, :], 3.0, rq[:, :], ALU.subtract, ALU.mult).then_inc(s["rs_ready"], 1)

                def round_of(A, B, C):
                    for t in range(NKC):
                        if B is not None:
                            weighted(B, t)
                            phase(B, t)
                        if C is not None:
                            values(C, t, 0)
                        if B is not None and t >= 1:
                            running(B, t - 1)
                        if C is not None:
                            rest(C, t, 0)
                        if A is not None:
                            taps(A, t)
                        if C is not None:
                            values(C, t, 1)
                        if B is not None and t >= 2:
                            match(B, t - 2)
                        if C is not None:
                            rest(C, t, 1)
                    if B is not None:
                        running(B, NKC - 1)
                    if A is not None:
                        taps(A, NKC)
                    if B is not None:
                        match(B, NKC - 2)
                    if A is not None:
                        taps(A, NKC + 1)
                    if B is not None:
                        match(B, NKC - 1)
                    if C is not None:
                        add(C)
                    if A is not None:
                        taps(A, NKC + 2)
                        taps(A, NKC + 3)
                        weights(A)
                        taps(A, NKC + 4)
                    if B is not None and A is None:
                        norm(B)
                    if A is not None:
                        taps(A, NKC + 5)
                        if B is not None:
                            norm(B)
                        taps(A, NKC + 6)

                round_of(0, None, None)
                round_of(1, 0, None)
                with v.Fori(1, G - 1) as g:
                    round_of(g + 1, g, g - 1)
                round_of(None, G - 1, G - 2)
                round_of(None, None, G - 1)

            @block.gpsimd
            def _(po):
                po.wait_ge(s["w_late"], 16 * N_LATE)
                for hd in range(KH):
                    po.tensor_scalar(wr[:, hd, :], wr[:, hd, :], nw[:, hd:hd + 1], -0.5, ALU.mult, ALU.mult).then_inc(s["wr_scaled"], 1)
                po.tensor_scalar(wo[:, :, :], wo[:, :, :], 0.5, None, ALU.mult).then_inc(s["wo_scaled"], 1)

                def rotate(g, c):
                    p = c % 2
                    i = g * NKC + c
                    after(po, "prod_ready", i - 1)
                    po.wait_ge(s["kvw_ready"], i + 1)
                    po.wait_ge(s["trig_ready"], i + 1)
                    po.tensor_tensor(ri[:, p, :, :], cs[:, p, :, :], kvw[:, p, :].unsqueeze(1).to_broadcast([128, 2, GT]), ALU.mult).then_inc(s["rot_ready"], 1)

                def products(g, c):
                    p = c % 2
                    i = g * NKC + c
                    po.wait_ge(s["run_ready"], i + 1)
                    after(po, "f_ready", i - 1)
                    if c % 2 == 0:
                        po.wait_ge(s["q_ready"], g * (2 * NQC) + (c + 2))
                    for m, q in ((ma, 0), (mb, 1)):
                        qq = z[:, 1 + NKC + 2 * (c // 2) + q, :].unsqueeze(1).to_broadcast([128, 2, GT])
                        ins = po.tensor_tensor(m[:, p, :, :], ri[:, p, :, :], qq, ALU.mult)
                    ins.then_inc(s["prod_ready"], 1)

                def gated(g, c):
                    po.wait_ge(s["f_ready"], g * NKC + c + 1)
                    po.wait_ge(s["g_ready"], g * KH + 2 * c + 2)
                    for i, hd in enumerate(heads_of(c)):
                        ins = po.tensor_tensor(f[:, hd, :], f[:, hd, :], sg[:, c % 2, i, :], ALU.mult)
                    ins.then_inc(s["h_ready"], 1)

                def normalise(g, c):
                    po.wait_ge(s["rs_ready"], g + 1)
                    for hd in heads_of(c):
                        po.tensor_tensor(f[:, hd, :], f[:, hd, :], rs[:, :], ALU.mult).then_inc(s["hn_ready"], 1)

                def round_of(B, C):
                    for t in range(NKC + 2):
                        if C is not None and t == 0:
                            normalise(C, 0)
                        if B is not None and t < NKC:
                            rotate(B, t)
                        if C is not None and t + 1 < NKC:
                            normalise(C, t + 1)
                        if B is not None and 1 <= t <= NKC:
                            products(B, t - 1)
                        if B is not None and t >= 2:
                            gated(B, t - 2)

                round_of(0, None)
                with po.Fori(1, G - 1) as g:
                    round_of(g, g - 1)
                round_of(G - 1, G - 2)
                round_of(None, G - 1)




def program(nc, a, out):
    with ExitStack() as ctx:
        k = Core(nc, ctx)
        embed(k, a)
        layernorm(k, "ln1_", k.H)
        attention(k, "at1_", k.H, a["at1_w"], a["at1_proj"], a["at1_proj_b"], a["at1_qk_b"], a["at1_v_b"], smooth=True)
        with ExitStack() as part:
            layernorm(k, "ln2_", k.H)
            cw = k.sb(part, "cw1", [TP, NTILE * (NE + 2)])
            eb = ExpertBuffers(k, part, "ex1_", a["ex1_up"], a["ex1_down"], 2 * HID)
            router(k, "rt1_", cw, a["rt1_gate"], True, eb, n_cols=NE + 2)
            experts(k, "ex1_", cw, NE + 2, eb, True)
        layernorm(k, "ln3_", k.H)
        memory_mixer(k, "mm_", a)
        with ExitStack() as part:
            k.Zr = k.sb(part, "Zr", [TP, NTILE * D])
            layernorm(k, "ln4_", k.H, keep=k.Zr)
            layernorm(k, "ln5_", k.Zr, gain=(a["ln1_g"], a["ln1_b"]))
            attention(k, "at2_", k.Zr, a["at2_w"], a["at2_proj"], a["at2_proj_b"])
            layernorm(k, "ln6_", k.Zr, gain=(a["ln2_g"], a["ln2_b"]))
            add_branch(k)
            cw = k.sb(part, "cw2", [TP, NTILE * NE])
            eb = ExpertBuffers(k, part, "ex2_", a["ex2_up"], a["ex2_down"], HID)
            router(k, "rt2_", cw, a["rt2_gate"], False, eb, gate_b=a["rt2_gate_b"], b2=a["ex2_b2"])
            experts(k, "ex2_", cw, NE, eb, False, b1=a["ex2_b1"])
        store(k, out)


def add_branch(k):
    with k.nc.Block() as block:

        @block.vector
        def _(v):
            v.tensor_tensor(k.H[:, :], k.H[:, :], k.Zr[:, :], ALU.add)


def store(k, out):
    nc = k.nc
    with k.phase() as ctx:
        stored = k.sem(ctx, "stored")
        with nc.Block() as block:

            @block.sync
            def _(sp):
                sp.dma_start(out.rearrange("b l d -> (b l) d").rearrange("(t p) d -> p t d", p=TP),
                             k.H[:, :].rearrange("p (t d) -> p t d", d=D)).then_inc(stored, 16)
                sp.wait_ge(stored, 16)


def layout(x):
    def col(v, n=1):
        return v.reshape(-1, n)

    def heads32(w):
        p = np.zeros((HEADS, 32) + w.shape[1:], w.dtype)
        p[:, 0:HD] = w.reshape((HEADS, HD) + w.shape[1:])
        return p.reshape((HEADS * 32,) + w.shape[1:])

    def qkv(w):
        return np.concatenate([heads32(w[0:D]), heads32(w[D:2 * D]), w[2 * D:3 * D]], axis=0).T

    a = {}
    a["patches"] = x["x"].reshape(B, 3, 4, 16, 4, 16).transpose(3, 5, 1, 0, 2, 4).reshape(KP, B * NP_)
    a["tokWT"] = x["L0_tok_W"].T
    a["tok_b"] = x["L0_tok_b"].reshape(1, D)
    a["txt"] = x["txt"]
    a["c_ident"] = np.eye(128, dtype=np.float32)
    a["at1_w"] = qkv(x["L0_attn_qkv_weight"])
    b = x["L0_attn_qkv_bias"]
    a["at1_qk_b"] = np.concatenate([heads32(b[0:D]), heads32(b[D:2 * D])]).reshape(6, 128).T
    a["at1_v_b"] = b[2 * D:].reshape(1, D)
    a["at1_proj"] = x["L0_attn_proj_weight"].T
    a["at1_proj_b"] = x["L0_attn_proj_bias"].reshape(1, D)
    a["rt1_gate"] = x["L0_ffn_gate_w"].T
    gate = np.concatenate([x["L0_ffn_routed_gate"], x["L0_ffn_shared_gate"]])
    up = np.concatenate([x["L0_ffn_routed_up"], x["L0_ffn_shared_up"]])
    down = np.concatenate([x["L0_ffn_routed_down"], x["L0_ffn_shared_down"]])
    a["ex1_up"] = np.concatenate([gate, up], axis=1).transpose(0, 2, 1)
    a["ex1_down"] = down.transpose(0, 2, 1)
    pair = np.array([[heads_of(c)[i] * HH + f for i in range(2) for f in range(HH)] for c in range(NKC)])
    nk = KH * HH
    qcol = nk + KH + 2 * np.arange(KQ * HH).reshape(NQC, 128)
    def chunks(w):
        sc = np.zeros(w.shape[:-1] + (1, 128), w.dtype)
        sc[..., 0, 0:KH] = w[..., nk:nk + KH]
        q = np.stack([w[..., qcol], w[..., qcol + 1]], axis=-2)
        return np.concatenate([sc, w[..., pair], q.reshape(w.shape[:-1] + (2 * NQC, 128))], axis=-2)
    a["mm_wi"] = chunks(x["L1_attn_W_in"]).reshape(D, NZ * 128)
    a["mm_cw"] = chunks(x["L1_attn_conv_w"]).transpose(2, 1, 0)
    ph = np.repeat(x["L1_attn_phase_scale"], HH)
    a["mm_par"] = np.stack([x["L1_attn_theta_raw"].reshape(-1)[pair], x["L1_attn_w_int_raw"].reshape(-1)[pair],
                            ph[pair]]).transpose(2, 0, 1)
    a["mm_hp"] = np.stack([x["L1_attn_score_scale"], x["L1_attn_score_bias"], x["L1_attn_decay_slopes"]], axis=1)
    a["mm_nw"] = x["L1_attn_gated_norm_weight"].reshape(KH, 128).T
    a["mm_wg"] = x["L1_attn_W_gate"]
    val, gt = np.arange(EX), EX + np.arange(EX)
    even = np.concatenate([val[:128], gt[:128], val[128:], gt[128:]])
    odd = np.concatenate([val[:128], gt[:128], gt[128:], val[128:]])
    order = np.stack([odd if h % 4 >= 2 else even for h in range(KH)])
    a["mm_wr"] = np.take_along_axis(x["L1_attn_W_readout"], order[:, None, :], axis=2).transpose(1, 0, 2)
    w = x["L1_attn_W_out"].reshape(KH, EX, D)
    by_chunk = w[[list(heads_of(c)) for c in range(NKC)]]
    rest = by_chunk[:, :, 128:].reshape(NKC, 1, 128, D)
    a["mm_wo"] = np.concatenate([by_chunk[:, :, :128], rest], axis=1).reshape(3 * NKC, 128, D).transpose(1, 0, 2)
    a["c_sel"] = np.zeros((KH, NKC, 128), np.float32)
    for c in range(NKC):
        for i, h in enumerate(heads_of(c)):
            a["c_sel"][h, c, HH * i:HH * i + HH] = 1
    pos = np.tile(np.arange(L), SPG)
    a["c_dist"] = np.tile((MAXLEN - 1 - pos).astype(np.float32), (KH, 1))
    a["c_mask"] = np.tile((pos > 0).astype(np.float32), (128, 1))
    a["c_mean"] = np.full((128, 128), 1.0 / (KH * 2 * HH), np.float32)
    a["ln1_g"], a["ln1_b"] = col(x["L1_ffn_ln1_g"]), col(x["L1_ffn_ln1_b"])
    a["ln2_g"], a["ln2_b"] = col(x["L1_ffn_ln2_g"]), col(x["L1_ffn_ln2_b"])
    a["at2_w"] = qkv(x["L1_ffn_qkv_w"])
    a["at2_proj"] = x["L1_ffn_proj_w"].T
    a["at2_proj_b"] = x["L1_ffn_proj_b"].reshape(1, D)
    a["rt2_gate"], a["rt2_gate_b"] = x["L1_ffn_gate_w"].T, x["L1_ffn_gate_b"].reshape(1, NE)
    a["ex2_up"] = x["L1_ffn_w1"].transpose(0, 2, 1)
    a["ex2_b1"] = x["L1_ffn_b1"].reshape(NE * IC, 128).T
    a["ex2_down"] = x["L1_ffn_w2"].transpose(0, 2, 1)
    half = NTILE // 2
    a["ex2_b2"] = np.zeros((half, NE, half, D), np.float32)
    for t in range(half):
        a["ex2_b2"][t, :, t] = x["L1_ffn_b2"]
    a["ex2_b2"] = a["ex2_b2"].reshape(half * NE, half, D)
    return {n: np.ascontiguousarray(v) for n, v in a.items()}


def build(nc, arrays):
    a = {n: nc.dram_tensor(n + "_dram", v.shape, F32, kind="ExternalInput").ap() for n, v in arrays.items()}
    a["h0"] = nc.dram_tensor("h0_scratch", (B, L, D), F32).ap()
    out = nc.dram_tensor("out_dram", (B, L, D), F32, kind="ExternalOutput").ap()
    program(nc, a, out)


def kernel(**inputs):
    import concourse.bacc as bacc
    from concourse.bass_utils import run_bass_kernel_spmd

    arrays = layout({n: np.asarray(v) for n, v in inputs.items()})
    nc = bacc.Bacc("TRN2", target_bir_lowering=False, num_devices=1)
    build(nc, arrays)
    r = run_bass_kernel_spmd(nc, [{n + "_dram": v for n, v in arrays.items()}], core_ids=[0])
    return r.results[0]["out_dram"]
```

```python
from contextlib import ExitStack, contextmanager

import numpy as np
import concourse.bass as bass
from concourse import mybir

F32 = mybir.dt.float32
BF16 = mybir.dt.bfloat16
I32 = mybir.dt.int32
ALU = mybir.AluOpType
ACT = mybir.ActivationFunctionType
X = mybir.AxisListType.X
ds = bass.ds

B, NP_, NTXT, D = 32, 16, 77, 192
L = NP_ + NTXT
T = B * L
TP = 124
TPG = 3
SPG = 4
GT = TP * TPG
G = T // GT
NTILE = T // TP
D1 = D - 128
KP = 768
HEADS, HD = 12, 16
HID, NE = 768, 8
IC = HID // 128
assert GT == SPG * L and G * GT == T


class Core:

    def __init__(self, nc, ctx):
        self.nc = nc
        self.cleared = []
        self.H = self.sb(ctx, "H", [TP, NTILE * D])
        self.x0 = self.sb(ctx, "x0", [128, T])
        self.x1 = self.sb(ctx, "x1", [D1, T])
        self.ident = self.sb(ctx, "ident", [128, 128])
        self.ones_row = self.sb(ctx, "ones_row", [1, 128])
        self.eps5 = self.sb(ctx, "eps5", [128, 1])
        self.eps6 = self.sb(ctx, "eps6", [128, 1])
        self.PS = ctx.enter_context(nc.psum_tensor("PS", [128, 8, 512], F32))

    def sb(self, ctx, name, shape, dt=F32):
        return ctx.enter_context(self.nc.sbuf_tensor(name, shape, dt))

    def sem(self, ctx, name):
        self.sems.append(self.nc.alloc_semaphore(name))
        return self.sems[-1]

    @contextmanager
    def phase(self):
        self.sems = []
        with ExitStack() as ctx:
            yield ctx
        for sem in self.sems:
            self.nc.gpsimd.sem_clear(sem)
        self.nc.extend_free_semaphores([sem.num for sem in self.cleared])
        self.cleared = self.sems


def embed(k, a):
    nc = k.nc
    KC = KP // 128
    NPT = B * NP_ // 128
    with k.phase() as ctx:
        xp = k.sb(ctx, "xp", [128, KC, B * NP_])
        wp = k.sb(ctx, "wp", [128, KC, D])
        bp = k.sb(ctx, "bp", [1, D])
        eo = k.sb(ctx, "eo", [128, NPT, D])
        loaded = k.sem(ctx, "em_loaded")
        consts = k.sem(ctx, "em_consts")
        mm = k.sem(ctx, "em_mm")
        ev = k.sem(ctx, "em_ev")
        joined = k.sem(ctx, "em_joined")
        h_in = k.sem(ctx, "em_h_in")
        with nc.Block() as block:

            @block.sync
            def _(sp):
                sp.dma_start(xp[:, :, :], a["patches"].rearrange("(c p) n -> p c n", p=128)).then_inc(loaded, 16)
                sp.dma_start(wp[:, :, :], a["tokWT"].rearrange("(c p) n -> p c n", p=128)).then_inc(loaded, 16)
                sp.dma_start(bp[:, :], a["tok_b"]).then_inc(loaded, 16)
                sp.dma_start(k.ident[:, :], a["c_ident"]).then_inc(loaded, 16)
                sp.dma_start(a["h0"][:, NP_:L, :], a["txt"]).then_inc(joined, 16)
                for m in range(NPT):
                    sp.wait_ge(ev, m + 1)
                    sp.dma_start(a["h0"][8 * m:8 * m + 8, 0:NP_, :], eo[:, m, :]).then_inc(joined, 16)
                sp.wait_ge(joined, 16 * (NPT + 1))
                sp.dma_start(k.H[:, :].rearrange("p (t d) -> p t d", d=D),
                             a["h0"].rearrange("b l d -> (b l) d").rearrange("(t p) d -> p t d", p=TP)).then_inc(h_in, 16)
                sp.wait_ge(h_in, 16)

            @block.vector
            def _(v):
                v.memset(k.ones_row[:, :], 1.0).then_inc(consts, 1)
                v.memset(k.eps5[:, :], 1e-5).then_inc(consts, 1)
                v.memset(k.eps6[:, :], 1e-6).then_inc(consts, 1)

            @block.tensor
            def _(pe):
                pe.wait_ge(loaded, 64)
                pe.wait_ge(consts, 3)
                for m in range(NPT):
                    for c in range(KC):
                        pe.matmul(k.PS[:, m, 0:D], xp[:, c, m * 128:(m + 1) * 128], wp[:, c, :],
                                  start=(c == 0), stop=False)
                    pe.matmul(k.PS[:, m, 0:D], k.ones_row[:, :], bp[:, :], start=False, stop=True).then_inc(mm, 1)

            @block.scalar
            def _(act):
                for m in range(NPT):
                    act.wait_ge(mm, m + 1)
                    act.activation(eo[:, m, :], k.PS[:, m, 0:D], ACT.Copy).then_inc(ev, 1)


def layernorm(k, tag, src, keep=None, gain=None, loads=(), add=None):
    nc = k.nc
    with k.phase() as ctx:
        st = k.sb(ctx, tag + "st", [TP, NTILE * 6])
        mv = k.sb(ctx, tag + "mv", [TP, NTILE * 2])
        sd = k.sb(ctx, tag + "sd", [TP, NTILE])
        rs = k.sb(ctx, tag + "rs", [TP, NTILE])
        xt = k.sb(ctx, tag + "xt", [TP, 2, TPG * D])
        gb = k.sb(ctx, tag + "gb", [128, 4])
        stats = k.sem(ctx, tag + "stats")
        aggr = k.sem(ctx, tag + "aggr")
        sd_ready = k.sem(ctx, tag + "sd_ready")
        rs_ready = k.sem(ctx, tag + "rs_ready")
        xt_ready = k.sem(ctx, tag + "xt_ready")
        turned = k.sem(ctx, tag + "turned")
        ps_free = k.sem(ctx, tag + "ps_free")
        gb_in = k.sem(ctx, tag + "gb_in")
        loaded = k.sem(ctx, tag + "loaded")
        with nc.Block() as block:
            @block.sync
            def _(sp):
                if gain:
                    for n, ap in enumerate(gain):
                        sp.dma_start(gb[0:128, n:n + 1], ap[0:128, :]).then_inc(gb_in, 16)
                        sp.dma_start(gb[0:D1, n + 2:n + 3], ap[128:D, :]).then_inc(gb_in, 16)
                for dst, ap in loads:
                    sp.dma_start(dst, ap).then_inc(loaded, 16)
                if loads:
                    sp.wait_ge(loaded, 16 * len(loads))

            if add:
                @block.gpsimd
                def _(po):
                    po.tensor_tensor(add[0][:, :], add[0][:, :], add[1][:, :], ALU.add)

            @block.vector
            def _(v):
                for t in range(NTILE):
                    v.bn_stats(st[:, t * 6:(t + 1) * 6], src[:, t * D:(t + 1) * D]).then_inc(stats, 1)
                v.wait_ge(stats, NTILE)
                for t in range(NTILE):
                    v.bn_aggr(mv[:, t * 2:t * 2 + 2], st[:, t * 6:t * 6 + 6]).then_inc(aggr, 1)
                v.wait_ge(sd_ready, 1)
                v.reciprocal(rs[:, :], sd[:, :]).then_inc(rs_ready, 1)
                v.wait_ge(rs_ready, 1)
                if keep is not None:
                    for t in range(NTILE):
                        v.tensor_scalar(keep[:, t * D:(t + 1) * D], src[:, t * D:(t + 1) * D], mv[:, t * 2:t * 2 + 1],
                                        rs[:, t:t + 1], ALU.subtract, ALU.mult)
                    return
                with v.Fori(0, G // 2) as i:
                    for half in range(2):
                        v.wait_ge(turned, i * 2 + half + 1)
                        for j in range(TPG):
                            t = (i * 2 + half) * TPG + j
                            ins = v.tensor_scalar(xt[:, half, j * D:(j + 1) * D], src[:, ds(t * D, D)],
                                                  mv[:, ds(t * 2, 1)], rs[:, ds(t, 1)], ALU.subtract, ALU.mult)
                        ins.then_inc(xt_ready, 1)

            @block.tensor
            def _(pe):
                if keep is not None:
                    return
                pe.sem_inc(turned, 2)
                with pe.Fori(0, G // 2) as i:
                    for half in range(2):
                        pe.wait_ge(xt_ready, i * 2 + half + 1)
                        pe.wait_ge(ps_free, i * 2 + half + 1)
                        for j in range(TPG):
                            pe.transpose(k.PS[:, 2 * half, j * TP:(j + 1) * TP], xt[:, half, j * D:j * D + 128],
                                         k.ident[0:TP, 0:TP])
                            ins = pe.transpose(k.PS[0:D1, 2 * half + 1, j * TP:(j + 1) * TP],
                                               xt[:, half, j * D + 128:(j + 1) * D], k.ident[0:TP, 0:TP])
                        ins.then_inc(turned, 1)

            @block.scalar
            def _(act):
                act.wait_ge(aggr, NTILE)
                act.activation(sd[:, :], mv[:, :].rearrange("p (t s) -> p t s", s=2)[:, :, 1], ACT.Sqrt,
                               bias=k.eps5[0:TP, :]).then_inc(sd_ready, 1)
                if keep is not None:
                    return
                act.sem_inc(ps_free, 2)
                if gain:
                    act.wait_ge(gb_in, 64)
                with act.Fori(0, G // 2) as i:
                    for half in range(2):
                        g = i * 2 + half
                        act.wait_ge(turned, g + 3)
                        for c, (dst, n) in enumerate(((k.x0, 128), (k.x1, D1))):
                            if gain:
                                ins = act.activation(dst[:, ds(g * GT, GT)], k.PS[0:n, 2 * half + c, 0:GT], ACT.Identity,
                                                     scale=gb[0:n, 2 * c:2 * c + 1], bias=gb[0:n, 2 * c + 1:2 * c + 2])
                            else:
                                ins = act.activation(dst[:, ds(g * GT, GT)], k.PS[0:n, 2 * half + c, 0:GT], ACT.Copy)
                        ins.then_inc(ps_free, 1)


class AttentionWeights:

    def __init__(self, k, ctx, tag, w, proj, proj_b, qk_b=None, v_b=None):
        cols = w.shape[1]
        self.w0 = k.sb(ctx, tag + "w0", [128, cols])
        self.w1 = k.sb(ctx, tag + "w1", [D1, cols])
        self.p0 = k.sb(ctx, tag + "p0", [128, D])
        self.p1 = k.sb(ctx, tag + "p1", [D1, D])
        self.pb = k.sb(ctx, tag + "pb", [1, D])
        self.loads = [(self.w0[:, :], w[0:128, :]), (self.w1[:, :], w[128:D, :]), (self.p0[:, :], proj[0:128, :]),
                      (self.p1[:, :], proj[128:D, :]), (self.pb[:, :], proj_b)]
        self.qkb = self.vb = None
        if qk_b is not None:
            self.qkb = k.sb(ctx, tag + "qkb", [128, qk_b.shape[1]])
            self.vb = k.sb(ctx, tag + "vb", [1, D])
            self.loads += [(self.qkb[:, :], qk_b), (self.vb[:, :], v_b)]


def attention(k, tag, resid, aw, smooth=False):
    nc = k.nc
    NC = HEADS // 4
    WQK = 2 * NC * 128
    WC = WQK + D
    VA = HD + 1
    with k.phase() as ctx:
        w0, w1, p0, p1, pb, qkb, vb = aw.w0, aw.w1, aw.p0, aw.p1, aw.pb, aw.qkb, aw.vb
        xg0 = k.sb(ctx, tag + "xg0", [128, GT])
        xg1 = k.sb(ctx, tag + "xg1", [D1, GT])
        qT = k.sb(ctx, tag + "qT", [128, NC, GT])
        kbd = k.sb(ctx, tag + "kbd", [128, NC, SPG, 4, L])
        vo = k.sb(ctx, tag + "vo", [L, 2, HEADS, VA])
        P = k.sb(ctx, tag + "P", [L, 2, NC, 4, L])
        PT = k.sb(ctx, tag + "PT", [L, 2, NC, 4, L])
        mx = k.sb(ctx, tag + "mx", [L, 2, NC, 4])
        rz = k.sb(ctx, tag + "rz", [L, 2, HEADS])
        o = k.sb(ctx, tag + "o", [L, 2, HEADS, HD])
        oT0 = k.sb(ctx, tag + "oT0", [128, GT])
        oT1 = k.sb(ctx, tag + "oT1", [D1, GT])
        sm = k.sb(ctx, tag + "sm", [128, 16])
        names = ("smooth_max", "smooth_ln", "smooth_sum", "smooth_exp", "smooth_cs", "smooth_inv", "smoothed",
                 "prep", "xg_begun", "xg_ready", "qk_mm", "q_ev", "k_ev_a", "k_ev_v", "v_mm", "v_ev", "s_mm", "mx_ready",
                 "s_free", "p_ready", "p_turned", "pt_ready", "o_mm", "rz_ready", "o_ready", "o_turned", "ot_ready",
                 "y_mm", "y_added")
        s = {n: k.sem(ctx, tag + n) for n in names}
        with nc.Block() as block:
            SB, TB, VB, OB = 0, NC, 2 * NC, 2 * NC + 1
            OT = 4 * L

            def after(e, sem, value):
                if not isinstance(value, int) or value > 0:
                    e.wait_ge(s[sem], value)

            def all_groups(e, group):
                group(0, True, False)
                with e.Fori(1, G - 1) as g:
                    group(g, False, False)
                group(G - 1, False, True)

            def ready(e):
                e.wait_ge(s["prep"], 3)
                if smooth:
                    e.wait_ge(s["smoothed"], 4)

            @block.gpsimd
            def _(po):
                po.memset(kbd[:, :, :, :, :], 0.0).then_inc(s["prep"], 1)
                for half in range(2):
                    po.memset(vo[:, half, :, HD:VA], 1.0).then_inc(s["prep"], 1)
                if smooth:
                    po.wait_ge(s["smoothed"], 4)

                def group(g, first, last):
                    if not first:
                        po.wait_ge(s["v_mm"], g * SPG)
                        po.sem_inc(s["xg_begun"], 1)
                    po.tensor_copy(xg0[:, :], k.x0[:, ds(g * GT, GT)]).then_inc(s["xg_ready"], 1)
                    po.tensor_copy(xg1[:, :], k.x1[:, ds(g * GT, GT)]).then_inc(s["xg_ready"], 1)

                all_groups(po, group)

            @block.vector
            def _(v):
                if smooth:
                    for c, (xx, ww, n) in enumerate(((k.x0, w0, 128), (k.x1, w1, D1))):
                        v.tensor_reduce(sm[0:n, c:c + 1], xx[:, :], X, ALU.max, apply_absolute_value=True).then_inc(s["smooth_max"], 1)
                        v.tensor_reduce(sm[0:n, 2 + c:3 + c], ww[:, :], X, ALU.max, apply_absolute_value=True).then_inc(s["smooth_max"], 1)
                    v.wait_ge(s["smooth_ln"], 4)
                    for c, n in enumerate((128, D1)):
                        v.tensor_scalar(sm[0:n, 6 + c:7 + c], sm[0:n, 6 + c:7 + c], -0.65, None, ALU.mult).then_inc(s["smooth_sum"], 1)
                    v.wait_ge(s["smooth_sum"], 2)
                    for c, n in enumerate((128, D1)):
                        v.scalar_tensor_tensor(sm[0:n, 8 + c:9 + c], sm[0:n, 4 + c:5 + c], 0.35, sm[0:n, 6 + c:7 + c],
                                               ALU.mult, ALU.add).then_inc(s["smooth_sum"], 1)
                    v.wait_ge(s["smooth_exp"], 2)
                    for c, n in enumerate((128, D1)):
                        v.tensor_scalar(sm[0:n, 10 + c:11 + c], sm[0:n, 10 + c:11 + c], 4.0 / 3.0, None, ALU.mult).then_inc(s["smooth_cs"], 1)
                    v.wait_ge(s["smooth_cs"], 2)
                    for c, n in enumerate((128, D1)):
                        v.tensor_scalar(sm[0:n, 12 + c:13 + c].bitcast(I32), sm[0:n, 10 + c:11 + c].bitcast(I32),
                                        -8388608, None, ALU.bitwise_and).then_inc(s["smooth_cs"], 1)
                    v.wait_ge(s["smooth_cs"], 4)
                    for c, n in enumerate((128, D1)):
                        v.reciprocal(sm[0:n, 14 + c:15 + c], sm[0:n, 12 + c:13 + c]).then_inc(s["smooth_inv"], 1)
                    v.wait_ge(s["smooth_inv"], 2)
                    for c, (xx, ww, n) in enumerate(((k.x0, w0, 128), (k.x1, w1, D1))):
                        v.tensor_scalar(ww[:, :], ww[:, :], sm[0:n, 12 + c:13 + c], None, ALU.mult).then_inc(s["smoothed"], 1)
                        v.tensor_scalar(xx[:, :], xx[:, :], sm[0:n, 14 + c:15 + c], None, ALU.mult).then_inc(s["smoothed"], 1)
                ready(v)

                def k_blocks(g):
                    for c in range(NC):
                        v.wait_ge(s["qk_mm"], g * 2 * NC + NC + c + 1)
                        for j in (2, 3):
                            r = slice(32 * j, 32 * j + 32)
                            dst = kbd[r, c, :, j, :]
                            src = k.PS[r, TB + c, 0:GT].rearrange("p (s l) -> p s l", s=SPG)
                            if qkb is not None:
                                ins = v.tensor_scalar(dst, src, qkb[r, NC + c:NC + c + 1], None, ALU.add)
                            else:
                                ins = v.tensor_copy(dst, src)
                        ins.then_inc(s["k_ev_v"], 1)

                def softmax_shift(u, h):
                    v.wait_ge(s["s_mm"], u + 1)
                    sc = k.PS[0:L, SB:SB + NC, 0:4 * L].rearrange("p c (j l) -> p c j l", j=4)
                    v.tensor_reduce(mx[:, h, :, :], sc, X, ALU.max).then_inc(s["mx_ready"], 1)
                    v.wait_ge(s["mx_ready"], u + 1)
                    after(v, "p_turned", u - 1)
                    for c in range(NC):
                        ins = v.tensor_tensor(P[:, h, c, :, :], sc[:, c, :, :],
                                              mx[:, h, c, :].unsqueeze(2).to_broadcast([L, 4, L]), ALU.subtract)
                    ins.then_inc(s["s_free"], 1)

                def keep_v(u, h):
                    v.wait_ge(s["v_mm"], u + 1)
                    after(v, "o_mm", u - 1)
                    v.tensor_copy(vo[:, h, :, 0:HD], k.PS[0:L, VB, 0:D].rearrange("p (h d) -> p h d", d=HD)).then_inc(s["v_ev"], 1)

                def normalise(u, h):
                    v.wait_ge(s["o_mm"], u + 1)
                    oo = k.PS[0:L, OB, 0:HEADS * VA].rearrange("p (h d) -> p h d", d=VA)
                    v.reciprocal(rz[:, h, :], oo[:, :, HD]).then_inc(s["rz_ready"], 1)
                    v.wait_ge(s["rz_ready"], u + 1)
                    after(v, "o_turned", u - 1)
                    v.tensor_tensor(o[:, h, :, :], oo[:, :, 0:HD], rz[:, h, :].unsqueeze(2).to_broadcast([L, HEADS, HD]),
                                    ALU.mult).then_inc(s["o_ready"], 1)

                def add(g):
                    v.wait_ge(s["y_mm"], g + 1)
                    for j in range(TPG):
                        r = resid[:, ds((g * TPG + j) * D, D)]
                        ins = v.tensor_tensor(r, k.PS[0:TP, TB + j, 0:D], r, ALU.add)
                    ins.then_inc(s["y_added"], 1)

                def group(g, first, last):
                    u = g * SPG
                    if first:
                        k_blocks(0)
                        softmax_shift(0, 0)
                        keep_v(0, 0)
                    softmax_shift(u + 1, 1)
                    keep_v(u + 1, 1)
                    if not first:
                        normalise(u - 1, 1)
                    softmax_shift(u + 2, 0)
                    keep_v(u + 2, 0)
                    normalise(u, 0)
                    softmax_shift(u + 3, 1)
                    if not first:
                        add(g - 1)
                    keep_v(u + 3, 1)
                    normalise(u + 1, 1)
                    if not last:
                        k_blocks(g + 1)
                    normalise(u + 2, 0)
                    if not last:
                        softmax_shift(u + 4, 0)
                        keep_v(u + 4, 0)

                all_groups(v, group)
                normalise(G * SPG - 1, 1)
                add(G - 1)

            @block.scalar
            def _(act):
                if smooth:
                    act.wait_ge(s["smooth_max"], 4)
                    for c, n in enumerate((128, D1)):
                        for q in (0, 2):
                            act.activation(sm[0:n, 4 + q + c:5 + q + c], sm[0:n, q + c:q + c + 1], ACT.Ln).then_inc(s["smooth_ln"], 1)
                    act.wait_ge(s["smooth_sum"], 4)
                    for c, n in enumerate((128, D1)):
                        act.activation(sm[0:n, 10 + c:11 + c], sm[0:n, 8 + c:9 + c], ACT.Exp).then_inc(s["smooth_exp"], 1)
                ready(act)
                act.preload_act_table(ACT.Exp)

                def q_and_k(g):
                    for c in range(NC):
                        act.wait_ge(s["qk_mm"], g * 2 * NC + c + 1)
                        if qkb is not None:
                            ins = act.activation(qT[:, c, :], k.PS[:, SB + c, 0:GT], ACT.Identity, bias=qkb[:, c:c + 1])
                        else:
                            ins = act.activation(qT[:, c, :], k.PS[:, SB + c, 0:GT], ACT.Copy)
                        ins.then_inc(s["q_ev"], 1)
                    for c in range(NC):
                        act.wait_ge(s["qk_mm"], g * 2 * NC + NC + c + 1)
                        for j in (0, 1):
                            r = slice(32 * j, 32 * j + 32)
                            dst = kbd[r, c, :, j, :]
                            src = k.PS[r, TB + c, 0:GT].rearrange("p (s l) -> p s l", s=SPG)
                            if qkb is not None:
                                ins = act.activation(dst, src, ACT.Identity, bias=qkb[r, NC + c:NC + c + 1])
                            else:
                                ins = act.activation(dst, src, ACT.Copy)
                        ins.then_inc(s["k_ev_a"], 1)

                def exps(u, h):
                    act.wait_ge(s["s_free"], u + 1)
                    act.activation(P[:, h, :, :, :], P[:, h, :, :, :], ACT.Exp, scale=float(HD) ** -0.5).then_inc(s["p_ready"], 1)

                def turned_p(u, h):
                    act.wait_ge(s["p_turned"], u + 1)
                    after(act, "o_mm", u - 1)
                    for c in range(NC):
                        ins = act.activation(PT[:, h, c, :, :], k.PS[0:L, TB + c, 0:4 * L].rearrange("p (j l) -> p j l", j=4), ACT.Copy)
                    ins.then_inc(s["pt_ready"], 1)

                def turned_out(u, n):
                    act.wait_ge(s["o_turned"], u + 1)
                    act.activation(oT0[:, n * L:(n + 1) * L], k.PS[:, TB, OT:OT + L], ACT.Copy).then_inc(s["ot_ready"], 1)
                    act.activation(oT1[:, n * L:(n + 1) * L], k.PS[0:D1, TB + 1, OT:OT + L], ACT.Copy).then_inc(s["ot_ready"], 1)

                def group(g, first, last):
                    u = g * SPG
                    if first:
                        q_and_k(0)
                        exps(0, 0)
                    for n in range(SPG):
                        if n + 1 == SPG and not last:
                            q_and_k(g + 1)
                        if n + 1 < SPG or not last:
                            exps(u + n + 1, (n + 1) % 2)
                        turned_p(u + n, n % 2)
                        if n >= 2:
                            turned_out(u + n - 2, n - 2)
                        elif not first:
                            turned_out(u + n - 2, n + 2)

                all_groups(act, group)
                for n in (2, 3):
                    turned_out((G - 1) * SPG + n, n)

            @block.tensor
            def _(pe):
                ready(pe)

                def q_and_k(g):
                    for half, base in ((0, SB), (1, TB)):
                        if half == 0:
                            after(pe, "s_free", g * SPG)
                        else:
                            after(pe, "pt_ready", g * SPG - 1)
                            after(pe, "ot_ready", 2 * (g * SPG - 3))
                        for c in range(NC):
                            wc = slice((half * NC + c) * 128, (half * NC + c + 1) * 128)
                            pe.matmul(k.PS[:, base + c, 0:GT], w0[:, wc], k.x0[:, ds(g * GT, GT)], start=True, stop=False)
                            pe.matmul(k.PS[:, base + c, 0:GT], w1[:, wc], k.x1[:, ds(g * GT, GT)], start=False, stop=True).then_inc(s["qk_mm"], 1)

                def scores_and_v(g, n):
                    u = g * SPG + n
                    t = slice(n * L, (n + 1) * L)
                    if n == 0:
                        pe.wait_ge(s["q_ev"], g * NC + NC)
                        pe.wait_ge(s["k_ev_a"], g * NC + NC)
                        pe.wait_ge(s["k_ev_v"], g * NC + NC)
                        pe.wait_ge(s["xg_ready"], g * 2 + 2)
                    after(pe, "s_free", u)
                    for c in range(NC):
                        ins = pe.matmul(k.PS[0:L, SB + c, 0:4 * L], qT[:, c, t], kbd[:, c, n, :, :], start=True, stop=True)
                    ins.then_inc(s["s_mm"], 1)
                    after(pe, "v_ev", u)
                    pe.matmul(k.PS[0:L, VB, 0:D], xg0[:, t], w0[:, WQK:WC], start=True, stop=False)
                    ins = pe.matmul(k.PS[0:L, VB, 0:D], xg1[:, t], w1[:, WQK:WC], start=False, stop=vb is None)
                    if vb is not None:
                        ins = pe.matmul(k.PS[0:L, VB, 0:D], k.ones_row[:, 0:L], vb[:, :], start=False, stop=True)
                    ins.then_inc(s["v_mm"], 1)

                def turn(p, o_too, h):
                    after(pe, "pt_ready", p)
                    after(pe, "ot_ready", 2 * (p - 2))
                    if o_too:
                        turn_o(p - 2, h)
                    pe.wait_ge(s["p_ready"], p + 1)
                    for c in range(NC):
                        for j in range(4):
                            ins = pe.transpose(k.PS[0:L, TB + c, j * L:(j + 1) * L], P[:, h, c, j, :], k.ident[0:L, 0:L])
                    ins.then_inc(s["p_turned"], 1)

                def weigh(u, h):
                    pe.wait_ge(s["v_ev"], u + 1)
                    pe.wait_ge(s["pt_ready"], u + 1)
                    after(pe, "o_ready", u)
                    for hd in range(HEADS):
                        ins = pe.matmul(k.PS[0:L, OB, hd * VA:(hd + 1) * VA], PT[:, h, hd // 4, hd % 4, :], vo[:, h, hd, :],
                                        start=True, stop=True)
                    ins.then_inc(s["o_mm"], 1)

                def turn_o(u, h):
                    pe.wait_ge(s["o_ready"], u + 1)
                    oc = o[:, h, :, :].rearrange("p h d -> p (h d)")
                    pe.transpose(k.PS[:, TB, OT:OT + L], oc[:, 0:128], k.ident[0:L, 0:L])
                    pe.transpose(k.PS[0:D1, TB + 1, OT:OT + L], oc[:, 128:D], k.ident[0:L, 0:L]).then_inc(s["o_turned"], 1)

                def project(g):
                    pe.wait_ge(s["ot_ready"], g * 2 * SPG + 2 * SPG)
                    for j in range(TPG):
                        t = slice(j * TP, (j + 1) * TP)
                        pe.matmul(k.PS[0:TP, TB + j, 0:D], oT0[:, t], p0[:, :], start=True, stop=False)
                        pe.matmul(k.PS[0:TP, TB + j, 0:D], oT1[:, t], p1[:, :], start=False, stop=False)
                        ins = pe.matmul(k.PS[0:TP, TB + j, 0:D], k.ones_row[:, 0:TP], pb[:, :], start=False, stop=True)
                    ins.then_inc(s["y_mm"], 1)

                def group(g, first, last):
                    u = g * SPG
                    if first:
                        q_and_k(0)
                        scores_and_v(0, 0)
                    for n in range(SPG):
                        if n + 1 < SPG:
                            scores_and_v(g, n + 1)
                        elif not last:
                            q_and_k(g + 1)
                        if n == 2 and not first:
                            pe.wait_ge(s["pt_ready"], u + 2)
                            project(g - 1)
                        if n >= 1 or not first:
                            weigh(u + n - 1, (n - 1) % 2)
                        if n + 1 == SPG and not last:
                            scores_and_v(g + 1, 0)
                        if n == 2 and not first:
                            pe.wait_ge(s["y_added"], g)
                        turn(u + n, n >= 2 or not first, n % 2)

                all_groups(pe, group)
                u = G * SPG
                weigh(u - 1, 1)
                pe.wait_ge(s["pt_ready"], u)
                pe.wait_ge(s["ot_ready"], 2 * (u - 2))
                turn_o(u - 2, 0)
                pe.wait_ge(s["ot_ready"], 2 * (u - 1))
                turn_o(u - 1, 1)
                project(G - 1)


class ExpertBuffers:

    def __init__(self, k, ctx, tag, up, down, n_up):
        self.up, self.down = up, down
        self.xh = k.sb(ctx, tag + "xh", [128, T], BF16)
        self.xl = k.sb(ctx, tag + "xl", [128, T], BF16)
        self.xr = k.sb(ctx, tag + "xr", [128, T], BF16)
        self.f0 = k.sb(ctx, tag + "f0", [128, n_up])
        self.f1 = k.sb(ctx, tag + "f1", [128, n_up])
        self.fd = k.sb(ctx, tag + "fd", [128, IC * D])
        self.uh, self.ul, self.rh, self.rl = (k.sb(ctx, tag + n, [128, 2, n_up], BF16) for n in ("uh", "ul", "rh", "rl"))
        self.dh, self.dl = (k.sb(ctx, tag + n, [128, 2, IC * D], BF16) for n in ("dh", "dl"))

    N_LOADS = 4

    def load(self, e):
        return ((self.f0[:, :], self.up[ds(e, 1), 0:128, :].rearrange("a p n -> (a p) n")),
                (self.f1[0:D1, :], self.up[ds(e, 1), 128:D, :].rearrange("a p n -> (a p) n")),
                (self.f1[D1:2 * D1, :], self.up[ds(e, 1), 128:D, :].rearrange("a p n -> (a p) n")),
                (self.fd[:, :].rearrange("p (c n) -> p c n", n=D),
                 self.down[ds(e, 1), :, :].rearrange("a (c p) n -> p (a c) n", p=128)))

    def parts(self):
        return (self.f0, self.uh, self.ul), (self.f1, self.rh, self.rl), (self.fd, self.dh, self.dl)


def router(k, tag, cw, gate, on_softmax, eb, gate_b=None, b2=None, n_cols=NE):
    nc = k.nc
    HT = NTILE // 2
    NB = 4
    with k.phase() as ctx:
        g0 = k.sb(ctx, tag + "g0", [128, NE])
        g1 = k.sb(ctx, tag + "g1", [D1, NE])
        gbias = k.sb(ctx, tag + "gbias", [TP, NE])
        big = lambda n: k.sb(ctx, tag + n, [TP, NTILE, NE])
        lg, pr, key, cand, oh1, oh2, rank = (big(n) for n in ("lg", "pr", "key", "cand", "oh1", "oh2", "rank"))
        r1 = k.sb(ctx, tag + "r1", [TP, 8, NTILE])
        w_in = k.sem(ctx, tag + "w_in")
        l_mm = k.sem(ctx, tag + "l_mm")
        l_ready = k.sem(ctx, tag + "l_ready")
        shifted = k.sem(ctx, tag + "shifted")
        exp_ready = k.sem(ctx, tag + "exp_ready")
        step = k.sem(ctx, tag + "step")
        e_in = k.sem(ctx, tag + "e_in")
        w_high = k.sem(ctx, tag + "w_high")
        x_high = k.sem(ctx, tag + "x_high")
        n_loads = 2 + (gate_b is not None)
        if b2 is not None:
            b2s = k.sb(ctx, tag + "b2s", [HT * NE, HT, D])
            cwT = k.sb(ctx, tag + "cwT", [HT * NE, 2, TP])
            b2_in = k.sem(ctx, tag + "b2_in")
            cw_ready = k.sem(ctx, tag + "cw_ready")
            cw_turned = k.sem(ctx, tag + "cw_turned")
            cwT_ready = k.sem(ctx, tag + "cwT_ready")
            b_mm = k.sem(ctx, tag + "b_mm")
            b_added = k.sem(ctx, tag + "b_added")
        with nc.Block() as block:

            @block.sync
            def _(sp):
                sp.dma_start(g0[:, :], gate[0:128, :]).then_inc(w_in, 16)
                sp.dma_start(g1[:, :], gate[128:D, :]).then_inc(w_in, 16)
                if gate_b is not None:
                    sp.dma_start(gbias[:, :], gate_b.to_broadcast([TP, NE])).then_inc(w_in, 16)
                for dst, src in eb.load(0):
                    sp.dma_start(dst, src).then_inc(e_in, 16)
                if b2 is not None:
                    sp.dma_start(b2s[:, :, :], b2).then_inc(b2_in, 16)

            @block.gpsimd
            def _(po):
                po.wait_ge(e_in, 16 * eb.N_LOADS)
                for full, high, low in eb.parts():
                    po.tensor_copy(high[:, 0, :], full[:, :]).then_inc(w_high, 1)
                for q, (full, high, low) in enumerate(eb.parts()):
                    po.wait_ge(w_high, q + 1)
                    po.tensor_tensor(low[:, 0, :], full[:, :], high[:, 0, :], ALU.subtract)

            @block.tensor
            def _(pe):
                pe.wait_ge(w_in, 16 * n_loads)
                for t in range(NTILE):
                    y = k.PS[0:TP, 0, t * NE:(t + 1) * NE]
                    c = slice(t * TP, (t + 1) * TP)
                    pe.matmul(y, k.x0[:, c], g0[:, :], start=True, stop=False)
                    ins = pe.matmul(y, k.x1[:, c], g1[:, :], start=False, stop=True)
                ins.then_inc(l_mm, 1)
                if b2 is None:
                    return
                pe.wait_ge(cw_ready, 1)
                for h in range(2):
                    pe.transpose(k.PS[0:HT * NE, 1 + h, 0:TP], cw[:, h * HT * NE:(h + 1) * HT * NE],
                                 k.ident[0:TP, 0:TP]).then_inc(cw_turned, 1)
                pe.wait_ge(b2_in, 16)
                for t in range(NTILE):
                    if t % HT == 0:
                        pe.wait_ge(cwT_ready, t // HT + 1)
                    if t >= NB:
                        pe.wait_ge(b_added, t - NB + 1)
                    pe.matmul(k.PS[0:TP, 3 + t % NB, 0:D], cwT[:, t // HT, :], b2s[:, t % HT, :],
                              start=True, stop=True).then_inc(b_mm, 1)

            @block.scalar
            def _(act):
                act.activation(eb.xh[:, :], k.x0[:, :], ACT.Copy).then_inc(x_high, 1)
                act.activation(eb.xr[0:D1, :], k.x1[:, :], ACT.Copy).then_inc(x_high, 1)
                act.wait_ge(l_mm, 1)
                act.activation(lg[:, :, :], k.PS[0:TP, 0, 0:NTILE * NE].rearrange("p (t e) -> p t e", e=NE), ACT.Copy).then_inc(l_ready, 1)
                act.wait_ge(shifted, 1)
                act.activation(pr[:, :, :], pr[:, :, :], ACT.Exp).then_inc(exp_ready, 1)
                if b2 is None:
                    return
                for h in range(2):
                    act.wait_ge(cw_turned, h + 1)
                    act.activation(cwT[:, h, :], k.PS[0:HT * NE, 1 + h, 0:TP], ACT.Copy).then_inc(cwT_ready, 1)

            @block.vector
            def _(v):
                v.wait_ge(x_high, 2)
                v.tensor_tensor(eb.xl[:, :], k.x0[:, :], eb.xh[:, :], ALU.subtract)
                v.tensor_tensor(eb.xr[D1:2 * D1, :], k.x1[:, :], eb.xr[0:D1, :], ALU.subtract)

                def over(x):
                    return x.unsqueeze(2).to_broadcast([TP, NTILE, NE])

                done = 0

                def after(ins):
                    nonlocal done
                    done += 1
                    ins.then_inc(step, 1)
                    v.wait_ge(step, done)

                for e in range(NE):
                    ins = v.memset(rank[:, :, e], float(NE - e))
                after(ins)
                cwv = cw[:, :].rearrange("p (t e) -> p t e", e=n_cols)
                if n_cols > NE:
                    after(v.memset(cwv[:, :, NE:n_cols], 0.5))
                v.wait_ge(l_ready, 1)
                if gate_b is not None:
                    v.wait_ge(w_in, 16 * n_loads)
                    after(v.tensor_tensor(lg[:, :, :], lg[:, :, :], gbias[:, :].unsqueeze(1).to_broadcast([TP, NTILE, NE]), ALU.add))
                after(v.tensor_reduce(r1[:, 0, :], lg[:, :, :], X, ALU.max))
                v.tensor_tensor(pr[:, :, :], lg[:, :, :], over(r1[:, 0, :]), ALU.subtract).then_inc(shifted, 1)
                v.wait_ge(exp_ready, 1)
                if on_softmax:
                    after(v.tensor_reduce(r1[:, 1, :], pr[:, :, :], X, ALU.add))
                    after(v.reciprocal(r1[:, 2, :], r1[:, 1, :]))
                    after(v.tensor_tensor(pr[:, :, :], pr[:, :, :], over(r1[:, 2, :]), ALU.mult))
                src = pr if on_softmax else lg
                for n, oh in enumerate((oh1, oh2)):
                    after(v.tensor_reduce(r1[:, 3, :], src[:, :, :], X, ALU.max))
                    after(v.tensor_tensor(cand[:, :, :], src[:, :, :], over(r1[:, 3, :]), ALU.is_equal))
                    after(v.tensor_tensor(cand[:, :, :], cand[:, :, :], rank[:, :, :], ALU.mult))
                    after(v.tensor_reduce(r1[:, 4, :], cand[:, :, :], X, ALU.max))
                    after(v.tensor_tensor(oh[:, :, :], cand[:, :, :], over(r1[:, 4, :]), ALU.is_equal))
                    if n == 0:
                        after(v.scalar_tensor_tensor(key[:, :, :], oh[:, :, :], -1e30, src[:, :, :], ALU.mult, ALU.add))
                        src = key
                after(v.tensor_tensor(oh1[:, :, :], oh1[:, :, :], oh2[:, :, :], ALU.add))
                after(v.tensor_tensor(pr[:, :, :], pr[:, :, :], oh1[:, :, :], ALU.mult))
                after(v.tensor_reduce(r1[:, 5, :], pr[:, :, :], X, ALU.add))
                if on_softmax:
                    after(v.tensor_scalar(r1[:, 5, :], r1[:, 5, :], 1e-8, None, ALU.add))
                after(v.reciprocal(r1[:, 6, :], r1[:, 5, :]))
                after(v.tensor_tensor(cwv[:, :, 0:NE], pr[:, :, :], over(r1[:, 6, :]), ALU.mult))
                if b2 is None:
                    return
                v.sem_inc(cw_ready, 1)
                for t in range(NTILE):
                    v.wait_ge(b_mm, t + 1)
                    r = k.H[:, t * D:(t + 1) * D]
                    v.tensor_tensor(r, k.PS[0:TP, 3 + t % NB, 0:D], r, ALU.add).then_inc(b_added, 1)


def experts(k, tag, cw, n_exp, eb, gated, b1=None):
    nc = k.nc
    NQ = 2 if gated else 1
    NU = NQ * HID
    NG = n_exp * G
    LAG = 2
    NB = 3
    assert n_exp % 2 == 0 and IC % 2 == 0 and IC % NB == 0
    with k.phase() as ctx:
        xh, xl, xr, uh, ul, rh, rl, dh, dl = eb.xh, eb.xl, eb.xr, eb.uh, eb.ul, eb.rh, eb.rl, eb.dh, eb.dl
        b1s = k.sb(ctx, tag + "b1s", [128, n_exp * IC])
        sg = k.sb(ctx, tag + "sg", [128, 2, GT])
        hf = k.sb(ctx, tag + "hf", [128, 2, GT])
        hi = k.sb(ctx, tag + "hi", [128, NB, GT], BF16)
        lo = k.sb(ctx, tag + "lo", [128, NB, GT], BF16)
        b1_in = k.sem(ctx, tag + "b1_in")
        w_in = k.sem(ctx, tag + "w_in")
        split_begun = k.sem(ctx, tag + "split_begun")
        w_high = k.sem(ctx, tag + "w_high")
        w_split = k.sem(ctx, tag + "w_split")
        up_mm = k.sem(ctx, tag + "up_mm")
        act_ready = k.sem(ctx, tag + "act_ready")
        hf_ready = k.sem(ctx, tag + "hf_ready")
        hi_ready = k.sem(ctx, tag + "hi_ready")
        h_ready = k.sem(ctx, tag + "h_ready")
        down_mm = k.sem(ctx, tag + "down_mm")
        y_added = k.sem(ctx, tag + "y_added")
        with nc.Block() as block:

            @block.sync
            def _(sp):
                if b1 is not None:
                    sp.dma_start(b1s[:, :], b1).then_inc(b1_in, 16)
                with sp.Fori(1, n_exp) as e:
                    sp.wait_ge(w_split, e + 1)
                    for dst, src in eb.load(e):
                        sp.dma_start(dst, src).then_inc(w_in, 16)

            @block.gpsimd
            def _(po):
                def split(e, h):
                    po.wait_ge(w_in, e * (16 * eb.N_LOADS))
                    po.wait_ge(y_added, e * (G * TPG) + 1)
                    po.sem_inc(split_begun, 1)
                    for full, high, low in eb.parts():
                        po.tensor_copy(high[:, h, :], full[:, :]).then_inc(w_high, 1)
                    for q, (full, high, low) in enumerate(eb.parts()):
                        po.wait_ge(w_high, (e - 1) * 3 + q + 1)
                        ins = po.tensor_tensor(low[:, h, :], full[:, :], high[:, h, :], ALU.subtract)
                    ins.then_inc(w_split, 1)

                split(1, 1)
                with po.Fori(1, n_exp // 2) as ee:
                    for h in range(2):
                        split(ee * 2 + h, h)

            @block.tensor
            def _(pe):
                pe.sem_inc(down_mm, NB)

                def first(h, n, c, g):
                    pe.wait_ge(hf_ready, n + 1)
                    x = ds(g * GT, GT)
                    for q in range(NQ):
                        w = slice(q * HID + c * 128, q * HID + (c + 1) * 128)
                        y = k.PS[:, 2 * (c % 2) + q, 0:GT]
                        pe.matmul(y, uh[:, h, w], xh[:, x], start=True, stop=False)
                        pe.matmul(y, uh[:, h, w], xl[:, x], start=False, stop=False)
                        pe.matmul(y, ul[:, h, w], xh[:, x], start=False, stop=False)
                        pe.matmul(y, rh[:, h, w], xr[:, x], start=False, stop=False)
                        ins = pe.matmul(y, rl[:, h, w], xr[:, x], start=False, stop=True)
                    ins.then_inc(up_mm, 1)

                def second(h, n, c, ng):
                    pe.wait_ge(h_ready, n + 3)
                    w = slice(c * D, (c + 1) * D)
                    for j in range(TPG):
                        if c == 0:
                            pe.wait_ge(y_added, ng * TPG + (j + 2 + (G - 1) * TPG))
                        y = k.PS[0:TP, 4 + j, 0:D]
                        t = slice(j * TP, (j + 1) * TP)
                        pe.matmul(y, hi[:, c % NB, t], dh[:, h, w], start=(c == 0), stop=False)
                        pe.matmul(y, hi[:, c % NB, t], dl[:, h, w], start=False, stop=False)
                        ins = pe.matmul(y, lo[:, c % NB, t], dh[:, h, w], start=False, stop=(c == IC - 1))
                    ins.then_inc(down_mm, 1)

                def group(h, g, ng, before):
                    for c in range(IC):
                        first(h, ng * IC + c, c, g)
                        if c >= LAG:
                            second(h, ng * IC + (c - LAG), c - LAG, ng)
                        elif before is not None:
                            second(before, (ng - 1) * IC + (c + IC - LAG), c + IC - LAG, ng - 1)

                def rest(h, e):
                    with pe.Fori(1, G) as g:
                        group(h, g, e * G + g, h)

                def weights(e):
                    pe.wait_ge(w_split, e + 2)

                weights(0)
                group(0, 0, 0, None)
                rest(0, 0)
                weights(1)
                group(1, 0, G, 0)
                rest(1, 1)
                with pe.Fori(1, n_exp // 2) as ee:
                    for h in range(2):
                        e = ee * 2 + h
                        weights(e)
                        group(h, 0, e * G, 1 - h)
                        rest(h, e)
                for c in range(IC - LAG, IC):
                    second(1, (NG - 1) * IC + c, c, NG - 1)

            @block.scalar
            def _(act):
                if b1 is not None:
                    act.wait_ge(b1_in, 16)
                act.preload_act_table(ACT.Silu if gated else ACT.Gelu)

                def high(n, c):
                    act.wait_ge(hf_ready, n + 3)
                    act.wait_ge(down_mm, n + 1)
                    act.activation(hi[:, c % NB, :], hf[:, c % 2, :], ACT.Copy).then_inc(hi_ready, 1)

                with act.Fori(0, n_exp) as e:
                    with act.Fori(0, G) as g:
                        for c in range(IC):
                            n = (e * G + g) * IC + c
                            bank = 2 * (c % 2)
                            act.wait_ge(up_mm, n + 1)
                            if gated:
                                act.wait_ge(hf_ready, n + 1)
                                act.activation(sg[:, c % 2, :], k.PS[:, bank, 0:GT], ACT.Silu).then_inc(act_ready, 1)
                            else:
                                act.wait_ge(h_ready, n + 1)
                                act.activation(hf[:, c % 2, :], k.PS[:, bank, 0:GT], ACT.Gelu,
                                               bias=b1s[:, ds(e * IC + c, 1)]).then_inc(hf_ready, 1)
                            high(n, c)

            @block.vector
            def _(v):
                v.sem_inc(hf_ready, 2)
                v.sem_inc(h_ready, 2)
                v.sem_inc(w_split, 2)
                v.sem_inc(y_added, G * TPG + 1)

                def low(n, c):
                    v.wait_ge(hi_ready, n + 1)
                    v.wait_ge(down_mm, n + 1)
                    v.tensor_tensor(lo[:, c % NB, :], hf[:, c % 2, :], hi[:, c % NB, :], ALU.subtract).then_inc(h_ready, 1)

                def chunk(n, c):
                    v.wait_ge(act_ready, n + 1)
                    v.wait_ge(h_ready, n + 1)
                    v.tensor_tensor(hf[:, c % 2, :], sg[:, c % 2, :], k.PS[:, 2 * (c % 2) + 1, 0:GT],
                                    ALU.mult).then_inc(hf_ready, 1)

                def add(e, g, ng):
                    v.wait_ge(down_mm, ng * IC + IC + NB)
                    for j in range(TPG):
                        t = g * TPG + j
                        r = k.H[:, ds(t * D, D)]
                        v.scalar_tensor_tensor(r, k.PS[0:TP, 4 + j, 0:D], cw[:, ds(t * n_exp + e, 1)], r,
                                               ALU.mult, ALU.add).then_inc(y_added, 1)

                def group(ng, before):
                    for c in range(IC):
                        if gated:
                            chunk(ng * IC + c, c)
                        if c == LAG - 1 and before is not None:
                            add(*before)
                        low(ng * IC + c, c)

                def rest(e):
                    with v.Fori(1, G) as g:
                        group(e * G + g, (e, g - 1, e * G + g - 1))

                group(0, None)
                rest(0)
                with v.Fori(1, n_exp) as e:
                    group(e * G, (e - 1, G - 1, e * G - 1))
                    rest(e)
                add(n_exp - 1, G - 1, NG - 1)


KH, KQ, HH = 12, 6, 64
NKC = KH // 2
NQC = KQ // 2
NZ = 1 + NKC + 2 * NQC
KS = 4
EX = 3 * HH
MAXLEN = 1024


KV_AT = (1, 2, 3, 4, 7, 8)
Q_AT = ((5, 6), (9, 10), (11, 12))
CONV = ((0, 1), (2,), (3,), (4, 5), (6, 7), (8, 9), (10, 11, 12))
assert len(KV_AT) == NKC == 6 and len(Q_AT) == NQC and NZ == 13


def heads_of(c):
    return 4 * (c // 2) + c % 2, 4 * (c // 2) + 2 + c % 2


PART = 32


class MixerWeights:

    def __init__(self, k, ctx, tag, a):
        sb = lambda n, shape: k.sb(ctx, tag + n, shape)
        self.wi0 = sb("wi0", [128, NZ * 128])
        self.wi1 = sb("wi1", [D1, NZ * 128])
        self.wg0 = sb("wg0", [128, KH * 128])
        self.wg1 = sb("wg1", [D1, KH * 128])
        self.wr = sb("wr", [128, KH, 2 * EX])
        self.wo = sb("wo", [128, 3 * NKC, D])
        self.cwt = sb("cwt", [128, NZ, KS])
        self.par = sb("par", [128, 4, NKC])
        self.nw = sb("nw", [128, KH])
        self.hp = sb("hp", [KH, 8])
        self.sel_source = a["c_sel"]
        self.tw = sb("tw", [KH, GT])
        self.mask = sb("mask", [128, GT])
        self.mean = sb("mean", [128, 128])
        self.loads = [(self.wi0[:, :], a["mm_wi"][0:128, :]), (self.wi1[:, :], a["mm_wi"][128:D, :]),
                      (self.cwt[:, :, :], a["mm_cw"]), (self.par[:, 0:3, :], a["mm_par"]), (self.hp[:, 0:3], a["mm_hp"]),
                      (self.tw[:, :], a["c_dist"]), (self.mask[:, :], a["c_mask"]),
                      (self.mean[:, :], a["c_mean"]), (self.wg0[:, :], a["mm_wg"][0:128, :]),
                      (self.wg1[:, :], a["mm_wg"][128:D, :]), (self.nw[:, :], a["mm_nw"]),
                      (self.wr[:, :, :], a["mm_wr"]), (self.wo[:, :, :], a["mm_wo"])]


def memory_mixer(k, tag, mw):
    nc = k.nc
    NWO = 3 * NKC
    with k.phase() as ctx:
        wi0, wi1, wg0, wg1, wr, wo, cwt = mw.wi0, mw.wi1, mw.wg0, mw.wg1, mw.wr, mw.wo, mw.cwt
        par, nw, hp, tw, mask, mean = mw.par, mw.nw, mw.hp, mw.tw, mw.mask, mw.mean
        halfpi = k.sb(ctx, tag + "halfpi", [128, 1])
        z = k.sb(ctx, tag + "z", [128, NZ, GT])
        r = k.sb(ctx, tag + "r", [128, NKC, GT])
        f = k.sb(ctx, tag + "f", [128, KH, GT])
        pw, pd = (k.sb(ctx, tag + n, [KH, GT]) for n in ("pw", "pd"))
        st, sa = pw, pd
        parts = k.sb(ctx, tag + "parts", [3 * PART, 2, GT], BF16)
        sel3 = k.sb(ctx, tag + "sel3", [3 * PART, NKC, 128], BF16)
        one = lambda n: k.sb(ctx, tag + n, [128, GT])
        two = lambda n: k.sb(ctx, tag + n, [128, 2, GT])
        four = lambda n: k.sb(ctx, tag + n, [128, 2, 2, GT])
        ab, t1, rq, rn, rs = (one(n) for n in ("ab", "t1", "rq", "rn", "rs"))
        kvw, cc, sq, t0, y0, y1 = (two(n) for n in ("kvw", "cc", "sq", "t0", "y0", "y1"))
        sg, cs, ri, ma, mb = (four(n) for n in ("sg", "cs", "ri", "ma", "mb"))
        sel_in = ma[0:3 * PART, :, :, :].rearrange("p a b n -> p (a b n)")[:, 0:NKC * 128]
        names = ("sel_in", "set", "wr_scaled", "wo_scaled", "par_a", "par_v", "tw_a", "z_mm", "tap_a", "tap_v", "z_taken",
                 "z_ready", "q_ready", "sp_a", "sp_v", "sp_ready", "pw_ready", "parts_set", "begun", "sum_parts_v", "sum_parts_ready", "parts_v", "parts_ready", "id_v", "id_ready", "r_a", "r_ready", "bc_mm",
                 "g_mm", "g_ready", "abs_ready", "newton", "phi_ready", "kvw_ready", "trig_a", "trig_ready", "cc_ready",
                 "rot_ready", "run_v", "run_ready", "prod_ready", "f_ready", "h_ready", "sq_ready", "ssq_mm", "rs_a",
                 "rs_v", "rs_ready", "hn_ready", "ro_mm", "th_ready", "y_ready", "wo_mm", "o_added", "par_ready",
                 "tw_ready")
        s = {n: k.sem(ctx, tag + n) for n in names}
        TH0, Y0, WO0, ADD0 = 2, 4, 4, 1
        BC, SS, RO, OB = 2, 3, 4, 6
        out_tile = lambda j: k.PS[0:TP, OB + j // 2, (j % 2) * D:(j % 2 + 1) * D]

        def after(e, sem, value):
            if not isinstance(value, int) or value > 0:
                e.wait_ge(s[sem], value)

        with nc.Block() as block:

            @block.sync
            def _(sp):
                sp.dma_start(sel_in, mw.sel_source.rearrange("p c n -> p (c n)")).then_inc(s["sel_in"], 16)

            @block.tensor
            def _(pe):
                pe.sem_inc(s["wo_mm"], WO0)

                def conv(g, m):
                    after(pe, "z_taken", g * NZ + (m - 1 if m >= 2 else 0))
                    wc = slice(m * 128, (m + 1) * 128)
                    pe.matmul(k.PS[:, m % 2, 0:GT], wi0[:, wc], k.x0[:, ds(g * GT, GT)], start=True, stop=False)
                    pe.matmul(k.PS[:, m % 2, 0:GT], wi1[:, wc], k.x1[:, ds(g * GT, GT)], start=False, stop=True).then_inc(s["z_mm"], 1)

                def weight(g, c):
                    if c == 0:
                        pe.wait_ge(s["parts_ready"], g + 1)
                        after(pe, "g_ready", g * KH)
                    elif c == 1:
                        pe.wait_ge(s["cc_ready"], g * NKC + 1)
                    else:
                        pe.wait_ge(s["g_ready"], g * KH + 2 * (c - 1))
                    pe.matmul(k.PS[:, BC, 0:GT], sel3[:, c, :], parts[:, 0, :], start=True, stop=True).then_inc(s["bc_mm"], 1)

                def inverse_sum(g, c):
                    if c == 0:
                        pe.wait_ge(s["sum_parts_ready"], g + 1)
                    pe.wait_ge(s["kvw_ready"], g * NKC + c + 1)
                    pe.matmul(k.PS[:, BC, 0:GT], sel3[:, c, :], parts[:, 1, :], start=True, stop=True).then_inc(s["bc_mm"], 1)

                def gate(g, c, i):
                    if i == 1:
                        pe.wait_ge(s["g_ready"], g * KH + 2 * c + 1)
                    elif c + 1 < NKC:
                        pe.wait_ge(s["cc_ready"], g * NKC + c + 2)
                    else:
                        pe.wait_ge(s["g_ready"], g * KH + 2 * c)
                    hd = heads_of(c)[i]
                    wc = slice(hd * 128, (hd + 1) * 128)
                    pe.matmul(k.PS[:, BC, 0:GT], wg0[:, wc], k.x0[:, ds(g * GT, GT)], start=True, stop=False)
                    pe.matmul(k.PS[:, BC, 0:GT], wg1[:, wc], k.x1[:, ds(g * GT, GT)], start=False, stop=True).then_inc(s["g_mm"], 1)

                def squares(g, c):
                    for n in (2 * c, 2 * c + 1):
                        if n == 0:
                            after(pe, "rs_ready", g)
                        pe.wait_ge(s["sq_ready"], g * KH + n + 1)
                        pe.matmul(k.PS[:, SS, 0:GT], mean[:, :], sq[:, n % 2, :], start=(n == 0), stop=(n == KH - 1)).then_inc(s["ssq_mm"], 1)

                def readout(g, c, i, q):
                    n = 2 * c + i
                    if q == 0:
                        pe.wait_ge(s["hn_ready"], g * KH + n + 1)
                        pe.wait_ge(s["th_ready"], g * (2 * KH) + (2 * (n - 1) + 1 + TH0))
                    elif q == 1:
                        pe.wait_ge(s["y_ready"], g * (2 * KH) + (2 * (n - 1) + 2 + Y0))
                    else:
                        pe.wait_ge(s["y_ready"], g * (2 * KH) + (2 * n + 1 + Y0))
                    hd = heads_of(c)[i]
                    pe.matmul(k.PS[:, RO + (3 * i + q) % 2, 0:GT], wr[:, hd, q * 128:(q + 1) * 128], f[:, hd, :],
                              start=True, stop=True).then_inc(s["ro_mm"], 1)

                def out_product(g, c, q):
                    if c == 0 and q == 0:
                        pe.wait_ge(s["o_added"], g + ADD0)
                        pe.wait_ge(s["wo_scaled"], 1)
                    pe.wait_ge(s["y_ready"], g * (2 * KH) + (4 * c + (1, 3, 4)[q] + Y0))
                    n = 3 * c + q
                    for j in range(TPG):
                        t = slice(j * TP, (j + 1) * TP)
                        y = y0[:, q, t] if q < 2 else y1[:, c % 2, t]
                        ins = pe.matmul(out_tile(j), y, wo[:, n, :], start=(n == 0 and j != 1), stop=(n == NWO - 1 and j != 0))
                    ins.then_inc(s["wo_mm"], 1)

                def round_of(A, B, C):
                    for t in range(NKC):
                        if B is not None:
                            weight(B, t)
                        if C is not None:
                            readout(C, t, 0, 0)
                            readout(C, t, 0, 1)
                        if C is not None and t >= 1:
                            out_product(C, t - 1, 0)
                            out_product(C, t - 1, 1)
                        if B is not None:
                            inverse_sum(B, t)
                        if C is not None and t >= 1:
                            out_product(C, t - 1, 2)
                        if A is not None and t > 0:
                            conv(A, CONV[t][0])
                        if C is not None:
                            readout(C, t, 0, 2)
                            readout(C, t, 1, 0)
                        if A is not None and t == 0:
                            conv(A, CONV[t][0])
                        if B is not None and t >= 1:
                            gate(B, t - 1, 0)
                        if C is not None:
                            readout(C, t, 1, 1)
                        if B is not None and t >= 1:
                            gate(B, t - 1, 1)
                        if C is not None:
                            readout(C, t, 1, 2)
                        for n in CONV[t][1:] if A is not None else ():
                            conv(A, n)
                        if B is not None and t >= 3:
                            squares(B, t - 3)
                    if B is not None:
                        gate(B, NKC - 1, 0)
                    if A is not None:
                        conv(A, CONV[NKC][0])
                    if B is not None:
                        gate(B, NKC - 1, 1)
                    if A is not None:
                        conv(A, CONV[NKC][1])
                    if C is not None:
                        for q in range(3):
                            out_product(C, NKC - 1, q)
                    if B is not None:
                        squares(B, NKC - 3)
                    if A is not None:
                        conv(A, CONV[NKC][2])
                    if B is not None:
                        squares(B, NKC - 2)
                        squares(B, NKC - 1)

                round_of(0, None, None)
                round_of(1, 0, None)
                pe.wait_ge(s["wr_scaled"], KH)
                with pe.Fori(1, G - 1) as g:
                    round_of(g + 1, g, g - 1)
                round_of(None, G - 1, G - 2)
                round_of(None, None, G - 1)

            @block.scalar
            def _(act):
                act.sem_inc(s["th_ready"], TH0)
                act.activation(par[:, 0, :], par[:, 0, :], ACT.Sigmoid).then_inc(s["par_a"], 1)
                act.activation(par[:, 1, :], par[:, 1, :], ACT.Exp).then_inc(s["par_a"], 1)
                act.activation(hp[:, 3:4], hp[:, 2:3], ACT.Abs).then_inc(s["tw_a"], 1)
                act.wait_ge(s["tw_a"], 1)
                act.activation(hp[:, 4:5], hp[:, 3:4], ACT.Exp, scale=-1.0).then_inc(s["tw_a"], 1)
                act.wait_ge(s["tw_a"], 2)
                act.activation(hp[:, 5:6], hp[:, 4:5], ACT.Ln, bias=1.0).then_inc(s["par_a"], 1)
                act.wait_ge(s["tw_ready"], 1)
                act.activation(tw[:, :], tw[:, :], ACT.Exp, scale=hp[:, 7:8]).then_inc(s["tw_a"], 1)
                act.wait_ge(s["par_ready"], 1)
                act.wait_ge(s["set"], 1)

                def tap(g, m):
                    n = KH if m == 0 else 128
                    act.wait_ge(s["z_mm"], g * NZ + m + 1)
                    if m in KV_AT:
                        after(act, "phi_ready", (g - 1) * NKC + KV_AT.index(m) + 1)
                    for q in range(NQC):
                        if m in Q_AT[q]:
                            after(act, "prod_ready", (g - 1) * NKC + (2 * q + 2))
                    act.activation(z[0:n, m, :], k.PS[0:n, m % 2, 0:GT], ACT.Copy, scale=cwt[0:n, m, KS - 1:KS]).then_inc(s["tap_a"], 1)

                def silu(g, m):
                    n = KH if m == 0 else 128
                    act.wait_ge(s["z_taken"], g * NZ + m + 1)
                    act.activation(z[0:n, m, :], z[0:n, m, :], ACT.Silu).then_inc(s["z_ready" if m == 0 or m in KV_AT else "q_ready"], 1)

                def phase_abs(g, c):
                    i = g * NKC + c
                    after(act, "phi_ready", i)
                    act.activation(ab[:, :], z[:, KV_AT[c], :], ACT.Abs, scale=par[:, 2, c:c + 1]).then_inc(s["abs_ready"], 1)

                def trig(g, c):
                    p = c % 2
                    i = g * NKC + c
                    act.wait_ge(s["phi_ready"], i + 1)
                    act.activation(cs[:, p, 0, :], cs[:, p, 1, :], ACT.Abs).then_inc(s["trig_a"], 1)
                    act.wait_ge(s["trig_a"], i + 1)
                    act.activation(cs[:, p, 1, :], cs[:, p, 1, :], ACT.Sin)
                    act.activation(cs[:, p, 0, :], cs[:, p, 0, :], ACT.Sin, scale=-1.0, bias=halfpi[:, :]).then_inc(s["trig_ready"], 1)

                def norm_scale(g, c):
                    i = g * NKC + c
                    after(act, "run_ready", i - 1)
                    act.wait_ge(s["bc_mm"], g * (2 * NKC) + 2 * c + 2)
                    act.activation(cc[:, c % 2, :], k.PS[:, BC, 0:GT], ACT.Copy, scale=par[:, 1, c:c + 1]).then_inc(s["cc_ready"], 1)

                def gate(g, c, i):
                    after(act, "h_ready", g * NKC + (c - 1))
                    act.wait_ge(s["g_mm"], g * KH + 2 * c + i + 1)
                    act.activation(sg[:, c % 2, i, :], k.PS[:, BC, 0:GT], ACT.Silu).then_inc(s["g_ready"], 1)

                def square(g, c):
                    act.wait_ge(s["h_ready"], g * NKC + c + 1)
                    for i, hd in enumerate(heads_of(c)):
                        n = 2 * c + i
                        after(act, "ssq_mm", g * KH + (n - 1))
                        act.activation(sq[:, n % 2, :], f[:, hd, :], ACT.Square).then_inc(s["sq_ready"], 1)

                def gates_tanh(g, c, i):
                    ro = g * (3 * KH) + 6 * c + 3 * i
                    act.wait_ge(s["y_ready"], g * (2 * KH) + (4 * (c - 1) + 2 * i + 2 + Y0))
                    act.wait_ge(s["ro_mm"], ro + 2)
                    act.activation(t0[:, i, :], k.PS[:, RO + (3 * i + 1) % 2, 0:GT], ACT.Tanh, scale=0.5).then_inc(s["th_ready"], 1)

                def rest_tanh(g, c, i):
                    ro = g * (3 * KH) + 6 * c + 3 * i
                    act.wait_ge(s["ro_mm"], ro + 3)
                    gr, vr = (slice(64, 128), slice(0, 64)) if i == 0 else (slice(0, 64), slice(64, 128))
                    act.activation(t1[vr, :], k.PS[gr, RO + (3 * i + 2) % 2, 0:GT], ACT.Tanh, scale=0.5).then_inc(s["th_ready"], 1)

                def softplus_start(g):
                    act.wait_ge(s["z_ready"], g * (1 + NKC) + 1)
                    after(act, "parts_ready", g)
                    after(act, "sum_parts_ready", g)
                    act.activation(st[:, :], z[0:KH, 0, :], ACT.Identity, scale=hp[:, 0:1], bias=hp[:, 1:2]).then_inc(s["sp_a"], 1)
                    act.wait_ge(s["sp_a"], g * 3 + 1)
                    act.activation(sa[:, :], st[:, :], ACT.Abs).then_inc(s["sp_a"], 1)

                def divisor_abs(g, c):
                    act.wait_ge(s["z_ready"], g * (1 + NKC) + 2 + c)
                    act.activation(r[:, c, :], z[:, KV_AT[c], :], ACT.Abs, scale=par[:, 2, c:c + 1]).then_inc(s["r_a"], 1)

                def softplus_end(g):
                    act.wait_ge(s["sp_a"], g * 3 + 2)
                    act.activation(sa[:, :], sa[:, :], ACT.Exp, scale=-1.0).then_inc(s["sp_a"], 1)
                    act.wait_ge(s["sp_a"], g * 3 + 3)
                    act.activation(sa[:, :], sa[:, :], ACT.Ln, bias=1.0).then_inc(s["sp_ready"], 1)

                def logarithms(g):
                    for c in range(NKC):
                        act.wait_ge(s["r_a"], g * (2 * NKC) + c + 1)
                        act.activation(r[:, c, :], r[:, c, :], ACT.Ln, bias=1.0).then_inc(s["r_a"], 1)

                def exponentials(g):
                    for c in range(NKC):
                        act.wait_ge(s["r_a"], g * (2 * NKC) + NKC + c + 1)
                        act.activation(r[:, c, :], r[:, c, :], ACT.Exp, scale=-1.0).then_inc(s["r_ready"], 1)

                def norm(g):
                    after(act, "rs_ready", g)
                    act.wait_ge(s["ssq_mm"], g * KH + KH)
                    act.activation(rq[:, :], k.PS[:, SS, 0:GT], ACT.Ln, bias=k.eps6[:, :]).then_inc(s["rs_a"], 1)
                    act.wait_ge(s["rs_a"], g * 2 + 1)
                    act.activation(rq[:, :], rq[:, :], ACT.Exp, scale=-0.5).then_inc(s["rs_a"], 1)

                def round_of(A, B, C):
                    act.preload_act_table(ACT.Silu)
                    for t in range(NKC):
                        if B is not None:
                            phase_abs(B, t)
                        if C is not None:
                            gates_tanh(C, t, 0)
                        if B is not None:
                            norm_scale(B, t)
                            if t > 0:
                                trig(B, t)
                        if C is not None:
                            rest_tanh(C, t, 0)
                        if B is not None and t == 0:
                            trig(B, t)
                        if A is not None:
                            tap(A, CONV[t][0])
                        if B is not None and t >= 1:
                            gate(B, t - 1, 0)
                        if C is not None:
                            gates_tanh(C, t, 1)
                        if B is not None and t >= 1:
                            gate(B, t - 1, 1)
                        if C is not None:
                            rest_tanh(C, t, 1)
                        if B is not None and t >= 3:
                            square(B, t - 3)
                        if A is not None:
                            if t >= 1:
                                if t == 1:
                                    silu(A, 0)
                                silu(A, KV_AT[t - 1])
                            if t >= 2:
                                divisor_abs(A, t - 2)
                            for m in CONV[t][1:]:
                                tap(A, m)
                        if B is not None and t < NQC:
                            silu(B, Q_AT[t][0])
                            silu(B, Q_AT[t][1])
                    if B is not None:
                        gate(B, NKC - 1, 0)
                        gate(B, NKC - 1, 1)
                    if A is not None:
                        tap(A, CONV[NKC][0])
                        silu(A, KV_AT[NKC - 1])
                        softplus_start(A)
                        divisor_abs(A, NKC - 2)
                    if B is not None:
                        square(B, NKC - 3)
                    if A is not None:
                        divisor_abs(A, NKC - 1)
                        tap(A, CONV[NKC][1])
                        softplus_end(A)
                        tap(A, CONV[NKC][2])
                    if B is not None:
                        square(B, NKC - 2)
                        square(B, NKC - 1)
                    if A is not None:
                        logarithms(A)
                    if B is not None:
                        norm(B)
                    if A is not None:
                        exponentials(A)

                round_of(0, None, None)
                round_of(1, 0, None)
                with act.Fori(1, G - 1) as g:
                    round_of(g + 1, g, g - 1)
                round_of(None, G - 1, G - 2)
                round_of(None, None, G - 1)

            @block.vector
            def _(v):
                v.sem_inc(s["y_ready"], Y0)
                v.sem_inc(s["o_added"], ADD0)
                v.memset(halfpi[:, :], float(np.pi / 2)).then_inc(s["set"], 1)
                v.wait_ge(s["par_a"], 3)
                v.tensor_scalar(par[:, 0, :], par[:, 0, :], -2.999, -0.001, ALU.mult, ALU.add).then_inc(s["par_v"], 1)
                v.tensor_scalar(par[:, 3, :], par[:, 1, :], 1e-6, None, ALU.add).then_inc(s["par_v"], 1)
                v.scalar_tensor_tensor(hp[:, 6:7], hp[:, 2:3], 0.0, hp[:, 5:6], ALU.max, ALU.add).then_inc(s["par_v"], 1)
                v.wait_ge(s["par_v"], 3)
                v.reciprocal(par[:, 3, :], par[:, 3, :]).then_inc(s["par_v"], 1)
                v.tensor_scalar(hp[:, 7:8], hp[:, 6:7], -1.0, None, ALU.mult).then_inc(s["tw_ready"], 1)
                v.wait_ge(s["par_v"], 4)
                v.scalar_tensor_tensor(par[:, 1, :], par[:, 1, :], float(HH) ** -0.5, par[:, 3, :], ALU.mult, ALU.mult).then_inc(s["par_v"], 1)
                v.wait_ge(s["par_v"], 5)
                v.tensor_tensor(par[:, 3, :], par[:, 0, :], par[:, 2, :], ALU.mult).then_inc(s["par_ready"], 1)
                v.wait_ge(s["par_ready"], 1)
                v.wait_ge(s["tw_a"], 3)
                v.wait_ge(s["parts_set"], 2)

                def taps(g, m):
                    n = KH if m == 0 else 128
                    v.wait_ge(s["tap_a"], g * NZ + m + 1)
                    zs = z[0:n, m, :].rearrange("p (s l) -> p s l", s=SPG)
                    ps = k.PS[0:n, m % 2, 0:GT].rearrange("p (s l) -> p s l", s=SPG)
                    for q in range(1, KS):
                        ins = v.scalar_tensor_tensor(zs[:, :, q:L], ps[:, :, 0:L - q], cwt[0:n, m, KS - 1 - q:KS - q], zs[:, :, q:L],
                                                     ALU.mult, ALU.add)
                        if q < KS - 1:
                            ins.then_inc(s["tap_v"], 1)
                            v.wait_ge(s["tap_v"], g * (2 * NZ) + 2 * m + q)
                    ins.then_inc(s["z_taken"], 1)

                def weights(g):
                    v.wait_ge(s["sp_ready"], g + 1)
                    v.scalar_tensor_tensor(st[:, :], st[:, :], 0.0, sa[:, :], ALU.max, ALU.add).then_inc(s["sp_v"], 1)
                    v.wait_ge(s["sp_v"], g * 2 + 1)
                    v.tensor_tensor(st[:, :], st[:, :], tw[:, :], ALU.mult).then_inc(s["sp_v"], 1)
                    v.wait_ge(s["sp_v"], g * 2 + 2)
                    v.tensor_scalar(pw[:, :], st[:, :], 1e-4, 5000.0, ALU.max, ALU.min).then_inc(s["pw_ready"], 1)
                    v.wait_ge(s["pw_ready"], g + 1)
                    v.tensor_tensor_scan(pd[:, :], mask[0:KH, :], pw[:, :], 0.0, ALU.mult, ALU.add).then_inc(s["id_v"], 1)
                    v.wait_ge(s["id_v"], g * 2 + 1)
                    v.tensor_scalar(pd[:, :], pd[:, :], 1e-4, None, ALU.max).then_inc(s["id_v"], 1)
                    v.wait_ge(s["id_v"], g * 2 + 2)
                    v.reciprocal(pd[:, :], pd[:, :]).then_inc(s["id_ready"], 1)

                def split_sums(g):
                    rest = rn[PART:PART + KH, :]
                    high, mid, low = (parts[q * PART:q * PART + KH, 1, :] for q in range(3))
                    after(v, "bc_mm", g * (2 * NKC))
                    v.wait_ge(s["id_ready"], g + 1)
                    v.tensor_copy(high, pd[:, :]).then_inc(s["sum_parts_v"], 1)
                    v.wait_ge(s["sum_parts_v"], g * 3 + 1)
                    v.tensor_tensor(rest, pd[:, :], high, ALU.subtract).then_inc(s["sum_parts_v"], 1)
                    v.wait_ge(s["sum_parts_v"], g * 3 + 2)
                    v.tensor_copy(mid, rest).then_inc(s["sum_parts_v"], 1)
                    v.wait_ge(s["sum_parts_v"], g * 3 + 3)
                    v.tensor_tensor(low, rest, mid, ALU.subtract).then_inc(s["sum_parts_ready"], 1)

                def weighted(g, c):
                    i = g * NKC + c
                    after(v, "rot_ready", i - 1)
                    v.wait_ge(s["bc_mm"], g * (2 * NKC) + 2 * c + 1)
                    v.tensor_tensor(kvw[:, c % 2, :], z[:, KV_AT[c], :], k.PS[:, BC, 0:GT], ALU.mult).then_inc(s["kvw_ready"], 1)

                def phase(g, c):
                    i = g * NKC + c
                    v.wait_ge(s["abs_ready"], i + 1)
                    v.wait_ge(s["r_ready"], i + 1)
                    v.scalar_tensor_tensor(ab[:, :], ab[:, :], 1.0, r[:, c, :], ALU.add, ALU.mult).then_inc(s["newton"], 1)
                    v.wait_ge(s["newton"], i * 2 + 1)
                    v.scalar_tensor_tensor(ab[:, :], ab[:, :], 2.0, r[:, c, :], ALU.subtract, ALU.mult).then_inc(s["newton"], 1)
                    v.wait_ge(s["newton"], i * 2 + 2)
                    v.scalar_tensor_tensor(cs[:, c % 2, 1, :], z[:, KV_AT[c], :], par[:, 3, c:c + 1], ab[:, :], ALU.mult, ALU.mult).then_inc(s["phi_ready"], 1)

                def running(g, c):
                    p = c % 2
                    i = g * NKC + c
                    v.wait_ge(s["rot_ready"], i + 1)
                    for h in range(2):
                        v.tensor_tensor_scan(ri[:, p, h, :], mask[:, :], ri[:, p, h, :], 0.0, ALU.mult, ALU.add).then_inc(s["run_v"], 1)
                    v.wait_ge(s["cc_ready"], i + 1)
                    v.wait_ge(s["run_v"], i * 2 + 2)
                    v.tensor_tensor(ri[:, p, :, :], ri[:, p, :, :], cc[:, p, :].unsqueeze(1).to_broadcast([128, 2, GT]), ALU.mult).then_inc(s["run_ready"], 1)

                def match(g, c):
                    p = c % 2
                    v.wait_ge(s["prod_ready"], g * NKC + c + 1)
                    after(v, "ro_mm", (g - 1) * (3 * KH) + 6 * c + 6)
                    for i, hd in enumerate(heads_of(c)):
                        w = slice(64 * i, 64 * i + 64)
                        v.tensor_tensor(f[0:64, hd, :], ma[w, p, 0, :], mb[w, p, 1, :], ALU.add)
                        ins = v.tensor_tensor(f[64:128, hd, :], ma[w, p, 1, :], mb[w, p, 0, :], ALU.subtract)
                    ins.then_inc(s["f_ready"], 1)

                def values(g, c, i):
                    n = 2 * c + i
                    v.wait_ge(s["wo_mm"], g * NWO + (3 * (c - 1) + i + 1 + WO0))
                    v.wait_ge(s["th_ready"], g * (2 * KH) + (2 * n + 1 + TH0))
                    v.scalar_tensor_tensor(y0[:, i, :], t0[:, i, :], 1.0, k.PS[:, RO + (3 * i) % 2, 0:GT], ALU.add, ALU.mult).then_inc(s["y_ready"], 1)

                def rest(g, c, i):
                    n = 2 * c + i
                    v.wait_ge(s["wo_mm"], g * NWO + (3 * (c - 1) + WO0))
                    v.wait_ge(s["th_ready"], g * (2 * KH) + (2 * n + 2 + TH0))
                    vr = slice(0, 64) if i == 0 else slice(64, 128)
                    v.scalar_tensor_tensor(y1[vr, c % 2, :], t1[vr, :], 1.0, k.PS[vr, RO + (3 * i + 2) % 2, 0:GT], ALU.add, ALU.mult).then_inc(s["y_ready"], 1)

                def add(g):
                    v.wait_ge(s["wo_mm"], (g + 1) * NWO + WO0)
                    for j in range(TPG):
                        h = k.H[:, ds((g * TPG + j) * D, D)]
                        ins = v.tensor_tensor(h, out_tile(j), h, ALU.add)
                    ins.then_inc(s["o_added"], 1)

                def norm(g):
                    v.wait_ge(s["rs_a"], g * 2 + 2)
                    v.scalar_tensor_tensor(rn[:, :], k.PS[:, SS, 0:GT], 1e-6, rq[:, :], ALU.add, ALU.mult).then_inc(s["rs_v"], 1)
                    v.wait_ge(s["rs_v"], g * 2 + 1)
                    v.tensor_tensor(rn[:, :], rn[:, :], rq[:, :], ALU.mult).then_inc(s["rs_v"], 1)
                    v.wait_ge(s["rs_v"], g * 2 + 2)
                    after(v, "hn_ready", g * KH)
                    v.scalar_tensor_tensor(rs[:, :], rn[:, :], 3.0, rq[:, :], ALU.subtract, ALU.mult).then_inc(s["rs_ready"], 1)

                def round_of(A, B, C):
                    for t in range(NKC):
                        if B is not None:
                            weighted(B, t)
                            phase(B, t)
                        if C is not None:
                            values(C, t, 0)
                        if B is not None and t >= 1:
                            running(B, t - 1)
                        if C is not None:
                            rest(C, t, 0)
                        if A is not None:
                            taps(A, CONV[t][0])
                        if C is not None:
                            values(C, t, 1)
                        if B is not None and t >= 2:
                            match(B, t - 2)
                        if C is not None:
                            rest(C, t, 1)
                        for n in CONV[t][1:] if A is not None else ():
                            taps(A, n)
                    if B is not None:
                        running(B, NKC - 1)
                        match(B, NKC - 2)
                    if A is not None:
                        taps(A, CONV[NKC][0])
                    if B is not None:
                        match(B, NKC - 1)
                    if A is not None:
                        taps(A, CONV[NKC][1])
                        weights(A)
                        taps(A, CONV[NKC][2])
                    if C is not None:
                        add(C)
                    if B is not None:
                        norm(B)
                    if A is not None:
                        split_sums(A)

                round_of(0, None, None)
                round_of(1, 0, None)
                with v.Fori(1, G - 1) as g:
                    round_of(g + 1, g, g - 1)
                round_of(None, G - 1, G - 2)
                round_of(None, None, G - 1)

            @block.gpsimd
            def _(po):
                po.memset(parts[:, :, :], 0.0).then_inc(s["parts_set"], 1)
                po.wait_ge(s["sel_in"], 16)
                po.tensor_copy(sel3[:, :, :].rearrange("p c n -> p (c n)"), sel_in).then_inc(s["parts_set"], 1)
                po.wait_ge(s["parts_set"], 2)
                for hd in range(KH):
                    po.tensor_scalar(wr[:, hd, :], wr[:, hd, :], nw[:, hd:hd + 1], -0.5, ALU.mult, ALU.mult).then_inc(s["wr_scaled"], 1)
                po.tensor_scalar(wo[:, :, :], wo[:, :, :], 0.5, None, ALU.mult).then_inc(s["wo_scaled"], 1)


                def split_weights(g):
                    rest = mb[PART:PART + KH, 0, 0, :]
                    high, mid, low = (parts[q * PART:q * PART + KH, 0, :] for q in range(3))
                    after(po, "bc_mm", g * (2 * NKC))
                    po.wait_ge(s["pw_ready"], g + 1)
                    po.sem_inc(s["begun"], 1)
                    po.tensor_copy(high, pw[:, :]).then_inc(s["parts_v"], 1)
                    po.wait_ge(s["parts_v"], g * 3 + 1)
                    po.tensor_tensor(rest, pw[:, :], high, ALU.subtract).then_inc(s["parts_v"], 1)
                    po.wait_ge(s["parts_v"], g * 3 + 2)
                    po.sem_inc(s["begun"], 1)
                    po.tensor_copy(mid, rest).then_inc(s["parts_v"], 1)
                    po.wait_ge(s["parts_v"], g * 3 + 3)
                    po.tensor_tensor(low, rest, mid, ALU.subtract).then_inc(s["parts_ready"], 1)
                    po.wait_ge(s["parts_ready"], g + 1)

                def rotate(g, c):
                    p = c % 2
                    i = g * NKC + c
                    after(po, "prod_ready", i - 1)
                    po.wait_ge(s["kvw_ready"], i + 1)
                    po.wait_ge(s["trig_ready"], i + 1)
                    po.tensor_tensor(ri[:, p, :, :], cs[:, p, :, :], kvw[:, p, :].unsqueeze(1).to_broadcast([128, 2, GT]), ALU.mult).then_inc(s["rot_ready"], 1)

                def products(g, c):
                    p = c % 2
                    i = g * NKC + c
                    po.wait_ge(s["run_ready"], i + 1)
                    after(po, "f_ready", i - 1)
                    if c % 2 == 0:
                        po.wait_ge(s["q_ready"], g * (2 * NQC) + (c + 2))
                    for m, q in ((ma, 0), (mb, 1)):
                        qq = z[:, Q_AT[c // 2][q], :].unsqueeze(1).to_broadcast([128, 2, GT])
                        ins = po.tensor_tensor(m[:, p, :, :], ri[:, p, :, :], qq, ALU.mult)
                    ins.then_inc(s["prod_ready"], 1)

                def gated(g, c):
                    po.wait_ge(s["f_ready"], g * NKC + c + 1)
                    po.wait_ge(s["g_ready"], g * KH + 2 * c + 2)
                    for i, hd in enumerate(heads_of(c)):
                        ins = po.tensor_tensor(f[:, hd, :], f[:, hd, :], sg[:, c % 2, i, :], ALU.mult)
                    ins.then_inc(s["h_ready"], 1)

                def normalise(g, c):
                    po.wait_ge(s["rs_ready"], g + 1)
                    for hd in heads_of(c):
                        po.tensor_tensor(f[:, hd, :], f[:, hd, :], rs[:, :], ALU.mult).then_inc(s["hn_ready"], 1)

                def round_of(A, B, C):
                    for t in range(NKC + 2):
                        if C is not None and t == 0:
                            normalise(C, 0)
                        if B is not None and t < NKC:
                            rotate(B, t)
                        if C is not None and t + 1 < NKC:
                            normalise(C, t + 1)
                        if B is not None and 1 <= t <= NKC:
                            products(B, t - 1)
                        if B is not None and t >= 2:
                            gated(B, t - 2)
                    if A is not None:
                        split_weights(A)

                round_of(0, None, None)
                round_of(1, 0, None)
                with po.Fori(1, G - 1) as g:
                    round_of(g + 1, g, g - 1)
                round_of(None, G - 1, G - 2)
                round_of(None, None, G - 1)




def program(nc, a, out):
    with ExitStack() as ctx:
        k = Core(nc, ctx)
        embed(k, a)
        with ExitStack() as part:
            aw = AttentionWeights(k, part, "at1_", a["at1_w"], a["at1_proj"], a["at1_proj_b"], a["at1_qk_b"], a["at1_v_b"])
            layernorm(k, "ln1_", k.H, loads=aw.loads)
            attention(k, "at1_", k.H, aw, smooth=True)
        with ExitStack() as part:
            layernorm(k, "ln2_", k.H)
            cw = k.sb(part, "cw1", [TP, NTILE * (NE + 2)])
            eb = ExpertBuffers(k, part, "ex1_", a["ex1_up"], a["ex1_down"], 2 * HID)
            router(k, "rt1_", cw, a["rt1_gate"], True, eb, n_cols=NE + 2)
            experts(k, "ex1_", cw, NE + 2, eb, True)
        with ExitStack() as part:
            mw = MixerWeights(k, part, "mm_", a)
            layernorm(k, "ln3_", k.H, loads=mw.loads)
            memory_mixer(k, "mm_", mw)
        with ExitStack() as part:
            k.Zr = k.sb(part, "Zr", [TP, NTILE * D])
            layernorm(k, "ln4_", k.H, keep=k.Zr)
            with ExitStack() as at2:
                aw = AttentionWeights(k, at2, "at2_", a["at2_w"], a["at2_proj"], a["at2_proj_b"])
                layernorm(k, "ln5_", k.Zr, gain=(a["ln1_g"], a["ln1_b"]), loads=aw.loads)
                attention(k, "at2_", k.Zr, aw)
            layernorm(k, "ln6_", k.Zr, gain=(a["ln2_g"], a["ln2_b"]), add=(k.H, k.Zr))
            cw = k.sb(part, "cw2", [TP, NTILE * NE])
            eb = ExpertBuffers(k, part, "ex2_", a["ex2_up"], a["ex2_down"], HID)
            router(k, "rt2_", cw, a["rt2_gate"], False, eb, gate_b=a["rt2_gate_b"], b2=a["ex2_b2"])
            experts(k, "ex2_", cw, NE, eb, False, b1=a["ex2_b1"])
        store(k, out)


def store(k, out):
    nc = k.nc
    with k.phase() as ctx:
        stored = k.sem(ctx, "stored")
        with nc.Block() as block:

            @block.sync
            def _(sp):
                sp.dma_start(out.rearrange("b l d -> (b l) d").rearrange("(t p) d -> p t d", p=TP),
                             k.H[:, :].rearrange("p (t d) -> p t d", d=D)).then_inc(stored, 16)
                sp.wait_ge(stored, 16)


def layout(x):
    def col(v, n=1):
        return v.reshape(-1, n)

    def heads32(w):
        p = np.zeros((HEADS, 32) + w.shape[1:], w.dtype)
        p[:, 0:HD] = w.reshape((HEADS, HD) + w.shape[1:])
        return p.reshape((HEADS * 32,) + w.shape[1:])

    def qkv(w):
        return np.concatenate([heads32(w[0:D]), heads32(w[D:2 * D]), w[2 * D:3 * D]], axis=0).T

    a = {}
    a["patches"] = x["x"].reshape(B, 3, 4, 16, 4, 16).transpose(3, 5, 1, 0, 2, 4).reshape(KP, B * NP_)
    a["tokWT"] = x["L0_tok_W"].T
    a["tok_b"] = x["L0_tok_b"].reshape(1, D)
    a["txt"] = x["txt"]
    a["c_ident"] = np.eye(128, dtype=np.float32)
    a["at1_w"] = qkv(x["L0_attn_qkv_weight"])
    b = x["L0_attn_qkv_bias"]
    a["at1_qk_b"] = np.concatenate([heads32(b[0:D]), heads32(b[D:2 * D])]).reshape(6, 128).T
    a["at1_v_b"] = b[2 * D:].reshape(1, D)
    a["at1_proj"] = x["L0_attn_proj_weight"].T
    a["at1_proj_b"] = x["L0_attn_proj_bias"].reshape(1, D)
    a["rt1_gate"] = x["L0_ffn_gate_w"].T
    gate = np.concatenate([x["L0_ffn_routed_gate"], x["L0_ffn_shared_gate"]])
    up = np.concatenate([x["L0_ffn_routed_up"], x["L0_ffn_shared_up"]])
    down = np.concatenate([x["L0_ffn_routed_down"], x["L0_ffn_shared_down"]])
    a["ex1_up"] = np.concatenate([gate, up], axis=1).transpose(0, 2, 1)
    a["ex1_down"] = down.transpose(0, 2, 1)
    pair = np.array([[heads_of(c)[i] * HH + f for i in range(2) for f in range(HH)] for c in range(NKC)])
    nk = KH * HH
    qcol = nk + KH + 2 * np.arange(KQ * HH).reshape(NQC, 128)
    def chunks(w):
        z = np.zeros(w.shape[:-1] + (NZ, 128), w.dtype)
        z[..., 0, 0:KH] = w[..., nk:nk + KH]
        z[..., KV_AT, :] = w[..., pair]
        z[..., [q[0] for q in Q_AT], :] = w[..., qcol]
        z[..., [q[1] for q in Q_AT], :] = w[..., qcol + 1]
        return z
    a["mm_wi"] = chunks(x["L1_attn_W_in"]).reshape(D, NZ * 128)
    a["mm_cw"] = chunks(x["L1_attn_conv_w"]).transpose(2, 1, 0)
    ph = np.repeat(x["L1_attn_phase_scale"], HH)
    a["mm_par"] = np.stack([x["L1_attn_theta_raw"].reshape(-1)[pair], x["L1_attn_w_int_raw"].reshape(-1)[pair],
                            ph[pair]]).transpose(2, 0, 1)
    a["mm_hp"] = np.stack([x["L1_attn_score_scale"], x["L1_attn_score_bias"], x["L1_attn_decay_slopes"]], axis=1)
    a["mm_nw"] = x["L1_attn_gated_norm_weight"].reshape(KH, 128).T
    a["mm_wg"] = x["L1_attn_W_gate"]
    val, gt = np.arange(EX), EX + np.arange(EX)
    even = np.concatenate([val[:128], gt[:128], val[128:], gt[128:]])
    odd = np.concatenate([val[:128], gt[:128], gt[128:], val[128:]])
    order = np.stack([odd if h % 4 >= 2 else even for h in range(KH)])
    a["mm_wr"] = np.take_along_axis(x["L1_attn_W_readout"], order[:, None, :], axis=2).transpose(1, 0, 2)
    w = x["L1_attn_W_out"].reshape(KH, EX, D)
    by_chunk = w[[list(heads_of(c)) for c in range(NKC)]]
    rest = by_chunk[:, :, 128:].reshape(NKC, 1, 128, D)
    a["mm_wo"] = np.concatenate([by_chunk[:, :, :128], rest], axis=1).reshape(3 * NKC, 128, D).transpose(1, 0, 2)
    a["c_sel"] = np.zeros((3 * PART, NKC, 128), np.float32)
    for c in range(NKC):
        for i, h in enumerate(heads_of(c)):
            a["c_sel"][h::PART, c, HH * i:HH * i + HH] = 1
    pos = np.tile(np.arange(L), SPG)
    a["c_dist"] = np.tile((MAXLEN - 1 - pos).astype(np.float32), (KH, 1))
    a["c_mask"] = np.tile((pos > 0).astype(np.float32), (128, 1))
    a["c_mean"] = np.full((128, 128), 1.0 / (KH * 2 * HH), np.float32)
    a["ln1_g"], a["ln1_b"] = col(x["L1_ffn_ln1_g"]), col(x["L1_ffn_ln1_b"])
    a["ln2_g"], a["ln2_b"] = col(x["L1_ffn_ln2_g"]), col(x["L1_ffn_ln2_b"])
    a["at2_w"] = qkv(x["L1_ffn_qkv_w"])
    a["at2_proj"] = x["L1_ffn_proj_w"].T
    a["at2_proj_b"] = x["L1_ffn_proj_b"].reshape(1, D)
    a["rt2_gate"], a["rt2_gate_b"] = x["L1_ffn_gate_w"].T, x["L1_ffn_gate_b"].reshape(1, NE)
    a["ex2_up"] = x["L1_ffn_w1"].transpose(0, 2, 1)
    a["ex2_b1"] = x["L1_ffn_b1"].reshape(NE * IC, 128).T
    a["ex2_down"] = x["L1_ffn_w2"].transpose(0, 2, 1)
    half = NTILE // 2
    a["ex2_b2"] = np.zeros((half, NE, half, D), np.float32)
    for t in range(half):
        a["ex2_b2"][t, :, t] = x["L1_ffn_b2"]
    a["ex2_b2"] = a["ex2_b2"].reshape(half * NE, half, D)
    return {n: np.ascontiguousarray(v) for n, v in a.items()}


def build(nc, arrays):
    a = {n: nc.dram_tensor(n + "_dram", v.shape, F32, kind="ExternalInput").ap() for n, v in arrays.items()}
    a["h0"] = nc.dram_tensor("h0_scratch", (B, L, D), F32).ap()
    out = nc.dram_tensor("out_dram", (B, L, D), F32, kind="ExternalOutput").ap()
    program(nc, a, out)


def kernel(**inputs):
    import concourse.bacc as bacc
    from concourse.bass_utils import run_bass_kernel_spmd

    arrays = layout({n: np.asarray(v) for n, v in inputs.items()})
    nc = bacc.Bacc("TRN2", target_bir_lowering=False, num_devices=1)
    build(nc, arrays)
    r = run_bass_kernel_spmd(nc, [{n + "_dram": v for n, v in arrays.items()}], core_ids=[0])
    return r.results[0]["out_dram"]
```
